# Optimizing a Trainium2 kernel written in Bass

```python
import numpy as np
import jax
import jax.numpy as jnp

def _softmax(x, axis=-1):
    return jax.nn.softmax(x, axis=axis)

def _gelu(x):
    return jax.nn.gelu(x, approximate=True)

def _silu(x):
    return jax.nn.silu(x)

def _sigmoid(x):
    return jax.nn.sigmoid(x)

def _layernorm(x, axis=-1, eps=1e-05):
    m = jnp.mean(x, axis=axis, keepdims=True)
    v = jnp.var(x, axis=axis, keepdims=True)
    return (x - m) / jnp.sqrt(v + eps)

def _scatter_add(tgt, idx, src, axis=0):
    return tgt.at[idx].add(src)

def _segment_sum(src, seg, n):
    return jax.ops.segment_sum(src, seg, n)
kernel_name = 'mk_adaln_ffn_d2_seqx_r8_b6c822'

def setup_inputs(seed: int=0):
    np.random.seed(seed)
    _w = jnp.asarray

    def _rec_inputs():
        import jax
        import jax.numpy as jnp
        _rk = jax.random.key(seed)
        x = -0.0002928 + 1 * jax.random.normal(jax.random.fold_in(_rk, 1), (8, 256, 128), jnp.float32)
        _lenS = 256 - jax.random.randint(jax.random.fold_in(_rk, 7), (8,), 0, max(1, 256 // 4) + 1, jnp.int32)
        _lenS2 = 256 - jax.random.randint(jax.random.fold_in(_rk, 8), (8,), 0, max(1, 256 // 4) + 1, jnp.int32)
        cond_64 = -0.0184271 + 1.00439 * jax.random.normal(jax.random.fold_in(_rk, 12), (8, 64), jnp.float32)
        _validS = jnp.arange(256)[None, :] < _lenS[:, None]
        _validS2 = jnp.arange(256)[None, :] < _lenS2[:, None]
        _causal = jnp.tril(jnp.ones((256, 256), dtype=bool))
        mask_BxS_bf1 = jnp.ones((8, 256), dtype=bool)
        return (x, cond_64, mask_BxS_bf1)
    x, cond_64, mask_BxS_bf1 = _rec_inputs()

    def _L0_cond_setup():
        import jax, jax.numpy as jnp
        import numpy as np
        DIM = 128
        HEADS = 16
        DIM_HEAD = 64
        SCALE = 8.0

        def ln(x, g, eps=1e-05):
            mean = x.mean(axis=-1, keepdims=True)
            var = ((x - mean) ** 2).mean(axis=-1, keepdims=True)
            return (x - mean) * jax.lax.rsqrt(var + eps) * g

        def l2norm(t):
            n = jnp.maximum(jnp.linalg.norm(t, axis=-1, keepdims=True), 1e-12)
            return t / n

        def rel_pos_bias(n, w0, b0, g0, w1, b1, g1, w2, b2, dtype):
            pos = jnp.arange(-n + 1, n, dtype=dtype)[:, None]
            h = jax.nn.silu(ln(pos @ w0 + b0, g0))
            h = jax.nn.silu(ln(h @ w1 + b1, g1))
            h = h @ w2 + b2
            i = jnp.arange(n)
            idx = i[:, None] - i[None, :] + n - 1
            bias = h[idx]
            return jnp.transpose(bias, (2, 0, 1))
        key = jax.random.key(seed)
        ks = jax.random.split(key, 16)
        b, n = (2, 256)
        inner = HEADS * DIM_HEAD
        s = 0.02
        return {'x': jax.random.normal(ks[0], (b, n, DIM), jnp.float32), 'mask': jnp.ones((b, n), dtype=bool), 'g_norm': jnp.ones((DIM,), jnp.float32), 'Wq': jax.random.normal(ks[1], (DIM, inner), jnp.float32) * s, 'Wkv': jax.random.normal(ks[2], (DIM, 2 * DIM_HEAD), jnp.float32) * s, 'q_scale': jnp.ones((DIM_HEAD,), jnp.float32), 'k_scale': jnp.ones((DIM_HEAD,), jnp.float32), 'null_kv': jax.random.normal(ks[3], (2, DIM_HEAD), jnp.float32), 'null_attn_bias': jax.random.normal(ks[4], (HEADS,), jnp.float32), 'w0': jax.random.normal(ks[5], (1, DIM), jnp.float32) * s, 'b0': jnp.zeros((DIM,), jnp.float32), 'g0': jnp.ones((DIM,), jnp.float32), 'w1': jax.random.normal(ks[6], (DIM, DIM), jnp.float32) * s, 'b1': jnp.zeros((DIM,), jnp.float32), 'g1': jnp.ones((DIM,), jnp.float32), 'w2': jax.random.normal(ks[7], (DIM, HEADS), jnp.float32) * s, 'b2': jnp.zeros((HEADS,), jnp.float32), 'Wout': jax.random.normal(ks[8], (inner, DIM), jnp.float32) * s, 'g_out': jnp.ones((DIM,), jnp.float32)}
    _L0_cond_all = _L0_cond_setup()
    _L0_cond_in = {k: v for k, v in _L0_cond_all.items() if k in ('g_norm', 'Wq', 'Wkv', 'q_scale', 'k_scale', 'null_attn_bias', 'w0', 'b0', 'g0', 'w1', 'b1', 'g1', 'w2', 'b2', 'Wout', 'g_out')}
    del _L0_cond_all

    def _L0_ffn_setup():
        import jax, jax.numpy as jnp
        import numpy as np
        B, S, D = (2, 256, 128)
        H = 256
        E = 8
        K = 2
        HS = 256 * 1
        SCALE = 1.0 / float(np.sqrt(D))
        key = jax.random.key(seed)
        ks = jax.random.split(key, 9)
        init = 0.02
        return {'x': jax.random.normal(ks[0], (B, S, D), dtype=jnp.float32), 'Wr': jax.random.normal(ks[1], (D, E), dtype=jnp.float32) * init, 'rb': jnp.zeros((E,), dtype=jnp.float32), 'W1': jax.random.normal(ks[2], (E, D, H), dtype=jnp.float32) * init, 'W2': jax.random.normal(ks[3], (E, H, D), dtype=jnp.float32) * init, 'W3': jax.random.normal(ks[4], (E, D, H), dtype=jnp.float32) * init, 'Ws1': jax.random.normal(ks[5], (D, HS), dtype=jnp.float32) * init, 'Ws2': jax.random.normal(ks[6], (HS, D), dtype=jnp.float32) * init, 'Ws3': jax.random.normal(ks[7], (D, HS), dtype=jnp.float32) * init}
    _L0_ffn_all = _L0_ffn_setup()
    _L0_ffn_in = {k: v for k, v in _L0_ffn_all.items() if k in ('Wr', 'rb', 'W1', 'W2', 'W3', 'Ws1', 'Ws2', 'Ws3')}
    del _L0_ffn_all

    def _L1_cond_setup():
        import jax, jax.numpy as jnp
        import numpy as np
        B, S, H = (4, 256, 128)
        E = 8
        M = 64
        K = 2
        N_SHARED = 2
        SM = M * N_SHARED
        G = 64
        GE_TEMP = 1.0
        ALPHA = 0.001
        SEQ_AUX = True
        NORM_TOPK = True
        COS_TEMP = 0.78
        CONS_ALPHA = 0.01
        LEAKY_SLOPE = 0.01
        EPS_COS = 1e-08

        def _leaky(x):
            return jnp.where(x >= 0, x, LEAKY_SLOPE * x)

        def _moe_forward(hidden_states, g, wt, wg, w_gate, w_up, w_down, sw_gate, sw_up, sw_down):
            b, s, h = hidden_states.shape
            x = hidden_states.reshape(-1, h)
            T = x.shape[0]
            logits_h = x @ wt.T
            logits_g = g @ wg.T
            logits_g = jnp.repeat(logits_g, s, axis=0)
            logits = (logits_h + logits_g / GE_TEMP) / (1.0 + 1.0 / GE_TEMP)
            scores = jax.nn.softmax(logits, axis=-1)
            topk_w, topk_idx = jax.lax.top_k(scores, K)
            if K > 1 and NORM_TOPK:
                topk_w = topk_w / (topk_w.sum(-1, keepdims=True) + 1e-20)
            onehot = jax.nn.one_hot(topk_idx.reshape(b, s * K), E, dtype=jnp.float32)
            ce = onehot.sum(1) / (s * K / E)
            aux_loss = (ce * scores.reshape(b, s, E).mean(1)).sum(1).mean() * ALPHA
            gp = _leaky(jnp.einsum('th,ehm->etm', x, w_gate))
            up = jnp.einsum('th,ehm->etm', x, w_up)
            y_all = jnp.einsum('etm,emh->eth', gp * up, w_down)
            y_sel = y_all[topk_idx, jnp.arange(T)[:, None], :]
            y = (y_sel * topk_w[..., None]).sum(1).reshape(b, s, h)
            p = _leaky(hidden_states @ sw_gate) * (hidden_states @ sw_up) @ sw_down
            y = y + p
            num = jnp.sum(y * p, -1)
            den = jnp.maximum(jnp.linalg.norm(y, axis=-1), EPS_COS) * jnp.maximum(jnp.linalg.norm(p, axis=-1), EPS_COS)
            closs = CONS_ALPHA * jnp.mean(num / den / (1.0 + COS_TEMP))
            return (y, aux_loss + closs)
        key = jax.random.key(seed)
        ks = jax.random.split(key, 12)
        sh = 1.0 / np.sqrt(H)
        sm = 1.0 / np.sqrt(M)
        ssm = 1.0 / np.sqrt(SM)
        sg = 1.0 / np.sqrt(G)
        return {'hidden_states': jax.random.normal(ks[0], (B, S, H), jnp.float32), 'g': jax.random.normal(ks[1], (B, G), jnp.float32), 'wt': jax.random.uniform(ks[2], (E, H), jnp.float32, -sh, sh), 'wg': jax.random.uniform(ks[3], (E, G), jnp.float32, -sg, sg), 'w_gate': jax.random.uniform(ks[4], (E, H, M), jnp.float32, -sh, sh), 'w_up': jax.random.uniform(ks[5], (E, H, M), jnp.float32, -sh, sh), 'w_down': jax.random.uniform(ks[6], (E, M, H), jnp.float32, -sm, sm), 'sw_gate': jax.random.uniform(ks[7], (H, SM), jnp.float32, -sh, sh), 'sw_up': jax.random.uniform(ks[8], (H, SM), jnp.float32, -sh, sh), 'sw_down': jax.random.uniform(ks[9], (SM, H), jnp.float32, -ssm, ssm)}
    _L1_cond_all = _L1_cond_setup()
    _L1_cond_in = {k: v for k, v in _L1_cond_all.items() if k in ('wt', 'wg', 'w_gate', 'w_up', 'w_down', 'sw_gate', 'sw_up', 'sw_down')}
    del _L1_cond_all

    def _L1_ffn_setup():
        import jax, jax.numpy as jnp
        import numpy as np
        S, B, D, H, DH = (512, 8, 128, 16, 64)

        def _forward(x, Wg, Wq, bq, Wkv, bkv, Wo, bo, ln_g, ln_b):
            s_len, bsz, d_model = x.shape
            n_head, _, d_head = Wq.shape
            cap = s_len // n_head
            scale = 1.0 / d_head ** 0.5
            h = jnp.transpose(x, (1, 0, 2))
            t = h
            probs = jax.nn.softmax(h @ Wg, axis=-1)
            scores = jnp.transpose(probs, (0, 2, 1))
            _, idx = jax.lax.top_k(scores, cap)
            idx = jnp.sort(idx, axis=-1)
            hg = jnp.take_along_axis(h[:, None, :, :], idx[..., None], axis=2)
            hg = jnp.transpose(hg, (1, 0, 2, 3))
            q = jnp.einsum('hbcd,hde->hbce', hg, Wq) + bq[:, None, None, :]
            kv = jnp.einsum('hbcd,hde->hbce', hg, Wkv) + bkv[:, None, None, :]
            k, v = jnp.split(kv, 2, axis=-1)
            att = jnp.einsum('hbid,hbjd->hbij', q, k) * scale
            p = jax.nn.softmax(att, axis=1)
            av = jnp.einsum('hbij,hbjd->hbid', p, v)
            ao = jnp.einsum('hbid,hde->hbie', av, Wo) + bo
            tok = jnp.transpose(idx, (1, 0, 2))
            b_ids = jnp.arange(bsz)[None, :, None]
            outs = jnp.zeros_like(t).at[b_ids, tok].add(ao)
            y = t + outs
            mu = jnp.mean(y, axis=-1, keepdims=True)
            var = jnp.var(y, axis=-1, keepdims=True)
            yn = (y - mu) * jax.lax.rsqrt(var + 1e-05) * ln_g + ln_b
            return jnp.transpose(yn, (1, 0, 2))
        key = jax.random.key(seed)
        ks = jax.random.split(key, 6)
        s = 0.02
        return {'x': jax.random.normal(ks[0], (S, B, D), jnp.float32), 'attn_mask': jnp.zeros((S, S), jnp.bool_), 'Wg': jax.random.normal(ks[1], (D, H), jnp.float32) * s, 'Wq': jax.random.normal(ks[2], (H, D, DH), jnp.float32) * s, 'bq': jnp.zeros((H, DH), jnp.float32), 'Wkv': jax.random.normal(ks[3], (H, D, 2 * DH), jnp.float32) * s, 'bkv': jnp.zeros((H, 2 * DH), jnp.float32), 'Wo': jax.random.normal(ks[4], (H, DH, D), jnp.float32) * s, 'bo': jnp.zeros((D,), jnp.float32), 'ln_g': jnp.ones((D,), jnp.float32), 'ln_b': jnp.zeros((D,), jnp.float32)}
    _L1_ffn_all = _L1_ffn_setup()
    _L1_ffn_in = {k: v for k, v in _L1_ffn_all.items() if k in ('attn_mask', 'Wg', 'Wq', 'bq', 'Wkv', 'bkv', 'Wo', 'bo', 'ln_g', 'ln_b')}
    del _L1_ffn_all
    return {'x': x, 'cond_64': cond_64, 'mask_BxS_bf1': mask_BxS_bf1, 'L0_cond_g_norm': _L0_cond_in['g_norm'], 'L0_cond_Wq': _L0_cond_in['Wq'], 'L0_cond_Wkv': _L0_cond_in['Wkv'], 'L0_cond_q_scale': _L0_cond_in['q_scale'], 'L0_cond_k_scale': _L0_cond_in['k_scale'], 'L0_cond_null_attn_bias': _L0_cond_in['null_attn_bias'], 'L0_cond_w0': _L0_cond_in['w0'], 'L0_cond_b0': _L0_cond_in['b0'], 'L0_cond_g0': _L0_cond_in['g0'], 'L0_cond_w1': _L0_cond_in['w1'], 'L0_cond_b1': _L0_cond_in['b1'], 'L0_cond_g1': _L0_cond_in['g1'], 'L0_cond_w2': _L0_cond_in['w2'], 'L0_cond_b2': _L0_cond_in['b2'], 'L0_cond_Wout': _L0_cond_in['Wout'], 'L0_cond_g_out': _L0_cond_in['g_out'], 'L0_ffn_Wr': _L0_ffn_in['Wr'], 'L0_ffn_rb': _L0_ffn_in['rb'], 'L0_ffn_W1': _L0_ffn_in['W1'], 'L0_ffn_W2': _L0_ffn_in['W2'], 'L0_ffn_W3': _L0_ffn_in['W3'], 'L0_ffn_Ws1': _L0_ffn_in['Ws1'], 'L0_ffn_Ws2': _L0_ffn_in['Ws2'], 'L0_ffn_Ws3': _L0_ffn_in['Ws3'], 'L1_cond_wt': _L1_cond_in['wt'], 'L1_cond_wg': _L1_cond_in['wg'], 'L1_cond_w_gate': _L1_cond_in['w_gate'], 'L1_cond_w_up': _L1_cond_in['w_up'], 'L1_cond_w_down': _L1_cond_in['w_down'], 'L1_cond_sw_gate': _L1_cond_in['sw_gate'], 'L1_cond_sw_up': _L1_cond_in['sw_up'], 'L1_cond_sw_down': _L1_cond_in['sw_down'], 'L1_ffn_attn_mask': _L1_ffn_in['attn_mask'], 'L1_ffn_Wg': _L1_ffn_in['Wg'], 'L1_ffn_Wq': _L1_ffn_in['Wq'], 'L1_ffn_bq': _L1_ffn_in['bq'], 'L1_ffn_Wkv': _L1_ffn_in['Wkv'], 'L1_ffn_bkv': _L1_ffn_in['bkv'], 'L1_ffn_Wo': _L1_ffn_in['Wo'], 'L1_ffn_bo': _L1_ffn_in['bo'], 'L1_ffn_ln_g': _L1_ffn_in['ln_g'], 'L1_ffn_ln_b': _L1_ffn_in['ln_b']}

def reference(x, cond_64, mask_BxS_bf1, L0_cond_g_norm, L0_cond_Wq, L0_cond_Wkv, L0_cond_q_scale, L0_cond_k_scale, L0_cond_null_attn_bias, L0_cond_w0, L0_cond_b0, L0_cond_g0, L0_cond_w1, L0_cond_b1, L0_cond_g1, L0_cond_w2, L0_cond_b2, L0_cond_Wout, L0_cond_g_out, L0_ffn_Wr, L0_ffn_rb, L0_ffn_W1, L0_ffn_W2, L0_ffn_W3, L0_ffn_Ws1, L0_ffn_Ws2, L0_ffn_Ws3, L1_cond_wt, L1_cond_wg, L1_cond_w_gate, L1_cond_w_up, L1_cond_w_down, L1_cond_sw_gate, L1_cond_sw_up, L1_cond_sw_down, L1_ffn_attn_mask, L1_ffn_Wg, L1_ffn_Wq, L1_ffn_bq, L1_ffn_Wkv, L1_ffn_bkv, L1_ffn_Wo, L1_ffn_bo, L1_ffn_ln_g, L1_ffn_ln_b):
    import jax
    import jax.numpy as jnp

    def _L0_cond_ref(x, mask, g_norm, Wq, Wkv, q_scale, k_scale, null_kv, null_attn_bias, w0, b0, g0, w1, b1, g1, w2, b2, Wout, g_out):
        import jax, jax.numpy as jnp
        import numpy as np
        DIM = 128
        HEADS = 16
        DIM_HEAD = 64
        SCALE = 8.0

        def ln(x, g, eps=1e-05):
            mean = x.mean(axis=-1, keepdims=True)
            var = ((x - mean) ** 2).mean(axis=-1, keepdims=True)
            return (x - mean) * jax.lax.rsqrt(var + eps) * g

        def l2norm(t):
            n = jnp.maximum(jnp.linalg.norm(t, axis=-1, keepdims=True), 1e-12)
            return t / n

        def rel_pos_bias(n, w0, b0, g0, w1, b1, g1, w2, b2, dtype):
            pos = jnp.arange(-n + 1, n, dtype=dtype)[:, None]
            h = jax.nn.silu(ln(pos @ w0 + b0, g0))
            h = jax.nn.silu(ln(h @ w1 + b1, g1))
            h = h @ w2 + b2
            i = jnp.arange(n)
            idx = i[:, None] - i[None, :] + n - 1
            bias = h[idx]
            return jnp.transpose(bias, (2, 0, 1))
        b, n, _ = x.shape
        xn = ln(x, g_norm)
        q = (xn @ Wq).reshape(b, n, HEADS, DIM_HEAD).transpose(0, 2, 1, 3)
        kv = xn @ Wkv
        k, v = (kv[..., :DIM_HEAD], kv[..., DIM_HEAD:])
        nk = jnp.broadcast_to(null_kv[0], (b, 1, DIM_HEAD))
        nv = jnp.broadcast_to(null_kv[1], (b, 1, DIM_HEAD))
        k = jnp.concatenate([nk, k], axis=1)
        v = jnp.concatenate([nv, v], axis=1)
        q = l2norm(q) * q_scale
        k = l2norm(k) * k_scale
        sim = jnp.einsum('bhid,bjd->bhij', q, k) * SCALE
        bias = rel_pos_bias(n, w0, b0, g0, w1, b1, g1, w2, b2, q.dtype)
        null_bias = jnp.broadcast_to(null_attn_bias[:, None, None], (HEADS, n, 1))
        attn_bias = jnp.concatenate([null_bias, bias], axis=-1)
        sim = sim + attn_bias
        neg = -jnp.finfo(sim.dtype).max
        causal = jnp.triu(jnp.ones((n, n + 1), dtype=bool), k=2)
        sim = jnp.where(causal, neg, sim)
        m = jnp.pad(mask, ((0, 0), (1, 0)), constant_values=True)[:, None, None, :]
        sim = jnp.where(m, sim, neg)
        attn = jax.nn.softmax(sim, axis=-1)
        out = jnp.einsum('bhij,bjd->bhid', attn, v)
        out = out.transpose(0, 2, 1, 3).reshape(b, n, HEADS * DIM_HEAD)
        return ln(out @ Wout, g_out)

    def _L0_ffn_ref(x, Wr, rb, W1, W2, W3, Ws1, Ws2, Ws3):
        import jax, jax.numpy as jnp
        import numpy as np
        B, S, D = (2, 256, 128)
        H = 256
        E = 8
        K = 2
        HS = 256 * 1
        SCALE = 1.0 / float(np.sqrt(D))
        logits = jnp.einsum('bsd,de->bse', x, Wr) * SCALE
        _, idx = jax.lax.top_k(logits + rb, K)
        gathered = jnp.take_along_axis(logits, idx, axis=-1)
        w = jax.nn.softmax(gathered, axis=-1)
        w_full = jnp.sum(jax.nn.one_hot(idx, E, dtype=x.dtype) * w[..., None], axis=-2)
        h = jnp.einsum('bsd,edh->bseh', x, W1) * jax.nn.silu(jnp.einsum('bsd,edh->bseh', x, W3))
        expert_out = jnp.einsum('bseh,ehd->bsed', h, W2)
        out = jnp.einsum('bsed,bse->bsd', expert_out, w_full)
        hs = jnp.einsum('bsd,dh->bsh', x, Ws1) * jax.nn.silu(jnp.einsum('bsd,dh->bsh', x, Ws3))
        out = out + jnp.einsum('bsh,hd->bsd', hs, Ws2)
        return out

    def _L1_cond_ref(hidden_states, g, wt, wg, w_gate, w_up, w_down, sw_gate, sw_up, sw_down):
        import jax, jax.numpy as jnp
        import numpy as np
        B, S, H = (4, 256, 128)
        E = 8
        M = 64
        K = 2
        N_SHARED = 2
        SM = M * N_SHARED
        G = 64
        GE_TEMP = 1.0
        ALPHA = 0.001
        SEQ_AUX = True
        NORM_TOPK = True
        COS_TEMP = 0.78
        CONS_ALPHA = 0.01
        LEAKY_SLOPE = 0.01
        EPS_COS = 1e-08

        def _leaky(x):
            return jnp.where(x >= 0, x, LEAKY_SLOPE * x)

        def _moe_forward(hidden_states, g, wt, wg, w_gate, w_up, w_down, sw_gate, sw_up, sw_down):
            b, s, h = hidden_states.shape
            x = hidden_states.reshape(-1, h)
            T = x.shape[0]
            logits_h = x @ wt.T
            logits_g = g @ wg.T
            logits_g = jnp.repeat(logits_g, s, axis=0)
            logits = (logits_h + logits_g / GE_TEMP) / (1.0 + 1.0 / GE_TEMP)
            scores = jax.nn.softmax(logits, axis=-1)
            topk_w, topk_idx = jax.lax.top_k(scores, K)
            if K > 1 and NORM_TOPK:
                topk_w = topk_w / (topk_w.sum(-1, keepdims=True) + 1e-20)
            onehot = jax.nn.one_hot(topk_idx.reshape(b, s * K), E, dtype=jnp.float32)
            ce = onehot.sum(1) / (s * K / E)
            aux_loss = (ce * scores.reshape(b, s, E).mean(1)).sum(1).mean() * ALPHA
            gp = _leaky(jnp.einsum('th,ehm->etm', x, w_gate))
            up = jnp.einsum('th,ehm->etm', x, w_up)
            y_all = jnp.einsum('etm,emh->eth', gp * up, w_down)
            y_sel = y_all[topk_idx, jnp.arange(T)[:, None], :]
            y = (y_sel * topk_w[..., None]).sum(1).reshape(b, s, h)
            p = _leaky(hidden_states @ sw_gate) * (hidden_states @ sw_up) @ sw_down
            y = y + p
            num = jnp.sum(y * p, -1)
            den = jnp.maximum(jnp.linalg.norm(y, axis=-1), EPS_COS) * jnp.maximum(jnp.linalg.norm(p, axis=-1), EPS_COS)
            closs = CONS_ALPHA * jnp.mean(num / den / (1.0 + COS_TEMP))
            return (y, aux_loss + closs)
        y, _ = _moe_forward(hidden_states, g, wt, wg, w_gate, w_up, w_down, sw_gate, sw_up, sw_down)
        return y

    def _L1_ffn_ref(x, attn_mask, Wg, Wq, bq, Wkv, bkv, Wo, bo, ln_g, ln_b):
        import jax, jax.numpy as jnp
        import numpy as np
        S, B, D, H, DH = (512, 8, 128, 16, 64)

        def _forward(x, Wg, Wq, bq, Wkv, bkv, Wo, bo, ln_g, ln_b):
            s_len, bsz, d_model = x.shape
            n_head, _, d_head = Wq.shape
            cap = s_len // n_head
            scale = 1.0 / d_head ** 0.5
            h = jnp.transpose(x, (1, 0, 2))
            t = h
            probs = jax.nn.softmax(h @ Wg, axis=-1)
            scores = jnp.transpose(probs, (0, 2, 1))
            _, idx = jax.lax.top_k(scores, cap)
            idx = jnp.sort(idx, axis=-1)
            hg = jnp.take_along_axis(h[:, None, :, :], idx[..., None], axis=2)
            hg = jnp.transpose(hg, (1, 0, 2, 3))
            q = jnp.einsum('hbcd,hde->hbce', hg, Wq) + bq[:, None, None, :]
            kv = jnp.einsum('hbcd,hde->hbce', hg, Wkv) + bkv[:, None, None, :]
            k, v = jnp.split(kv, 2, axis=-1)
            att = jnp.einsum('hbid,hbjd->hbij', q, k) * scale
            p = jax.nn.softmax(att, axis=1)
            av = jnp.einsum('hbij,hbjd->hbid', p, v)
            ao = jnp.einsum('hbid,hde->hbie', av, Wo) + bo
            tok = jnp.transpose(idx, (1, 0, 2))
            b_ids = jnp.arange(bsz)[None, :, None]
            outs = jnp.zeros_like(t).at[b_ids, tok].add(ao)
            y = t + outs
            mu = jnp.mean(y, axis=-1, keepdims=True)
            var = jnp.var(y, axis=-1, keepdims=True)
            yn = (y - mu) * jax.lax.rsqrt(var + 1e-05) * ln_g + ln_b
            return jnp.transpose(yn, (1, 0, 2))
        return _forward(x, Wg, Wq, bq, Wkv, bkv, Wo, bo, ln_g, ln_b)
    x = x + _L0_ffn_ref(_L0_cond_ref(x, mask_BxS_bf1, L0_cond_g_norm, L0_cond_Wq, L0_cond_Wkv, L0_cond_q_scale, L0_cond_k_scale, cond_64, L0_cond_null_attn_bias, L0_cond_w0, L0_cond_b0, L0_cond_g0, L0_cond_w1, L0_cond_b1, L0_cond_g1, L0_cond_w2, L0_cond_b2, L0_cond_Wout, L0_cond_g_out), L0_ffn_Wr, L0_ffn_rb, L0_ffn_W1, L0_ffn_W2, L0_ffn_W3, L0_ffn_Ws1, L0_ffn_Ws2, L0_ffn_Ws3)
    x = x + _L1_ffn_ref(_L1_cond_ref(x, cond_64, L1_cond_wt, L1_cond_wg, L1_cond_w_gate, L1_cond_w_up, L1_cond_w_down, L1_cond_sw_gate, L1_cond_sw_up, L1_cond_sw_down), L1_ffn_attn_mask, L1_ffn_Wg, L1_ffn_Wq, L1_ffn_bq, L1_ffn_Wkv, L1_ffn_bkv, L1_ffn_Wo, L1_ffn_bo, L1_ffn_ln_g, L1_ffn_ln_b)
    return x

_drawn_inputs = setup_inputs


def setup_inputs(seed=0):
    import zlib

    import numpy as np

    out = dict(_drawn_inputs(seed))
    spreads = {'L0_cond_g_norm': (1.0, 0.6),
     'L0_cond_q_scale': (1.0, 0.6),
     'L0_cond_k_scale': (1.0, 0.6),
     'L0_cond_b0': (0.0, 0.8),
     'L0_cond_g0': (1.0, 0.6),
     'L0_cond_b1': (0.0, 0.8),
     'L0_cond_g1': (1.0, 0.6),
     'L0_cond_b2': (0.0, 0.8),
     'L0_cond_g_out': (1.0, 0.6),
     'L0_ffn_rb': (0.0, 0.273),
     'L1_ffn_bq': (0.0, 0.1),
     'L1_ffn_bkv': (0.0, 0.1),
     'L1_ffn_bo': (0.0, 0.1),
     'L1_ffn_ln_g': (1.0, 0.2),
     'L1_ffn_ln_b': (0.0, 0.1)}
    factors = {'L0_cond_null_attn_bias': 3.261,
     'L0_cond_w0': 8.0,
     'L0_cond_w1': 6.644,
     'L0_cond_w2': 7.871,
     'L0_ffn_Wr': 3.806,
     'L0_ffn_W1': 2.771,
     'L0_ffn_W2': 2.723}
    for name, (base, spread) in spreads.items():
        noise = np.random.default_rng([zlib.crc32(name.encode()), seed]).standard_normal(out[name].shape)
        drawn = base * np.exp(spread * noise) if base else spread * noise
        out[name] = jnp.asarray(drawn.astype(out[name].dtype))
    for name, factor in factors.items():
        out[name] = (out[name] * factor).astype(out[name].dtype)
    return out
```

```python
from contextlib import ExitStack

import concourse.bass as bass
from concourse import mybir

F32 = mybir.dt.float32
F32R = mybir.dt.float32r
BF16 = mybir.dt.bfloat16
I32 = mybir.dt.int32
U8 = mybir.dt.uint8
ALU = mybir.AluOpType
ACT = mybir.ActivationFunctionType
AX = mybir.AxisListType.X

P = 128
B, S, D = 8, 256, 128
T = S // P
HEADS, DH = 16, 64
PAIRS = HEADS // 2
GROUPS = HEADS // 4
E = 8
HID = 256
HC = HID // P
M1 = 64
X0 = E + 1
X1 = E // 2 + 1
BIG = 1e30
LN_EPS = 1e-5
SCALE_QK = 8.0
SCALE_R0 = 1.0 / float(D) ** 0.5
RSQRT_MAGIC = float(0x5F3759DF)

SPLIT = [("wq", HEADS * DH), ("wkv", 2 * DH), ("wr", E), ("wt", E), ("w3", X0 * HID), ("w1", X0 * HID),
         ("mg", X1 * P), ("mu", X1 * P)]
NSPLIT = sum(n for _, n in SPLIT)
CHUNKS = 4
CHUNK = NSPLIT // CHUNKS
DOWN = [("w2", X0 * HC * D), ("wout", PAIRS * D), ("wd", X1 * D)]
NDOWN = sum(n for _, n in DOWN)
ROWS = [("w0", D), ("b0", D), ("g0", D), ("b1", D), ("g1", D), ("nk", P), ("nv", P), ("cond", B * DH)]
NROWS = sum(n for _, n in ROWS)
KROWS = [("null_bias", HEADS), ("rb", E), ("ln_g", D), ("ln_b", D), ("nv_row", DH)]
NKROWS = sum(n for _, n in KROWS)
COLS = ["g_norm", "q_scale", "k_scale", "g_out", "b2", "pos0", "pos1"]
MATS = [("w1m", D), ("w2m", HEADS), ("wg", E), ("ident", P), ("rank", T * E), ("sel", E // 2 * P)]
NMATS = sum(n for _, n in MATS)

KT = S + 2
SB1, SB0 = 0, KT
SW = KT + P + 2
REL = S + P

M_ALL = ["QT1", "XT", "Q0", "Q1", "QT2", "OT0", "Q2", "Q3", "KV", "QT3", "OT1", "OT2", "OT3", "KT", "WO", "QT0"]
M_PRE = ["XT", "Q0", "Q1", "Q2", "Q3", "KV", "KT", "QT0"]
M_ATT = [n for n in M_ALL if n not in M_PRE]
D_ALL = ["YT", "LOG0"] + [f"D{e}" for e in range(X0)] + ["X1T", "LOG1", "WT", "WB0", "WB1", "DOWN"]
ND = len(D_ALL)
NGU = X0 + 3
QROUNDS = 5

RSQRT_STEPS = 11
PRE_STEPS = 1 + RSQRT_STEPS
ATT_STEPS = GROUPS + 3 + RSQRT_STEPS
ROUTE_STEPS = 17
MOE_STEPS = 2 * ROUTE_STEPS + 3 + RSQRT_STEPS


def offsets(parts):
    at, out = 0, {}
    for name, n in parts:
        out[name] = (at, n)
        at += n
    return out


def m_use(name, b, att, pre):
    order = [n for n in M_ALL if (att and n in M_ATT) or (pre and n in M_PRE)]
    first = 0 if (isinstance(b, int) and b < 0) else b * len(M_ALL) + len(M_PRE)
    return first + order.index(name)


def d_use(name, m):
    return m * ND + D_ALL.index(name)


def wait(eng, sem, value):
    if isinstance(value, int) and value <= 0:
        return
    eng.wait_ge(sem, value)


class Steps:

    def __init__(self, eng, sem, per):
        self.eng, self.sem, self.per = eng, sem, per

    def start(self, b):
        self.b, self.k = b, 0

    def link(self, ins):
        self.k += 1
        ins.then_inc(self.sem, 1)
        self.eng.wait_ge(self.sem, self.b * self.per + self.k)

    def end(self):
        assert self.k == self.per, (self.k, self.per)


def build(nc, x_in, mask_in, split_in, down_in, rows_in, krows_in, cols_in, mats_in, rel_dram, out):
    with ExitStack() as ctx:
        def sb(name, shape, dt=F32):
            return ctx.enter_context(nc.sbuf_tensor(name, shape, dt))

        def sem(name):
            return ctx.enter_context(nc.semaphore(name))

        def bank(name):
            return ctx.enter_context(nc.psum_tensor(name, [P, 512], F32))
        bank_s = [bank("bank_s0"), bank("bank_s1")]
        bank_pt = bank("bank_pt")
        bank_pv = bank("bank_pv")
        bank_m = bank("bank_m")
        bank_g, bank_u, bank_d = bank("bank_g"), bank("bank_u"), bank("bank_d")

        w_hi, w_lo = sb("w_hi", [P, NSPLIT], F32R), sb("w_lo", [P, NSPLIT], F32R)
        down = sb("down", [P, NDOWN])
        krows, cols, mats = sb("krows", [P, NKROWS]), sb("cols", [P, len(COLS)]), sb("mats", [P, NMATS])
        x_sb = sb("x_sb", [P, B * T, D])
        bias_all = sb("bias_all", [P, HEADS, S + 1])
        bias_b = sb("bias_b", [P, HEADS, SW])
        mask_u8 = sb("mask_u8", [P, B, S], U8)
        mask_add = sb("mask_add", [P, B, SW], BF16)
        mask_row, idle = sb("mask_row", [P, SW]), sb("idle", [P, HEADS + 2])
        x_stat, x_mv = sb("x_stat", [P, B * T, 6]), sb("x_mv", [P, B * T, 2])
        x_var, x_rstd, x_tmp = sb("x_var", [P, B * T]), sb("x_rstd", [P, B * T]), sb("x_tmp", [P, B * T])
        kscale = sb("kscale", [P, 1])
        cond_logit = sb("cond_logit", [P, B * E])
        null_out = sb("null_out", [P, D])
        xn = sb("xn", [P, T, D])
        xnT_hi, xnT_lo = sb("xnT_hi", [P, S], F32R), sb("xnT_lo", [P, S], F32R)
        q_raw = sb("q_raw", [P, T, HEADS * DH])
        kv_raw = sb("kv_raw", [P, T, 2 * DH])
        sq = sb("sq", [P, 2, 512])
        ss, rn, rn_tmp = sb("ss", [P, T * HEADS + T]), sb("rn", [P, T * HEADS + T]), sb("rn_tmp", [P, T * HEADS + T])
        qn = sb("qn", [P, T, HEADS * DH])
        kn = sb("kn", [P, T, P])
        val = sb("val", [P, T, DH])
        kT = sb("kT", [P, SW])
        qT = sb("qT", [P, 2, 2, S])
        prob = sb("prob", [P, 2, SW])
        s_min, s_sum = sb("s_min", [P, 2, T]), sb("s_sum", [P, T, HEADS])
        probT = sb("probT", [P, 2, 3 * P])
        r_sum = sb("r_sum", [P, T, 4])
        on = sb("on", [P, 2, T, 4 * DH])
        oT = sb("oT", [P, PAIRS, S])
        y_raw, yn = sb("y_raw", [P, T, D]), sb("yn", [P, T, D])
        y_stat, y_mv, y_var = sb("y_stat", [P, T, 6]), sb("y_mv", [P, T, 2]), sb("y_var", [P, T])
        y_rstd, y_tmp = sb("y_rstd", [P, T]), sb("y_tmp", [P, T])
        yT_hi, yT_lo = sb("yT_hi", [P, S], F32R), sb("yT_lo", [P, S], F32R)
        act_g, gated = sb("act_g", [P, 512]), sb("gated", [P, 512])
        hid = sb("hid", [P, X1 * S])
        acc = sb("acc", [P, T, D])
        lg, cand, eq, oh1, oh2, w_tok = (sb(n, [P, T, E]) for n in ("lg", "cand", "eq", "oh1", "oh2", "w_tok"))
        top, ldiff, ltanh = sb("top", [P, T]), sb("ldiff", [P, T]), sb("ltanh", [P, T])
        wT = sb("wT", [E, S])
        o_stat, o_mv, o_var = sb("o_stat", [P, T, 6]), sb("o_mv", [P, T, 2]), sb("o_var", [P, T])
        o_rstd, o_tmp = sb("o_rstd", [P, T]), sb("o_tmp", [P, T])
        norm, resid, out_sb = sb("norm", [P, T, D]), sb("resid", [P, T, D]), sb("out_sb", [P, T, D])

        rows = q_raw[:].rearrange("p t n -> p (t n)")[:, 0:NROWS]
        stage = [oT[:].rearrange("p a s -> p (a s)")[:, 0:CHUNK], qn[:].rearrange("p t n -> p (t n)")[:, 0:CHUNK]]
        hb, hs, hT = sq[:, 0, 0:2 * D].rearrange("p (t d) -> p t d", t=2), \
            sq[:, 0, 2 * D:4 * D].rearrange("p (t d) -> p t d", t=2), sq[:, 1, 0:2 * D]
        rel = prob[0:HEADS, 0, 0:REL]
        cond_rep = bias_b[0:DH].rearrange("p h w -> p (h w)")[:, 0:B * P].rearrange("p (b n) -> p b n", b=B)
        nv_rep = xn[:, 0, :]

        so, do, ro, ko, mo = offsets(SPLIT), offsets(DOWN), offsets(ROWS), offsets(KROWS), offsets(MATS)

        def hi(name, a=0, n=None):
            at, size = so[name]
            return w_hi[:, at + a:at + a + (size if n is None else n)]

        def lo(name, a=0, n=None):
            at, size = so[name]
            return w_lo[:, at + a:at + a + (size if n is None else n)]

        def dn(name, i):
            return down[:, do[name][0] + i * D:do[name][0] + (i + 1) * D]

        def row(name):
            return rows[:, ro[name][0]:ro[name][0] + ro[name][1]]

        def krow(name):
            return krows[:, ko[name][0]:ko[name][0] + ko[name][1]]

        def mat(name):
            return mats[:, mo[name][0]:mo[name][0] + mo[name][1]]

        def col(name, n=P):
            return cols[0:n, COLS.index(name):COLS.index(name) + 1]

        ident = mat("ident")
        rank = mat("rank").rearrange("p (t e) -> p t e", t=T)
        sel = mat("sel")[0:E, :]

        ld_small, ld_x, ld_mask, ld_down = sem("ld_small"), sem("ld_x"), sem("ld_mask"), sem("ld_down")
        ld_w = [sem(f"ld_w{c}") for c in range(CHUNKS)]
        rel_stored, bias_loaded, out_stored = sem("rel_stored"), sem("bias_loaded"), sem("out_stored")
        hi_split, lo_split = sem("hi_split"), sem("lo_split")
        set_pe, set_act, set_dve = sem("set_pe"), sem("set_act"), sem("set_dve")
        rel_ready, bias_ready = sem("rel_ready"), sem("bias_ready")
        steps_pre, steps_att, steps_moe = sem("steps_pre"), sem("steps_att"), sem("steps_moe")
        m_full, m_free, m_hi = sem("m_full"), sem("m_free"), sem("m_hi")
        d_full, d_free, d_hi = sem("d_full"), sem("d_free"), sem("d_hi")
        xn_ready, sq_ready, ss_ready = sem("xn_ready"), sem("sq_ready"), sem("ss_ready")
        qn_ready, kn_ready, val_ready = sem("qn_ready"), sem("kn_ready"), sem("val_ready")
        batch_bias, mask_ready = sem("batch_bias"), sem("mask_ready")
        s_full, s_read, p_ready = sem("s_full"), sem("s_read"), sem("p_ready")
        pt_full, pt_copied, pv_done, on_ready = sem("pt_full"), sem("pt_copied"), sem("pv_done"), sem("on_ready")
        yn_ready = sem("yn_ready")
        g_full, act_ready, g_read = sem("g_full"), sem("act_ready"), sem("g_read")
        u_full, u_read = sem("u_full"), sem("u_read")
        diff_ready, tanh_ready, w_ready = sem("diff_ready"), sem("tanh_ready"), sem("w_ready")
        resid_ready, norm_ready, out_ready = sem("resid_ready"), sem("norm_ready"), sem("out_ready")

        block = ctx.enter_context(nc.Block())

        COND_T0, COND_T1, COND, NV_T, NK_T, HT0, HW1, HT1, HW2, NULL_OUT = range(1, 11)

        @block.sync
        def _(sp):
            sp.dma_start(cols[:], cols_in).then_inc(ld_small, 16)
            sp.dma_start(rows, rows_in.partition_broadcast(P)).then_inc(ld_small, 16)
            sp.dma_start(mats[:], mats_in).then_inc(ld_small, 16)
            sp.dma_start(krows[:], krows_in.partition_broadcast(P)).then_inc(ld_small, 16)
            sp.dma_start(x_sb[:], x_in.rearrange("b (t p) d -> p (b t) d", p=P)).then_inc(ld_x, 16)
            for c in range(2):
                sp.dma_start(stage[c], split_in[:, c * CHUNK:(c + 1) * CHUNK]).then_inc(ld_w[c], 16)
            sp.dma_start(mask_u8[:], mask_in.partition_broadcast(P)).then_inc(ld_mask, 16)
            sp.dma_start(down[:], down_in).then_inc(ld_down, 16)
            for c in range(2, CHUNKS):
                sp.wait_ge(lo_split, c - 1)
                sp.dma_start(stage[c % 2], split_in[:, c * CHUNK:(c + 1) * CHUNK]).then_inc(ld_w[c], 16)
            sp.wait_ge(rel_ready, 1)
            copies = rel_dram.rearrange("h i r -> h (i r)").rearrange("h (i r) -> h i r", r=REL)
            sp.dma_start(copies, rel[:, None, :].broadcast_to([HEADS, P, REL])).then_inc(rel_stored, 16)
            sp.wait_ge(rel_stored, 16)
            band = bass.AP(rel_dram.tensor, P - 1, [[REL - 1, P], [P * REL, HEADS], [1, S]])
            sp.dma_start(bias_all[:, :, 0:S], band).then_inc(bias_loaded, 16)
            out_v = out.rearrange("b (t p) d -> b p t d", p=P)

            def store(m):
                sp.wait_ge(out_ready, m + 1)
                sp.dma_start(out_v[m], out_sb[:]).then_inc(out_stored, 16)
            for m in range(B):
                store(m)
            sp.wait_ge(out_stored, 16 * B)

        @block.tensor
        def _(pe):
            def split3(dst, a_hi, a_lo, b_hi, b_lo):
                nc.tensor.matmul(dst, a_hi, b_hi, start=True, stop=False)
                nc.tensor.matmul(dst, a_lo, b_hi, start=False, stop=False)
                return nc.tensor.matmul(dst, a_hi, b_lo, start=False, stop=True)

            pe.wait_ge(ld_small, 64)
            for half in range(2):
                if half:
                    pe.wait_ge(set_dve, 1)
                for i in range(4):
                    b0 = (4 * half + i) * DH
                    mm = nc.tensor.transpose(bank_u[0:DH, i * P:(i + 1) * P], row("cond")[:, b0:b0 + DH], ident)
                mm.then_inc(set_pe, 1)
            pe.wait_ge(set_dve, 2)
            for b in range(B):
                mm = nc.tensor.matmul(bank_g[:, b * E:(b + 1) * E], cond_rep[:, b, :], mat("wg")[0:DH, :],
                                      start=True, stop=True)
            mm.then_inc(set_pe, 1)
            nc.tensor.transpose(bank_d[:, 0:P], row("nv"), ident).then_inc(set_pe, 1)
            pe.wait_ge(set_dve, 4)
            nc.tensor.transpose(bank_pt[:, 0:P], kn[:, 0, :], ident).then_inc(set_pe, 1)
            for layer in range(2):
                pe.wait_ge(set_dve, 6 + 3 * layer)
                for t in range(2):
                    mm = nc.tensor.transpose(bank_m[:, t * P:(t + 1) * P], hs[:, t, :], ident)
                mm.then_inc(set_pe, 1)
                pe.wait_ge(set_dve, 7 + 3 * layer)
                if layer == 0:
                    for t in range(2):
                        mm = nc.tensor.matmul(bank_pv[:, t * D:(t + 1) * D], hT[:, t * P:(t + 1) * P], mat("w1m"),
                                              start=True, stop=True)
                else:
                    mm = nc.tensor.matmul(bank_pv[0:HEADS, 0:S], mat("w2m"), hT, start=True, stop=True)
                mm.then_inc(set_pe, 1)
            pe.wait_ge(ld_down, 16)
            pe.wait_ge(set_dve, 3)
            for j in range(PAIRS):
                mm = nc.tensor.matmul(bank_d[:, 0:D], nv_rep, dn("wout", j), start=(j == 0), stop=(j == PAIRS - 1))
            mm.then_inc(set_pe, 1)
            pe.wait_ge(set_dve, 11)

            def take_m(name, b, att, pre):
                wait(pe, m_free, m_use(name, b, att, pre))

            def q_transposes(g, bq, b, att, pre):
                take_m(f"QT{g}", b, att, pre)
                if g == 0:
                    pe.wait_ge(qn_ready, bq + 1)
                for j in range(2):
                    for t in range(T):
                        c = (2 * g + j) * P
                        mm = nc.tensor.transpose(bank_m[:, (j * T + t) * P:(j * T + t + 1) * P], qn[:, t, c:c + P], ident)
                mm.then_inc(m_full, 1)

            def scores(h, bq, use_q):
                g, j, o = h // 4, h % 4 // 2, DH * (h % 2)
                wait(pe, m_free, use_q + 1)
                wait(pe, s_read, bq * HEADS + h - 1)
                q = qT[o:o + DH, g % 2, j, :]
                dst = bank_s[h % 2]
                nc.tensor.matmul(dst[:, SB0:SB0 + P + 1], q[:, 0:P], kT[o:o + DH, SB0:SB0 + P + 1], start=True, stop=True)
                nc.tensor.matmul(dst[:, SB1:SB1 + S + 1], q[:, P:2 * P], kT[o:o + DH, SB1:SB1 + S + 1],
                                 start=True, stop=True).then_inc(s_full, 1)

            def p_transposes(h, b):
                n = b * HEADS + h
                pe.wait_ge(p_ready, n + 1)
                wait(pe, pt_copied, n)
                p = prob[:, h % 2, :]
                nc.tensor.transpose(bank_pt[:, 0:P], p[:, SB0:SB0 + P], ident)
                nc.tensor.transpose(bank_pt[:, P:2 * P], p[:, SB1:SB1 + P], ident)
                nc.tensor.transpose(bank_pt[:, 2 * P:3 * P], p[:, SB1 + P:SB1 + 2 * P], ident).then_inc(pt_full, 1)

            def values(h, b):
                n = b * HEADS + h
                pe.wait_ge(pt_copied, n + 1)
                if h == 0:
                    pe.wait_ge(val_ready, b + 1)
                if h % 4 == 0:
                    wait(pe, on_ready, b * GROUPS + h // 4)
                pt, o = probT[:, h % 2, :], (h % 4) * DH
                out0 = bank_pv[:, o:o + DH]
                out1 = bank_pv[:, 4 * DH + o:4 * DH + o + DH]
                nc.tensor.matmul(out0, pt[:, 0:P], val[:, 0, :], start=True, stop=True)
                nc.tensor.matmul(out1, pt[:, P:2 * P], val[:, 0, :], start=True, stop=False)
                nc.tensor.matmul(out1, pt[:, 2 * P:3 * P], val[:, 1, :], start=False, stop=True).then_inc(pv_done, 1)

            def o_transposes(g, b, att, pre):
                take_m(f"OT{g}", b, att, pre)
                pe.wait_ge(on_ready, b * GROUPS + g + 1)
                for j in range(2):
                    for t in range(T):
                        mm = nc.tensor.transpose(bank_m[:, (j * T + t) * P:(j * T + t + 1) * P],
                                                 on[:, g % 2, t, j * P:(j + 1) * P], ident)
                mm.then_inc(m_full, 1)

            def out_projection(b, att, pre):
                take_m("WO", b, att, pre)
                for t in range(T):
                    for j in range(PAIRS):
                        mm = nc.tensor.matmul(bank_m[:, t * D:(t + 1) * D], oT[:, j, t * P:(t + 1) * P], dn("wout", j),
                                              start=(j == 0), stop=(j == PAIRS - 1))
                mm.then_inc(m_full, 1)

            def x_transposes(b, att, pre):
                take_m("XT", b, att, pre)
                pe.wait_ge(xn_ready, b + 2)
                for t in range(T):
                    mm = nc.tensor.transpose(bank_m[:, t * P:(t + 1) * P], xn[:, t, :], ident)
                mm.then_inc(m_full, 1)

            def q_round(r, b, att, pre):
                take_m(f"Q{r}", b, att, pre)
                t, c = r // 2, r % 2 * 512
                split3(bank_m[:], xnT_hi[:, t * P:(t + 1) * P], xnT_lo[:, t * P:(t + 1) * P],
                       hi("wq", c, 512), lo("wq", c, 512)).then_inc(m_full, 1)

            def kv_round(b, att, pre):
                take_m("KV", b, att, pre)
                for t in range(T):
                    mm = split3(bank_m[:, t * P:(t + 1) * P], xnT_hi[:, t * P:(t + 1) * P],
                                xnT_lo[:, t * P:(t + 1) * P], hi("wkv"), lo("wkv"))
                mm.then_inc(m_full, 1)

            def k_transposes(b, att, pre):
                take_m("KT", b, att, pre)
                pe.wait_ge(kn_ready, b + 2)
                for t in range(T):
                    mm = nc.tensor.transpose(bank_m[:, t * P:(t + 1) * P], kn[:, t, :], ident)
                mm.then_inc(m_full, 1)

            def take_d(name, m):
                wait(pe, d_free, d_use(name, m))

            def tok_transposes(name, src, ready, m):
                take_d(name, m)
                if ready is not None:
                    pe.wait_ge(ready, m + 1)
                for t in range(T):
                    mm = nc.tensor.transpose(bank_d[:, t * P:(t + 1) * P], src[:, t, :], ident)
                mm.then_inc(d_full, 1)

            def logits(name, weight, m):
                take_d(name, m)
                for t in range(T):
                    mm = split3(bank_d[:, t * E:(t + 1) * E], yT_hi[:, t * P:(t + 1) * P],
                                yT_lo[:, t * P:(t + 1) * P], hi(weight), lo(weight))
                mm.then_inc(d_full, 1)

            def gate_up(k, m):
                if k < X0:
                    parts = [(("w3", "w1"), (k * HC + c) * P) for c in range(HC)]
                else:
                    pairs = {X0: [X1 - 1], X0 + 1: [0, 1], X0 + 2: [2, 3]}[k]
                    parts = [(("mg", "mu"), j * P) for j in pairs]
                for side, (dst, read, full) in enumerate(((bank_g, g_read, g_full), (bank_u, u_read, u_full))):
                    wait(pe, read, m * NGU + k)
                    for c, (names, at) in enumerate(parts):
                        mm = split3(dst[:, c * S:(c + 1) * S], hi(names[side], at, P), lo(names[side], at, P),
                                    yT_hi[:], yT_lo[:])
                    mm.then_inc(full, 1)

            def expert_down(e, m):
                take_d(f"D{e}", m)
                pe.wait_ge(u_read, m * NGU + e + 1)
                for t in range(T):
                    for c in range(HC):
                        h0 = (e % 2) * 512 + c * S + t * P
                        mm = nc.tensor.matmul(bank_d[:, t * D:(t + 1) * D], hid[:, h0:h0 + P], dn("w2", e * HC + c),
                                              start=(c == 0), stop=(c == HC - 1))
                mm.then_inc(d_full, 1)

            def weight_transposes(m):
                take_d("WT", m)
                pe.wait_ge(w_ready, 2 * m + 2)
                for t in range(T):
                    mm = nc.tensor.transpose(bank_d[0:E, t * P:(t + 1) * P], w_tok[:, t, :], ident)
                mm.then_inc(d_full, 1)

            def weight_rows(r, m):
                take_d(f"WB{r}", m)
                for j in range(2):
                    mm = nc.tensor.matmul(bank_d[:, j * S:(j + 1) * S], sel[:, (2 * r + j) * P:(2 * r + j + 1) * P],
                                          wT[:], start=True, stop=True)
                mm.then_inc(d_full, 1)

            def layer1_down(m):
                take_d("DOWN", m)
                for t in range(T):
                    for j in range(X1):
                        mm = nc.tensor.matmul(bank_d[:, t * D:(t + 1) * D], hid[:, j * S + t * P:j * S + (t + 1) * P],
                                              dn("wd", j), start=(j == 0), stop=(j == X1 - 1))
                mm.then_inc(d_full, 1)

            def turn(b, att, moe, pre):
                m = b - 1
                for h in range(HEADS):
                    if att:
                        if h in (1, 5, 9):
                            q_transposes(h // 4 + 1, b, b, att, pre)
                        if h < HEADS - 1:
                            g = (h + 1) // 4
                            use = m_use(f"QT{g}", b, att, pre) if g else m_use("QT1", b, att, pre) - 1
                            scores(h + 1, b, use)
                    if moe and h == 0:
                        tok_transposes("YT", yn, yn_ready, m)
                    if moe and h == 1:
                        logits("LOG0", "wr", m)
                    if moe and 1 <= h <= X0:
                        gate_up(h - 1, m)
                    if att:
                        p_transposes(h, b)
                    if moe and 2 <= h <= X0 + 1:
                        expert_down(h - 2, m)
                    if moe and h == 11:
                        tok_transposes("X1T", acc, None, m)
                    if moe and h == 12:
                        logits("LOG1", "wt", m)
                        gate_up(X0, m)
                    if moe and h == 13:
                        gate_up(X0 + 1, m)
                        weight_transposes(m)
                    if moe and h == 14:
                        weight_rows(0, m)
                        gate_up(X0 + 2, m)
                    if moe and h == 15:
                        weight_rows(1, m)
                    if pre and h == 2:
                        x_transposes(b, att, pre)
                    if pre and h in (3, 4):
                        q_round(h - 3, b, att, pre)
                    if pre and h in (6, 7):
                        q_round(h - 4, b, att, pre)
                    if pre and h == 8:
                        kv_round(b, att, pre)
                    if att and h in (5, 9, 13):
                        o_transposes(h // 4 - 1, b, att, pre)
                    if att and h >= 1:
                        values(h - 1, b)
                if att:
                    values(HEADS - 1, b)
                    o_transposes(3, b, att, pre)
                if pre:
                    k_transposes(b, att, pre)
                if att:
                    out_projection(b, att, pre)
                if pre:
                    q_transposes(0, b + 1, b, att, pre)
                    scores(0, b + 1, m_use("QT0", b, att, pre))
                if moe:
                    layer1_down(m)

            pe.wait_ge(lo_split, CHUNKS)
            turn(-1, False, False, True)
            turn(0, True, False, True)
            with pe.Fori(1, B - 1) as b:
                turn(b, True, True, True)
            turn(B - 1, True, True, False)
            turn(B, False, True, False)

        @block.scalar
        def _(act):
            def split_hi(c):
                act.wait_ge(ld_w[c], 16)
                nc.scalar.activation(w_hi[:, c * CHUNK:(c + 1) * CHUNK], stage[c % 2], ACT.Copy).then_inc(hi_split, 1)

            split_hi(0)
            split_hi(1)
            for layer in range(2):
                act.wait_ge(set_dve, 5 + 3 * layer)
                nc.scalar.activation(hs, hb, ACT.Tanh, scale=0.5).then_inc(set_act, 1)
            split_hi(2)
            split_hi(3)

            def copy_m(name, b, att, pre, dst, scale=None, hi_only=False):
                u = m_use(name, b, att, pre)
                wait(act, m_full, u + 1)
                src = bank_m[:, 0:dst.free_size()]
                if scale is None:
                    i = nc.scalar.activation(dst, src, ACT.Copy)
                else:
                    i = nc.scalar.activation(dst, src, ACT.Copy, scale=scale)
                return i

            def copy_q(g, b, att, pre):
                bq = b + 1 if g == 0 else b
                wait(act, s_full, bq * HEADS + 4 * g - 4)
                copy_m(f"QT{g}", b, att, pre, qT[:, g % 2, :, :].rearrange("p j s -> p (j s)")).then_inc(m_free, 1)

            def copy_o(g, b, att, pre):
                copy_m(f"OT{g}", b, att, pre,
                       oT[:, 2 * g:2 * g + 2, :].rearrange("p j s -> p (j s)")).then_inc(m_free, 1)

            def exps(h, b):
                n = b * HEADS + h
                act.wait_ge(s_read, n + 1)
                p = prob[:, h % 2, :]
                for t, (at, w) in enumerate(((SB0, P + 1), (SB1, S + 1))):
                    i = nc.scalar.activation(p[:, at:at + w], p[:, at:at + w], ACT.Exp, scale=-1.0,
                                             bias=s_min[:, h % 2, t:t + 1], accum_out=s_sum[:, t, h:h + 1])
                i.then_inc(p_ready, 1)

            def copy_pt(h, b):
                n = b * HEADS + h
                act.wait_ge(pt_full, n + 1)
                wait(act, pv_done, n - 1)
                nc.scalar.activation(probT[:, h % 2, :], bank_pt[:, 0:3 * P], ACT.Copy).then_inc(pt_copied, 1)

            def gate_act(k, m):
                n = m * NGU + k
                act.wait_ge(g_full, n + 1)
                wait(act, g_read, n)
                w = S if k == X0 else 512
                if k < X0:
                    i = nc.scalar.activation(act_g[:, 0:w], bank_g[:, 0:w], ACT.Tanh, scale=0.5)
                else:
                    i = nc.scalar.activation(act_g[:, 0:w], bank_g[:, 0:w], ACT.Relu, scale=0.99)
                i.then_inc(act_ready, 1)

            def copy_hi(name, scale, m):
                act.wait_ge(d_full, d_use(name, m) + 1)
                nc.scalar.activation(yT_hi[:], bank_d[:, 0:S], ACT.Copy, scale=scale).then_inc(d_hi, 1)

            def route_tanh(i, m):
                act.wait_ge(diff_ready, 2 * m + i + 1)
                nc.scalar.activation(ltanh[:], ldiff[:], ACT.Tanh, scale=0.5).then_inc(tanh_ready, 1)

            def turn(b, att, moe, pre):
                m = b - 1
                for h in range(HEADS):
                    if att:
                        if h in (1, 5, 9):
                            copy_q(h // 4 + 1, b, att, pre)
                        if h < HEADS - 1:
                            exps(h + 1, b)
                    if moe and h == 0:
                        copy_hi("YT", col("g_out"), m)
                    if moe and 1 <= h <= X0:
                        gate_act(h - 1, m)
                    if att:
                        copy_pt(h, b)
                    if moe and h == 1:
                        route_tanh(0, m)
                    if moe and h == 11:
                        copy_hi("X1T", 1.0, m)
                    if moe and h == 12:
                        gate_act(X0, m)
                        route_tanh(1, m)
                    if moe and h == 13:
                        gate_act(X0 + 1, m)
                        act.wait_ge(d_full, d_use("WT", m) + 1)
                        nc.scalar.activation(wT[:], bank_d[0:E, 0:S], ACT.Copy).then_inc(d_free, 1)
                    if moe and h == 14:
                        gate_act(X0 + 2, m)
                    if pre and h == 2:
                        copy_m("XT", b, att, pre, xnT_hi[:], col("g_norm")).then_inc(m_hi, 1)
                    if pre and h in (3, 4, 6, 7):
                        r = h - 3 if h < 5 else h - 4
                        if r == 0:
                            wait(act, qn_ready, b + 1)
                        copy_m(f"Q{r}", b, att, pre, q_raw[:, r // 2, r % 2 * 512:(r % 2 + 1) * 512]).then_inc(m_free, 1)
                    if pre and h == 8:
                        wait(act, val_ready, b + 1)
                        copy_m("KV", b, att, pre, kv_raw[:].rearrange("p t n -> p (t n)")).then_inc(m_free, 1)
                    if att and h in (5, 9, 13):
                        copy_o(h // 4 - 1, b, att, pre)
                if att:
                    copy_o(3, b, att, pre)
                if pre:
                    wait(act, s_full, (b + 1) * HEADS)
                    copy_m("KT", b, att, pre, kT[:, SB1:SB1 + S], kscale[:, 0:1])
                    nc.scalar.activation(kT[:, SB0:SB0 + P], bank_m[:, 0:P], ACT.Copy,
                                         scale=kscale[:, 0:1]).then_inc(m_free, 1)
                    copy_q(0, b, att, pre)
                    exps(0, b + 1)

            act.wait_ge(set_dve, 11)
            turn(-1, False, False, True)
            turn(0, True, False, True)
            with act.Fori(1, B - 1) as b:
                turn(b, True, True, True)
            turn(B - 1, True, True, False)
            turn(B, False, True, False)

        @block.gpsimd
        def _(pool):
            for c in range(CHUNKS):
                pool.wait_ge(hi_split, c + 1)
                cs = slice(c * CHUNK, (c + 1) * CHUNK)
                nc.gpsimd.tensor_tensor(w_lo[:, cs], stage[c % 2], w_hi[:, cs].bitcast(F32),
                                        ALU.subtract).then_inc(lo_split, 1)

            def batch_mask(h, b):
                wait(pool, s_read, b * HEADS + h + 1)
                if h == 0:
                    pool.wait_ge(mask_ready, b + 2)
                nc.gpsimd.tensor_tensor(bias_b[:, h, SB1:SB1 + S + 1], bias_all[:, h, :],
                                        mask_row[:, SB1:SB1 + S + 1], ALU.add)
                nc.gpsimd.tensor_tensor(bias_b[:, h, SB0:SB0 + P + 1], bias_all[:, h, P:S + 1],
                                        mask_row[:, SB0:SB0 + P + 1], ALU.add).then_inc(batch_bias, 1)

            def square(k, b, att, pre):
                name = f"Q{k}" if k < 4 else "KV"
                pool.wait_ge(m_free, m_use(name, b, att, pre) + 1)
                wait(pool, ss_ready, (b + 1) * QROUNDS + k - 1)
                if k < 4:
                    src = q_raw[:, k // 2, k % 2 * 512:(k % 2 + 1) * 512]
                    dst = sq[:, k % 2, :]
                else:
                    src = kv_raw[:, :, 0:DH]
                    dst = sq[:, k % 2, 0:T * DH].rearrange("p (t d) -> p t d", t=T)
                nc.gpsimd.tensor_tensor(dst, src, src, ALU.mult).then_inc(sq_ready, 1)

            def turn(b, att, moe, pre):
                m = b - 1
                for h in range(HEADS):
                    if pre:
                        batch_mask(h, b)
                    if pre and h in (4, 5, 7, 8):
                        square(h - 4 if h < 6 else h - 5, b, att, pre)
                    if pre and h == 9:
                        square(4, b, att, pre)
                    if moe and h == 11:
                        pool.wait_ge(d_free, d_use("X1T", m))
                        wait(pool, out_ready, m)
                        nc.gpsimd.tensor_tensor(resid[:], acc[:], krow("ln_b")[:, None, :].broadcast_to([P, T, D]),
                                                ALU.add).then_inc(resid_ready, 1)
                if moe:
                    pool.wait_ge(norm_ready, m + 1)
                    pool.wait_ge(resid_ready, m + 1)
                    wait(pool, out_stored, 16 * m)
                    nc.gpsimd.tensor_tensor(out_sb[:], norm[:], resid[:], ALU.add).then_inc(out_ready, 1)

            pool.wait_ge(bias_ready, 1)
            pool.wait_ge(set_dve, 11)
            turn(-1, False, False, True)
            turn(0, True, False, True)
            with pool.Fori(1, B - 1) as b:
                turn(b, True, True, True)
            turn(B - 1, True, True, False)
            turn(B, False, True, False)

        @block.vector
        def _(dve):
            V = nc.vector
            chain = Steps(dve, sem("steps_set"), 0)
            chain.start(0)
            pre_steps = Steps(dve, steps_pre, PRE_STEPS)
            att_steps = Steps(dve, steps_att, ATT_STEPS)
            moe_steps = Steps(dve, steps_moe, MOE_STEPS)

            def rsqrt(steps, y, x, tmp):
                steps.link(V.tensor_scalar(y.bitcast(I32), x.bitcast(I32), 1, None, ALU.arith_shift_right))
                steps.link(V.tensor_scalar(y.bitcast(I32), y.bitcast(I32), -1.0, RSQRT_MAGIC, ALU.mult, ALU.add))
                for _ in range(3):
                    steps.link(V.tensor_tensor(tmp, y, y, ALU.mult))
                    steps.link(V.scalar_tensor_tensor(out=tmp, in0=tmp, scalar=-0.5, in1=x, op0=ALU.mult, op1=ALU.mult))
                    steps.link(V.scalar_tensor_tensor(out=y, in0=tmp, scalar=1.5, in1=y, op0=ALU.add, op1=ALU.mult))

            dve.wait_ge(ld_small, 64)
            for half in range(2):
                dve.wait_ge(set_pe, COND_T0 + half)
                V.tensor_copy(cond_rep[:, 4 * half:4 * half + 4, :],
                              bank_u[0:DH, :].rearrange("p (b n) -> p b n", b=4)).then_inc(set_dve, 1)
            dve.wait_ge(set_pe, COND)
            V.tensor_copy(cond_logit[:], bank_g[:, 0:B * E])
            dve.wait_ge(set_pe, NV_T)
            V.tensor_copy(nv_rep, bank_d[:, 0:P]).then_inc(set_dve, 1)
            nk2, nk_ss, nk_r, nk_t = kn[:, 1, :], rn[:, 0:1], rn[:, 1:2], rn[:, 2:3]
            chain.link(V.tensor_tensor(nk2, row("nk"), row("nk"), ALU.mult))
            chain.link(V.tensor_reduce(nk_ss, nk2[:, 0:DH], AX, ALU.add))
            chain.link(V.tensor_scalar(nk_ss, nk_ss, 1e-24, None, ALU.max))
            rsqrt(chain, nk_r, nk_ss, nk_t)
            V.tensor_scalar(kn[:, 0, :], row("nk"), nk_r, None, ALU.mult).then_inc(set_dve, 1)
            chain.link(V.tensor_tensor(kscale[:], col("q_scale"), col("k_scale"), ALU.mult))
            chain.link(V.tensor_scalar(kscale[:], kscale[:], -SCALE_QK, None, ALU.mult))
            chain.link(V.memset(kT[:], 0.0))
            dve.wait_ge(set_pe, NK_T)
            chain.link(V.tensor_scalar(kT[:, S:S + 1], bank_pt[:, 0:1], kscale[:, 0:1], None, ALU.mult))
            chain.link(V.tensor_scalar(kT[:, SB0 + P:SB0 + P + 1], bank_pt[:, 0:1], kscale[:, 0:1], None, ALU.mult))

            def bias_layer(layer):
                gain = row(f"g{layer}")
                if layer == 0:
                    for t in range(2):
                        first = V.scalar_tensor_tensor(out=hb[:, t, :], in0=row("w0"), scalar=col(f"pos{t}"),
                                                       in1=row("b0"), op0=ALU.mult, op1=ALU.add)
                    chain.link(first)
                if layer == 1:
                    dve.wait_ge(set_pe, HW1)
                    chain.link(V.tensor_tensor(hb, bank_pv[:, 0:2 * D].rearrange("p (t d) -> p t d", t=2),
                                               row("b1")[:, None, :].broadcast_to([P, 2, D]), ALU.add))
                for t in range(2):
                    stat = V.bn_stats(y_stat[:, t, :], hb[:, t, :])
                chain.link(stat)
                for t in range(2):
                    stat = V.bn_aggr(y_mv[:, t, :], y_stat[:, t, :])
                chain.link(stat)
                chain.link(V.tensor_scalar(y_var[:], y_mv[:, :, 1], LN_EPS, None, ALU.add))
                rsqrt(chain, y_rstd[:], y_var[:], y_tmp[:])
                for t in range(2):
                    chain.link(V.tensor_scalar(hb[:, t, :], hb[:, t, :], y_mv[:, t, 0:1], y_rstd[:, t:t + 1],
                                               ALU.subtract, ALU.mult))
                V.tensor_tensor(hb, hb, gain[:, None, :].broadcast_to([P, 2, D]), ALU.mult).then_inc(set_dve, 1)
                dve.wait_ge(set_act, layer + 1)
                chain.link(V.scalar_tensor_tensor(out=hs, in0=hs, scalar=1.0, in1=hb, op0=ALU.add, op1=ALU.mult))
                V.tensor_scalar(hs, hs, 0.5, None, ALU.mult).then_inc(set_dve, 1)
                dve.wait_ge(set_pe, HT0 + 2 * layer)
                V.tensor_copy(hT, bank_m[:, 0:2 * P]).then_inc(set_dve, 1)

            bias_layer(0)
            bias_layer(1)
            dve.wait_ge(set_pe, HW2)
            V.tensor_scalar(rel[:, 0:S], bank_pv[0:HEADS, 0:S], col("b2", HEADS), -1.0, ALU.add, ALU.mult)
            V.memset(rel[:, S:REL], BIG).then_inc(rel_ready, 1)
            dve.wait_ge(ld_x, 16)
            for i in range(B * T):
                stat = V.bn_stats(x_stat[:, i, :], x_sb[:, i, :])
            chain.link(stat)
            for i in range(B * T):
                stat = V.bn_aggr(x_mv[:, i, :], x_stat[:, i, :])
            chain.link(stat)
            chain.link(V.tensor_scalar(x_var[:], x_mv[:, :, 1], LN_EPS, None, ALU.add))
            rsqrt(chain, x_rstd[:], x_var[:], x_tmp[:])
            dve.wait_ge(ld_mask, 16)
            chain.link(V.memset(mask_add[:], 0.0))
            V.tensor_scalar(mask_add[:, :, SB1:SB1 + S], mask_u8[:], -BIG, BIG, ALU.mult, ALU.add)
            chain.link(V.tensor_scalar(mask_add[:, :, SB0:SB0 + P], mask_u8[:, :, 0:P], -BIG, BIG, ALU.mult, ALU.add))
            dve.wait_ge(set_pe, NULL_OUT)
            V.tensor_copy(null_out[:], bank_d[:, 0:D]).then_inc(set_dve, 1)
            dve.wait_ge(bias_loaded, 16)
            V.tensor_scalar(bias_all[:, :, S], krow("null_bias"), -1.0, None, ALU.mult).then_inc(bias_ready, 1)

            def carry_wait(at):
                V.memset(idle[:, at:at + 1], 0.0)

            def score_min(h, b):
                n = b * HEADS + h
                dve.wait_ge(s_full, n + 1)
                dve.wait_ge(batch_bias, n + 1)
                wait(dve, pt_full, n - 1)
                carry_wait(h)
                for t, (at, w) in enumerate(((SB0, P + 1), (SB1, S + 1))):
                    i = V.tensor_tensor_reduce(out=prob[:, h % 2, at:at + w], in0=bank_s[h % 2][:, at:at + w],
                                               in1=bias_b[:, h, at:at + w], scale=1.0, scalar=3e38, op0=ALU.add,
                                               op1=ALU.min, accum_out=s_min[:, h % 2, t:t + 1])
                i.then_inc(s_read, 1)

            def normalise_values(g, b):
                dve.wait_ge(pv_done, b * HEADS + 4 * g + 4)
                att_steps.link(V.reciprocal(r_sum[:], s_sum[:, :, 4 * g:4 * g + 4]))
                V.tensor_tensor(on[:, g % 2].rearrange("p t (h d) -> p t h d", h=4),
                                bank_pv[:].rearrange("p (t h d) -> p t h d", t=T, h=4),
                                r_sum[:, :, :, None].broadcast_to([P, T, 4, DH]), ALU.mult).then_inc(on_ready, 1)

            def output_norm(b, att, pre):
                use = m_use("WO", b, att, pre)
                dve.wait_ge(m_full, use + 1)
                V.tensor_tensor(y_raw[:], bank_m[:, 0:T * D].rearrange("p (t d) -> p t d", t=T),
                                null_out[:, None, :].broadcast_to([P, T, D]), ALU.add).then_inc(m_free, 1)
                dve.wait_ge(m_free, use + 1)
                for t in range(T):
                    stat = V.bn_stats(y_stat[:, t, :], y_raw[:, t, :])
                att_steps.link(stat)
                carry_wait(HEADS)
                for t in range(T):
                    stat = V.bn_aggr(y_mv[:, t, :], y_stat[:, t, :])
                att_steps.link(stat)
                att_steps.link(V.tensor_scalar(y_var[:], y_mv[:, :, 1], LN_EPS, None, ALU.add))
                rsqrt(att_steps, y_rstd[:], y_var[:], y_tmp[:])
                for t in range(T):
                    i = V.tensor_scalar(yn[:, t, :], y_raw[:, t, :], y_mv[:, t, 0:1], y_rstd[:, t:t + 1],
                                        ALU.subtract, ALU.mult)
                i.then_inc(yn_ready, 1)

            def take_mask(b):
                wait(dve, batch_bias, (b + 1) * HEADS)
                V.tensor_scalar(mask_row[:], mask_add[:, b + 1, :], 1.0, None, ALU.mult).then_inc(mask_ready, 1)

            def normalise_x(b):
                for t in range(T):
                    n = (b + 1) * T + t
                    i = V.tensor_scalar(xn[:, t, :], x_sb[:, n, :], x_mv[:, n, 0:1], x_rstd[:, bass.ds(n, 1)],
                                        ALU.subtract, ALU.mult)
                i.then_inc(xn_ready, 1)

            def x_low(b):
                dve.wait_ge(m_hi, b + 2)
                V.scalar_tensor_tensor(out=xnT_lo[:], in0=bank_m[:, 0:S], scalar=col("g_norm"),
                                       in1=xnT_hi[:].bitcast(F32), op0=ALU.mult, op1=ALU.subtract).then_inc(m_free, 1)

            def sum_squares(k, b):
                dve.wait_ge(sq_ready, (b + 1) * QROUNDS + k + 1)
                if k < 4:
                    dst, n = ss[:, k * E:(k + 1) * E], 512
                else:
                    dst, n = ss[:, T * HEADS:T * HEADS + T], T * DH
                V.tensor_reduce(dst, sq[:, k % 2, 0:n].rearrange("p (h d) -> p h d", d=DH), AX,
                                ALU.add).then_inc(ss_ready, 1)

            def normalise_qk(b, att, pre):
                dve.wait_ge(ss_ready, (b + 2) * QROUNDS)
                pre_steps.link(V.tensor_scalar(ss[:], ss[:], 1e-24, None, ALU.max))
                rsqrt(pre_steps, rn[:], ss[:], rn_tmp[:])
                if att:
                    dve.wait_ge(m_full, m_use("QT3", b, att, pre) + 1)
                for t in range(T):
                    i = V.tensor_tensor(qn[:, t, :].rearrange("p (h d) -> p h d", d=DH),
                                        q_raw[:, t, :].rearrange("p (h d) -> p h d", d=DH),
                                        rn[:, t * HEADS:(t + 1) * HEADS, None].broadcast_to([P, HEADS, DH]), ALU.mult)
                i.then_inc(qn_ready, 1)
                for t in range(T):
                    i = V.tensor_scalar(kn[:, t, :].rearrange("p (c d) -> p c d", c=2),
                                        kv_raw[:, t, None, 0:DH].broadcast_to([P, 2, DH]),
                                        rn[:, T * HEADS + t:T * HEADS + t + 1], None, ALU.mult)
                i.then_inc(kn_ready, 1)

            def shift_values(b):
                wait(dve, pv_done, (b + 1) * HEADS)
                V.tensor_tensor(val[:], kv_raw[:, :, DH:2 * DH], krow("nv_row")[:, None, :].broadcast_to([P, T, DH]),
                                ALU.subtract).then_inc(val_ready, 1)

            def token_low(name, i, scale, m):
                dve.wait_ge(d_hi, 2 * m + i + 1)
                V.scalar_tensor_tensor(out=yT_lo[:], in0=bank_d[:, 0:S], scalar=scale, in1=yT_hi[:].bitcast(F32),
                                       op0=ALU.mult, op1=ALU.subtract).then_inc(d_free, 1)

            def pick(src, dst):
                each = [P, T, E]
                moe_steps.link(V.tensor_reduce(top[:], src, AX, ALU.max))
                moe_steps.link(V.tensor_tensor(eq[:], src, top[:, :, None].broadcast_to(each), ALU.is_equal))
                moe_steps.link(V.tensor_tensor(eq[:], eq[:], rank, ALU.mult))
                moe_steps.link(V.tensor_reduce(top[:], eq[:], AX, ALU.max))
                moe_steps.link(V.tensor_tensor(dst, rank, top[:, :, None].broadcast_to(each), ALU.is_equal))

            def route(i, m):
                each = [P, T, E]
                use = d_use(f"LOG{i}", m)
                dve.wait_ge(d_full, use + 1)
                src = bank_d[:, 0:T * E].rearrange("p (t e) -> p t e", t=T)
                if i == 0:
                    V.tensor_scalar(lg[:], src, SCALE_R0, None, ALU.mult).then_inc(d_free, 1)
                    dve.wait_ge(d_free, use + 1)
                    moe_steps.link(V.tensor_tensor(cand[:], lg[:], krow("rb")[:, None, :].broadcast_to(each), ALU.add))
                    chosen = cand[:]
                else:
                    V.tensor_tensor(lg[:], src, cond_logit[:, bass.ds(m * E, E)][:, None, :].broadcast_to(each),
                                    ALU.add).then_inc(d_free, 1)
                    dve.wait_ge(d_free, use + 1)
                    moe_steps.link(V.tensor_scalar(lg[:], lg[:], 0.5, None, ALU.mult))
                    chosen = lg[:]
                pick(chosen, oh1[:])
                moe_steps.link(V.scalar_tensor_tensor(out=cand[:], in0=oh1[:], scalar=-BIG, in1=chosen,
                                                      op0=ALU.mult, op1=ALU.add))
                pick(cand[:], oh2[:])
                moe_steps.link(V.tensor_tensor(eq[:], oh1[:], oh2[:], ALU.subtract))
                moe_steps.link(V.tensor_tensor(cand[:], eq[:], lg[:], ALU.mult))
                V.tensor_reduce(ldiff[:], cand[:], AX, ALU.add).then_inc(diff_ready, 1)
                moe_steps.link(V.tensor_tensor(oh1[:], oh1[:], oh2[:], ALU.add))
                dve.wait_ge(tanh_ready, 2 * m + i + 1)
                moe_steps.link(V.tensor_tensor(eq[:], eq[:], ltanh[:, :, None].broadcast_to(each), ALU.mult))
                moe_steps.link(V.tensor_tensor(w_tok[:], eq[:], oh1[:], ALU.add))
                V.tensor_scalar(w_tok[:], w_tok[:], 0.25 if i == 0 else 0.5, None, ALU.mult).then_inc(w_ready, 1)

            def gate_up(k, m):
                n = m * NGU + k
                w = S if k == X0 else 512
                dve.wait_ge(act_ready, n + 1)
                wait(dve, u_read, n)
                if k < X0:
                    i = V.scalar_tensor_tensor(out=gated[:, 0:w], in0=act_g[:, 0:w], scalar=1.0, in1=bank_g[:, 0:w],
                                               op0=ALU.add, op1=ALU.mult)
                else:
                    i = V.scalar_tensor_tensor(out=gated[:, 0:w], in0=bank_g[:, 0:w], scalar=0.01, in1=act_g[:, 0:w],
                                               op0=ALU.mult, op1=ALU.add)
                i.then_inc(g_read, 1)
                dve.wait_ge(g_read, n + 1)
                dve.wait_ge(u_full, n + 1)
                if 2 <= k < X0:
                    dve.wait_ge(d_full, d_use(f"D{k - 2}", m) + 1)
                at = k % 2 * 512 if k < X0 else {X0: 4 * S, X0 + 1: 0, X0 + 2: 512}[k]
                V.tensor_tensor(hid[:, at:at + w], gated[:, 0:w], bank_u[:, 0:w], ALU.mult).then_inc(u_read, 1)

            def add_expert(e, m):
                use = d_use(f"D{e}", m)
                dve.wait_ge(d_full, use + 1)
                wait(dve, d_free, use)
                if e == 0:
                    dve.wait_ge(w_ready, 2 * m + 1)
                    wait(dve, resid_ready, m)
                for t in range(T):
                    before = x_sb[:, m * T + t, :] if e == 0 else acc[:, t, :]
                    scale = w_tok[:, t, e:e + 1] if e < E else 0.5
                    i = V.scalar_tensor_tensor(out=acc[:, t, :], in0=bank_d[:, t * D:(t + 1) * D], scalar=scale,
                                               in1=before, op0=ALU.mult, op1=ALU.add)
                i.then_inc(d_free, 1)

            def weight_hidden(r, m):
                dve.wait_ge(d_full, d_use(f"WB{r}", m) + 1)
                dve.wait_ge(u_read, m * NGU + X0 + 2 + r)
                h = hid[:, r * 512:(r + 1) * 512]
                V.tensor_tensor(h, h, bank_d[:], ALU.mult).then_inc(d_free, 1)

            def last_norm(m):
                use = d_use("DOWN", m)
                dve.wait_ge(d_full, use + 1)
                for t in range(T):
                    stat = V.bn_stats(o_stat[:, t, :], bank_d[:, t * D:(t + 1) * D])
                moe_steps.link(stat)
                carry_wait(HEADS + 1)
                for t in range(T):
                    stat = V.bn_aggr(o_mv[:, t, :], o_stat[:, t, :])
                moe_steps.link(stat)
                moe_steps.link(V.tensor_scalar(o_var[:], o_mv[:, :, 1], LN_EPS, None, ALU.add))
                rsqrt(moe_steps, o_rstd[:], o_var[:], o_tmp[:])
                wait(dve, out_ready, m)
                for t in range(T):
                    i = V.tensor_scalar(norm[:, t, :], bank_d[:, t * D:(t + 1) * D], o_mv[:, t, 0:1],
                                        o_rstd[:, t:t + 1], ALU.subtract, ALU.mult)
                i.then_inc(d_free, 1)
                dve.wait_ge(d_free, use + 1)
                V.tensor_tensor(norm[:], norm[:], krow("ln_g")[:, None, :].broadcast_to([P, T, D]),
                                ALU.mult).then_inc(norm_ready, 1)

            def turn(b, att, moe, pre):
                m = b - 1
                att_steps.start(b)
                pre_steps.start(b + 1)
                moe_steps.start(m)
                if pre:
                    take_mask(b)
                for h in range(HEADS):
                    if att and h in (5, 9, 13):
                        normalise_values(h // 4 - 1, b)
                    if att and h < HEADS - 1:
                        score_min(h + 1, b)
                    if moe and h == 0:
                        token_low("YT", 0, col("g_out"), m)
                    if moe and 1 <= h <= X0:
                        gate_up(h - 1, m)
                    if moe and h == 1:
                        route(0, m)
                    if moe and 2 <= h <= X0 + 1:
                        add_expert(h - 2, m)
                    if moe and h == 11:
                        token_low("X1T", 1, 1.0, m)
                    if moe and h == 12:
                        gate_up(X0, m)
                        route(1, m)
                    if moe and h == 13:
                        gate_up(X0 + 1, m)
                    if moe and h == 14:
                        weight_hidden(0, m)
                        gate_up(X0 + 2, m)
                    if moe and h == 15:
                        weight_hidden(1, m)
                    if pre and h == 1:
                        normalise_x(b)
                    if pre and h == 2:
                        x_low(b)
                    if pre and h in (5, 6, 8, 9, 10):
                        sum_squares({5: 0, 6: 1, 8: 2, 9: 3, 10: 4}[h], b)
                    if pre and h == 11:
                        normalise_qk(b, att, pre)
                if att:
                    normalise_values(3, b)
                if pre:
                    shift_values(b)
                if att:
                    output_norm(b, att, pre)
                    att_steps.end()
                if pre:
                    score_min(0, b + 1)
                    pre_steps.end()
                if moe:
                    last_norm(m)
                    moe_steps.end()

            turn(-1, False, False, True)
            turn(0, True, False, True)
            with dve.Fori(1, B - 1) as b:
                turn(b, True, True, True)
            turn(B - 1, True, True, False)
            turn(B, False, True, False)


def kernel(**inputs):
    import numpy as np
    import concourse.bacc as bacc
    from concourse.bass_utils import run_bass_kernel_spmd

    i = {name: np.asarray(a) for name, a in inputs.items()}
    assert i["x"].shape == (B, S, D) and i["x"].shape[0] // i["L1_ffn_Wq"].shape[0] == 0

    def by_input(w):
        return w.transpose(1, 0, 2).reshape(w.shape[1], -1)

    def by_chunk(w):
        return w.reshape(-1, P, w.shape[-1]).transpose(1, 0, 2).reshape(P, -1)

    def padded(w):
        return np.concatenate([w, np.zeros((P - w.shape[0], w.shape[1]), w.dtype)]) if w.shape[0] < P else w

    c = np.concatenate
    split = c([i["L0_cond_Wq"], i["L0_cond_Wkv"], i["L0_ffn_Wr"], i["L1_cond_wt"].T,
               by_input(i["L0_ffn_W3"]), i["L0_ffn_Ws3"], by_input(i["L0_ffn_W1"]), i["L0_ffn_Ws1"],
               by_input(i["L1_cond_w_gate"]), i["L1_cond_sw_gate"], by_input(i["L1_cond_w_up"]),
               i["L1_cond_sw_up"]], axis=1)
    down = c([by_chunk(i["L0_ffn_W2"].reshape(-1, D)), by_chunk(i["L0_ffn_Ws2"]), by_chunk(i["L0_cond_Wout"]),
              by_chunk(i["L1_cond_w_down"].reshape(-1, D)), i["L1_cond_sw_down"]], axis=1)
    cond = i["cond_64"]
    rows = c([i["L0_cond_w0"][0], i["L0_cond_b0"], i["L0_cond_g0"], i["L0_cond_b1"], i["L0_cond_g1"],
              cond[0], cond[0], cond[1], cond[1], cond.reshape(-1)])
    krows = c([i["L0_cond_null_attn_bias"], i["L0_ffn_rb"], i["L1_ffn_ln_g"], i["L1_ffn_ln_b"], cond[1]])
    pos = np.arange(S - 1, -1, -1, dtype=np.float32).reshape(2, P)
    b2 = c([i["L0_cond_b2"], np.zeros(P - HEADS, np.float32)])
    cols = np.stack([i["L0_cond_g_norm"], c([i["L0_cond_q_scale"]] * 2), c([i["L0_cond_k_scale"]] * 2),
                     i["L0_cond_g_out"], b2, pos[0], pos[1]], axis=1)
    rank = np.broadcast_to(np.tile(np.arange(E, 0, -1, dtype=np.float32), T), (P, T * E))
    sel = np.repeat(np.eye(E, dtype=np.float32), M1, axis=1)
    mats = c([i["L0_cond_w1"], i["L0_cond_w2"], padded(i["L1_cond_wg"].T), np.eye(P, dtype=np.float32), rank,
              padded(sel)], axis=1)
    arrays = {"x": i["x"], "mask": i["mask_BxS_bf1"].view(np.uint8), "split": split, "down": down, "rows": rows,
              "krows": krows, "cols": cols, "mats": mats}
    arrays = {name: np.ascontiguousarray(a) for name, a in arrays.items()}
    nc = bacc.Bacc("TRN2", target_bir_lowering=False, num_devices=1)
    args = [nc.dram_tensor(f"in_{name}", a.shape, mybir.dt.from_np(a.dtype), kind="ExternalInput").ap()
            for name, a in arrays.items()]
    rel = nc.dram_tensor("bias_by_distance", (HEADS, P, REL), F32, kind="Internal").ap()
    out = nc.dram_tensor("out", (B, S, D), F32, kind="ExternalOutput").ap()
    build(nc, *args, rel, out)
    r = run_bass_kernel_spmd(nc, [{f"in_{name}": a for name, a in arrays.items()}], core_ids=[0])
    return r.results[0]["out"]
```

```python
from contextlib import ExitStack

import concourse.bass as bass
from concourse import mybir

F32 = mybir.dt.float32
F32R = mybir.dt.float32r
BF16 = mybir.dt.bfloat16
I32 = mybir.dt.int32
U8 = mybir.dt.uint8
ALU = mybir.AluOpType
ACT = mybir.ActivationFunctionType
AX = mybir.AxisListType.X

P = 128
B, S, D = 8, 256, 128
T = S // P
HEADS, DH = 16, 64
PAIRS = HEADS // 2
GROUPS = HEADS // 4
E = 8
HID = 256
HC = HID // P
M1 = 64
X0 = E + 1
X1 = E // 2 + 1
BIG = 1e30
LN_EPS = 1e-5
SCALE_QK = 8.0
SCALE_R0 = 1.0 / float(D) ** 0.5
RSQRT_MAGIC = float(0x5F3759DF)
HALLEY_A = 0.375 ** 0.5
HALLEY_B = -1.25 / HALLEY_A

SPLIT = [("wq", HEADS * DH), ("wkv", 2 * DH), ("wr", E), ("wt", E), ("w3", X0 * HID), ("w1", X0 * HID),
         ("mg", X1 * P), ("mu", X1 * P)]
NSPLIT = sum(n for _, n in SPLIT)
CHUNKS = 4
CHUNK = NSPLIT // CHUNKS
DOWN = [("w2", X0 * HC * D), ("wout", PAIRS * D), ("wd", X1 * D)]
NDOWN = sum(n for _, n in DOWN)
ROWS = [("w0", D), ("b0", D), ("g0", D), ("b1", D), ("g1", D), ("nk", P), ("nv", P), ("cond", B * DH)]
NROWS = sum(n for _, n in ROWS)
KROWS = [("null_bias", HEADS), ("rb", E), ("ln_g", D), ("ln_b", D), ("nv_row", DH)]
NKROWS = sum(n for _, n in KROWS)
COLS = ["g_norm", "q_scale", "k_scale", "g_out", "b2", "pos0", "pos1"]
MATS = [("w1m", D), ("w2m", HEADS), ("wg", E), ("ident", P), ("sel", E // 2 * P)]
NMATS = sum(n for _, n in MATS)

KT = S + 2
SB1, SB0 = 0, KT
SW = KT + P + 2
REL = S + P

M_ALL = [("QT1", "att"), ("XT", "pre"), ("Q0", "pre"), ("OT3", "moe"), ("Q1", "pre"), ("WO", "moe"), ("Q2", "pre"),
         ("QT2", "att"), ("Q3", "pre"), ("KV", "pre"), ("OT0", "att"), ("QT3", "att"), ("OT1", "att"),
         ("QT0", "pre"), ("KT", "pre"), ("OT2", "att")]
Q_AT = {1: 0, 2: 1, 3: 2, 5: 3}
LEAD = 3
D_ALL = ["YT", "LOG0"] + [f"D{e}" for e in range(X0)] + ["X1T", "LOG1", "WT", "WB0", "WB1", "DOWN"]
ND = len(D_ALL)
NGU = X0 + 3
QROUNDS = 5

RSQRT_STEPS = 8
PRE_STEPS = 1 + RSQRT_STEPS
NORM_STEPS = 3 + RSQRT_STEPS
ROUTE_STEPS = 8


def offsets(parts):
    at, out = 0, {}
    for name, n in parts:
        out[name] = (at, n)
        at += n
    return out


def parts(b):
    return {"att": 0 <= b < B, "pre": b < B - 1, "moe": 1 <= b <= B, "tail": b >= 2}


FULL = {"att": True, "pre": True, "moe": True, "tail": True}


def m_order(has):
    return [name for name, part in M_ALL if has[part]]


def m_first(b):
    if isinstance(b, int):
        return sum(len(m_order(parts(i))) for i in range(-1, b))
    return b * len(M_ALL) + sum(len(m_order(parts(i))) for i in (-1, 0)) - len(M_ALL)


def m_use(name, b, has):
    return m_first(b) + m_order(has).index(name)


def d_use(name, m):
    return m * ND + D_ALL.index(name)


def wait(eng, sem, value):
    if isinstance(value, int) and value <= 0:
        return
    eng.wait_ge(sem, value)


class Steps:

    def __init__(self, eng, sem, per):
        self.eng, self.sem, self.per = eng, sem, per

    def start(self, b):
        self.b, self.k = b, 0

    def link(self, ins):
        self.k += 1
        ins.then_inc(self.sem, 1)
        self.eng.wait_ge(self.sem, self.b * self.per + self.k)

    def end(self):
        assert self.k == self.per, (self.k, self.per)


def build(nc, x_in, mask_in, split_in, down_in, rows_in, krows_in, cols_in, mats_in, rel_dram, out):
    with ExitStack() as ctx:
        def sb(name, shape, dt=F32):
            return ctx.enter_context(nc.sbuf_tensor(name, shape, dt))

        def sem(name):
            return ctx.enter_context(nc.semaphore(name))

        def bank(name):
            return ctx.enter_context(nc.psum_tensor(name, [P, 512], F32))
        bank_s = [bank("bank_s0"), bank("bank_s1")]
        bank_pt = bank("bank_pt")
        bank_pv = bank("bank_pv")
        bank_m = bank("bank_m")
        bank_g, bank_u, bank_d = bank("bank_g"), bank("bank_u"), bank("bank_d")

        w_hi, w_lo = sb("w_hi", [P, NSPLIT], F32R), sb("w_lo", [P, NSPLIT], F32R)
        down = sb("down", [P, NDOWN])
        krows, cols, mats = sb("krows", [P, NKROWS]), sb("cols", [P, len(COLS)]), sb("mats", [P, NMATS])
        x_sb = sb("x_sb", [P, B * T, D])
        bias_all = sb("bias_all", [P, HEADS, S + 1])
        bias_b = sb("bias_b", [P, HEADS, SW])
        mask_u8 = sb("mask_u8", [P, B, S], U8)
        mask_add = sb("mask_add", [P, B, SW], BF16)
        mask_row, idle = sb("mask_row", [P, SW]), sb("idle", [P, HEADS + 2])
        x_stat, x_mv = sb("x_stat", [P, B * T, 6]), sb("x_mv", [P, B * T, 2])
        x_var, x_rstd, x_tmp = sb("x_var", [P, B * T]), sb("x_rstd", [P, B * T]), sb("x_tmp", [P, B * T])
        kscale = sb("kscale", [P, 1])
        cond_logit = sb("cond_logit", [P, B * E])
        null_out = sb("null_out", [P, D])
        xn = sb("xn", [P, T, D])
        xnT_hi, xnT_lo = sb("xnT_hi", [P, S], F32R), sb("xnT_lo", [P, S], F32R)
        q_raw = sb("q_raw", [P, T, HEADS * DH])
        kv_raw = sb("kv_raw", [P, T, 2 * DH])
        sq = sb("sq", [P, 2, 512])
        ss, rn, rn_tmp = sb("ss", [P, T * HEADS + T]), sb("rn", [P, T * HEADS + T]), sb("rn_tmp", [P, T * HEADS + T])
        qn = sb("qn", [P, T, HEADS * DH])
        kn = sb("kn", [P, T, P])
        val = sb("val", [P, T, DH])
        kT = sb("kT", [P, SW])
        qT = sb("qT", [P, 2, 2, S])
        prob = sb("prob", [P, 4, SW])
        s_min, s_sum = sb("s_min", [P, 4, T]), sb("s_sum", [P, T, HEADS])
        probT = sb("probT", [P, 2, 3 * P])
        r_sum = sb("r_sum", [P, T, 4])
        on = sb("on", [P, 2, T, 4 * DH])
        oT = sb("oT", [P, PAIRS, S])
        y_raw, yn = sb("y_raw", [P, T, D]), sb("yn", [P, T, D])
        y_stat, y_mv, y_var = sb("y_stat", [P, T, 6]), sb("y_mv", [P, T, 2]), sb("y_var", [P, T])
        y_rstd, y_tmp = sb("y_rstd", [P, T]), sb("y_tmp", [P, T])
        yT_hi, yT_lo = sb("yT_hi", [P, S], F32R), sb("yT_lo", [P, S], F32R)
        act_g, gated = sb("act_g", [P, 512]), sb("gated", [P, 512])
        hid = sb("hid", [P, X1 * S])
        acc = sb("acc", [P, T, D])
        lg, chosen, top8, ldiff, w_tok = (sb(n, [P, T, E]) for n in ("lg", "chosen", "top8", "ldiff", "w_tok"))
        cand, cand_left = sb("cand", [P, T, 2 * E]), sb("cand_left", [P, T, 2 * E])
        lsum = sb("lsum", [P, T])
        wT = sb("wT", [E, S])
        o_stat, o_mv, o_var = sb("o_stat", [P, T, 6]), sb("o_mv", [P, T, 2]), sb("o_var", [P, T])
        o_rstd, o_tmp = sb("o_rstd", [P, T]), sb("o_tmp", [P, T])
        norm, resid, out_sb = sb("norm", [P, T, D]), sb("resid", [P, T, D]), sb("out_sb", [P, T, D])

        rows = q_raw[:].rearrange("p t n -> p (t n)")[:, 0:NROWS]
        stage = [oT[:].rearrange("p a s -> p (a s)")[:, 0:CHUNK], qn[:].rearrange("p t n -> p (t n)")[:, 0:CHUNK]]
        hb, hs, hT = sq[:, 0, 0:2 * D].rearrange("p (t d) -> p t d", t=2), \
            sq[:, 0, 2 * D:4 * D].rearrange("p (t d) -> p t d", t=2), sq[:, 1, 0:2 * D]
        rel = prob[0:HEADS, 0, 0:REL]
        cond_rep = bias_b[0:DH].rearrange("p h w -> p (h w)")[:, 0:B * P].rearrange("p (b n) -> p b n", b=B)
        nv_rep = xn[:, 0, :]

        so, do, ro, ko, mo = offsets(SPLIT), offsets(DOWN), offsets(ROWS), offsets(KROWS), offsets(MATS)

        def hi(name, a=0, n=None):
            at, size = so[name]
            return w_hi[:, at + a:at + a + (size if n is None else n)]

        def lo(name, a=0, n=None):
            at, size = so[name]
            return w_lo[:, at + a:at + a + (size if n is None else n)]

        def dn(name, i):
            return down[:, do[name][0] + i * D:do[name][0] + (i + 1) * D]

        def row(name):
            return rows[:, ro[name][0]:ro[name][0] + ro[name][1]]

        def krow(name):
            return krows[:, ko[name][0]:ko[name][0] + ko[name][1]]

        def mat(name):
            return mats[:, mo[name][0]:mo[name][0] + mo[name][1]]

        def col(name, n=P):
            return cols[0:n, COLS.index(name):COLS.index(name) + 1]

        ident = mat("ident")
        sel = mat("sel")[0:E, :]

        ld_small, ld_x, ld_mask, ld_down = sem("ld_small"), sem("ld_x"), sem("ld_mask"), sem("ld_down")
        ld_w = [sem(f"ld_w{c}") for c in range(CHUNKS)]
        rel_stored, bias_loaded, out_stored = sem("rel_stored"), sem("bias_loaded"), sem("out_stored")
        hi_split, lo_split = sem("hi_split"), sem("lo_split")
        set_pe, set_act, set_dve = sem("set_pe"), sem("set_act"), sem("set_dve")
        rel_ready, bias_ready = sem("rel_ready"), sem("bias_ready")
        steps_pre, steps_norm, steps_route, steps_last = (sem(n) for n in ("steps_pre", "steps_norm", "steps_route", "steps_last"))
        sum_ready = sem("sum_ready")
        m_full, m_free, m_hi = sem("m_full"), sem("m_free"), sem("m_hi")
        d_full, d_free, d_hi = sem("d_full"), sem("d_free"), sem("d_hi")
        xn_ready, sq_ready, ss_ready = sem("xn_ready"), sem("sq_ready"), sem("ss_ready")
        qn_ready, kn_ready, val_ready = sem("qn_ready"), sem("kn_ready"), sem("val_ready")
        batch_bias, mask_ready = sem("batch_bias"), sem("mask_ready")
        s_full, s_read, p_ready = sem("s_full"), sem("s_read"), sem("p_ready")
        pt_full, pt_copied, pv_done, on_ready = sem("pt_full"), sem("pt_copied"), sem("pv_done"), sem("on_ready")
        yn_ready = sem("yn_ready")
        g_full, act_ready, g_read = sem("g_full"), sem("act_ready"), sem("g_read")
        u_full, u_read = sem("u_full"), sem("u_read")
        diff_ready, tanh_ready, w_ready = sem("diff_ready"), sem("tanh_ready"), sem("w_ready")
        resid_ready, norm_ready, out_ready = sem("resid_ready"), sem("norm_ready"), sem("out_ready")

        block = ctx.enter_context(nc.Block())

        COND_T0, COND_T1, COND, NV_T, NK_T, HT0, HW1, HT1, HW2, NULL_OUT = range(1, 11)

        @block.sync
        def _(sp):
            sp.dma_start(cols[:], cols_in).then_inc(ld_small, 16)
            sp.dma_start(rows, rows_in.partition_broadcast(P)).then_inc(ld_small, 16)
            sp.dma_start(mats[:], mats_in).then_inc(ld_small, 16)
            sp.dma_start(krows[:], krows_in.partition_broadcast(P)).then_inc(ld_small, 16)
            sp.dma_start(x_sb[:], x_in.rearrange("b (t p) d -> p (b t) d", p=P)).then_inc(ld_x, 16)
            for c in range(2):
                sp.dma_start(stage[c], split_in[:, c * CHUNK:(c + 1) * CHUNK]).then_inc(ld_w[c], 16)
            sp.dma_start(mask_u8[:], mask_in.partition_broadcast(P)).then_inc(ld_mask, 16)
            sp.dma_start(down[:], down_in).then_inc(ld_down, 16)
            for c in range(2, CHUNKS):
                sp.wait_ge(lo_split, c - 1)
                sp.dma_start(stage[c % 2], split_in[:, c * CHUNK:(c + 1) * CHUNK]).then_inc(ld_w[c], 16)
            sp.wait_ge(rel_ready, 1)
            copies = rel_dram.rearrange("h i r -> h (i r)").rearrange("h (i r) -> h i r", r=REL)
            sp.dma_start(copies, rel[:, None, :].broadcast_to([HEADS, P, REL])).then_inc(rel_stored, 16)
            sp.wait_ge(rel_stored, 16)
            band = bass.AP(rel_dram.tensor, P - 1, [[REL - 1, P], [P * REL, HEADS], [1, S]])
            sp.dma_start(bias_all[:, :, 0:S], band).then_inc(bias_loaded, 16)
            out_v = out.rearrange("b (t p) d -> b p t d", p=P)

            def store(m):
                sp.wait_ge(out_ready, m + 1)
                sp.dma_start(out_v[m], out_sb[:]).then_inc(out_stored, 16)
            for m in range(B):
                store(m)
            sp.wait_ge(out_stored, 16 * B)

        @block.tensor
        def _(pe):
            def split3(dst, a_hi, a_lo, b_hi, b_lo):
                nc.tensor.matmul(dst, a_hi, b_hi, start=True, stop=False)
                nc.tensor.matmul(dst, a_lo, b_hi, start=False, stop=False)
                return nc.tensor.matmul(dst, a_hi, b_lo, start=False, stop=True)

            pe.wait_ge(ld_small, 64)
            for half in range(2):
                if half:
                    pe.wait_ge(set_dve, 1)
                for i in range(4):
                    b0 = (4 * half + i) * DH
                    mm = nc.tensor.transpose(bank_u[0:DH, i * P:(i + 1) * P], row("cond")[:, b0:b0 + DH], ident)
                mm.then_inc(set_pe, 1)
            pe.wait_ge(set_dve, 2)
            for b in range(B):
                mm = nc.tensor.matmul(bank_g[:, b * E:(b + 1) * E], cond_rep[:, b, :], mat("wg")[0:DH, :],
                                      start=True, stop=True)
            mm.then_inc(set_pe, 1)
            nc.tensor.transpose(bank_d[:, 0:P], row("nv"), ident).then_inc(set_pe, 1)
            pe.wait_ge(set_dve, 4)
            nc.tensor.transpose(bank_pt[:, 0:P], kn[:, 0, :], ident).then_inc(set_pe, 1)
            for layer in range(2):
                pe.wait_ge(set_dve, 6 + 3 * layer)
                for t in range(2):
                    mm = nc.tensor.transpose(bank_m[:, t * P:(t + 1) * P], hs[:, t, :], ident)
                mm.then_inc(set_pe, 1)
                pe.wait_ge(set_dve, 7 + 3 * layer)
                if layer == 0:
                    for t in range(2):
                        mm = nc.tensor.matmul(bank_pv[:, t * D:(t + 1) * D], hT[:, t * P:(t + 1) * P], mat("w1m"),
                                              start=True, stop=True)
                else:
                    mm = nc.tensor.matmul(bank_pv[0:HEADS, 0:S], mat("w2m"), hT, start=True, stop=True)
                mm.then_inc(set_pe, 1)
            pe.wait_ge(ld_down, 16)
            pe.wait_ge(set_dve, 3)
            for j in range(PAIRS):
                mm = nc.tensor.matmul(bank_d[:, 0:D], nv_rep, dn("wout", j), start=(j == 0), stop=(j == PAIRS - 1))
            mm.then_inc(set_pe, 1)
            pe.wait_ge(set_dve, 11)

            def take_m(name, b, has):
                wait(pe, m_free, m_use(name, b, has))

            def q_transposes(g, bq, b, has):
                take_m(f"QT{g}", b, has)
                pe.wait_ge(qn_ready, bq * GROUPS + g + 1)
                for j in range(2):
                    for t in range(T):
                        c = (2 * g + j) * P
                        mm = nc.tensor.transpose(bank_m[:, (j * T + t) * P:(j * T + t + 1) * P], qn[:, t, c:c + P], ident)
                mm.then_inc(m_full, 1)

            def scores(h, bq, use=None):
                g, j, o = h // 4, h % 4 // 2, DH * (h % 2)
                if use is not None:
                    pe.wait_ge(m_free, use + 1)
                wait(pe, s_read, bq * HEADS + h - 1)
                q = qT[o:o + DH, g % 2, j, :]
                dst = bank_s[h % 2]
                nc.tensor.matmul(dst[:, SB0:SB0 + P + 1], q[:, 0:P], kT[o:o + DH, SB0:SB0 + P + 1], start=True, stop=True)
                nc.tensor.matmul(dst[:, SB1:SB1 + S + 1], q[:, P:2 * P], kT[o:o + DH, SB1:SB1 + S + 1],
                                 start=True, stop=True).then_inc(s_full, 1)

            def p_transposes(h, b):
                n = b * HEADS + h
                pe.wait_ge(p_ready, n + 1)
                wait(pe, pt_copied, n)
                p = prob[:, h % 4, :]
                nc.tensor.transpose(bank_pt[:, 0:P], p[:, SB0:SB0 + P], ident)
                nc.tensor.transpose(bank_pt[:, P:2 * P], p[:, SB1:SB1 + P], ident)
                nc.tensor.transpose(bank_pt[:, 2 * P:3 * P], p[:, SB1 + P:SB1 + 2 * P], ident).then_inc(pt_full, 1)

            def values(h, b):
                n = b * HEADS + h
                pe.wait_ge(pt_copied, n + 1)
                if h == 0:
                    pe.wait_ge(val_ready, b + 1)
                if h % 4 == 0:
                    wait(pe, on_ready, b * GROUPS + h // 4)
                pt, o = probT[:, h % 2, :], (h % 4) * DH
                out0 = bank_pv[:, o:o + DH]
                out1 = bank_pv[:, 4 * DH + o:4 * DH + o + DH]
                nc.tensor.matmul(out0, pt[:, 0:P], val[:, 0, :], start=True, stop=True)
                nc.tensor.matmul(out1, pt[:, P:2 * P], val[:, 0, :], start=True, stop=False)
                nc.tensor.matmul(out1, pt[:, 2 * P:3 * P], val[:, 1, :], start=False, stop=True).then_inc(pv_done, 1)

            def o_transposes(g, bo, b, has):
                take_m(f"OT{g}", b, has)
                pe.wait_ge(on_ready, bo * GROUPS + g + 1)
                for j in range(2):
                    for t in range(T):
                        mm = nc.tensor.transpose(bank_m[:, (j * T + t) * P:(j * T + t + 1) * P],
                                                 on[:, g % 2, t, j * P:(j + 1) * P], ident)
                mm.then_inc(m_full, 1)

            def out_projection(b, has):
                take_m("WO", b, has)
                for t in range(T):
                    for j in range(PAIRS):
                        mm = nc.tensor.matmul(bank_m[:, t * D:(t + 1) * D], oT[:, j, t * P:(t + 1) * P], dn("wout", j),
                                              start=(j == 0), stop=(j == PAIRS - 1))
                mm.then_inc(m_full, 1)

            def x_transposes(b, has):
                take_m("XT", b, has)
                pe.wait_ge(xn_ready, b + 2)
                for t in range(T):
                    mm = nc.tensor.transpose(bank_m[:, t * P:(t + 1) * P], xn[:, t, :], ident)
                mm.then_inc(m_full, 1)

            def q_round(r, b, has):
                take_m(f"Q{r}", b, has)
                t, c = r // 2, r % 2 * 512
                split3(bank_m[:], xnT_hi[:, t * P:(t + 1) * P], xnT_lo[:, t * P:(t + 1) * P],
                       hi("wq", c, 512), lo("wq", c, 512)).then_inc(m_full, 1)

            def kv_round(b, has):
                take_m("KV", b, has)
                for t in range(T):
                    mm = split3(bank_m[:, t * P:(t + 1) * P], xnT_hi[:, t * P:(t + 1) * P],
                                xnT_lo[:, t * P:(t + 1) * P], hi("wkv"), lo("wkv"))
                mm.then_inc(m_full, 1)

            def k_transposes(b, has):
                take_m("KT", b, has)
                pe.wait_ge(kn_ready, b + 2)
                for t in range(T):
                    mm = nc.tensor.transpose(bank_m[:, t * P:(t + 1) * P], kn[:, t, :], ident)
                mm.then_inc(m_full, 1)

            def take_d(name, m):
                wait(pe, d_free, d_use(name, m))

            def tok_transposes(name, src, ready, m):
                take_d(name, m)
                if ready is not None:
                    pe.wait_ge(ready, m + 1)
                for t in range(T):
                    mm = nc.tensor.transpose(bank_d[:, t * P:(t + 1) * P], src[:, t, :], ident)
                mm.then_inc(d_full, 1)

            def logits(name, weight, m):
                take_d(name, m)
                for t in range(T):
                    mm = split3(bank_d[:, t * E:(t + 1) * E], yT_hi[:, t * P:(t + 1) * P],
                                yT_lo[:, t * P:(t + 1) * P], hi(weight), lo(weight))
                mm.then_inc(d_full, 1)

            def gate_up(k, m):
                if k < X0:
                    parts = [(("w3", "w1"), (k * HC + c) * P) for c in range(HC)]
                else:
                    pairs = {X0: [X1 - 1], X0 + 1: [0, 1], X0 + 2: [2, 3]}[k]
                    parts = [(("mg", "mu"), j * P) for j in pairs]
                for side, (dst, read, full) in enumerate(((bank_g, g_read, g_full), (bank_u, u_read, u_full))):
                    wait(pe, read, m * NGU + k)
                    for c, (names, at) in enumerate(parts):
                        mm = split3(dst[:, c * S:(c + 1) * S], hi(names[side], at, P), lo(names[side], at, P),
                                    yT_hi[:], yT_lo[:])
                    mm.then_inc(full, 1)

            def expert_down(e, m):
                take_d(f"D{e}", m)
                pe.wait_ge(u_read, m * NGU + e + 1)
                for t in range(T):
                    for c in range(HC):
                        h0 = (e % 2) * 512 + c * S + t * P
                        mm = nc.tensor.matmul(bank_d[:, t * D:(t + 1) * D], hid[:, h0:h0 + P], dn("w2", e * HC + c),
                                              start=(c == 0), stop=(c == HC - 1))
                mm.then_inc(d_full, 1)

            def weight_transposes(m):
                take_d("WT", m)
                pe.wait_ge(w_ready, 2 * m + 2)
                for t in range(T):
                    mm = nc.tensor.transpose(bank_d[0:E, t * P:(t + 1) * P], w_tok[:, t, :], ident)
                mm.then_inc(d_full, 1)

            def weight_rows(r, m):
                take_d(f"WB{r}", m)
                for j in range(2):
                    mm = nc.tensor.matmul(bank_d[:, j * S:(j + 1) * S], sel[:, (2 * r + j) * P:(2 * r + j + 1) * P],
                                          wT[:], start=True, stop=True)
                mm.then_inc(d_full, 1)

            def layer1_down(m):
                take_d("DOWN", m)
                for t in range(T):
                    for j in range(X1):
                        mm = nc.tensor.matmul(bank_d[:, t * D:(t + 1) * D], hid[:, j * S + t * P:j * S + (t + 1) * P],
                                              dn("wd", j), start=(j == 0), stop=(j == X1 - 1))
                mm.then_inc(d_full, 1)

            def turn(b, has):
                att, pre, moe, tail = (has[n] for n in ("att", "pre", "moe", "tail"))
                m, m1 = b - 1, b - 2
                for h in range(HEADS):
                    if moe and h == 2:
                        o_transposes(3, m, b, has)
                    if moe and h == 3:
                        out_projection(b, has)
                    ahead = h + LEAD
                    if att and ahead < HEADS:
                        scores(ahead, b, m_use(f"QT{ahead // 4}", b, has) if ahead % 4 == 0 else None)
                    if pre and ahead >= HEADS:
                        scores(ahead - HEADS, b + 1, m_use("KT", b, has) if ahead == HEADS else None)
                    if pre and h == 1:
                        x_transposes(b, has)
                    if pre and h == 12:
                        k_transposes(b, has)
                    if moe and h == 6:
                        tok_transposes("YT", yn, yn_ready, m)
                    if tail:
                        if h == 0:
                            tok_transposes("X1T", acc, None, m1)
                        if h == 1:
                            logits("LOG1", "wt", m1)
                        if h == 3:
                            weight_transposes(m1)
                        if h in (1, 2, 3):
                            gate_up(X0 + h - 1, m1)
                    if moe and h == 0:
                        values(HEADS - 1, m)
                    if moe and 6 < h < 6 + X0:
                        gate_up(h - 6, m)
                    if att:
                        p_transposes(h, b)
                    if att and h in (0, 4, 8):
                        q_transposes(h // 4 + 1, b, b, has)
                    if tail:
                        if h in (3, 4):
                            weight_rows(h - 3, m1)
                        if h == 5:
                            layer1_down(m1)
                    if moe and 7 <= h < 7 + X0:
                        expert_down(h - 7, m)
                    if pre and h in Q_AT:
                        q_round(Q_AT[h], b, has)
                    if pre and h == 6:
                        kv_round(b, has)
                    if pre and h == 11:
                        q_transposes(0, b + 1, b, has)
                    if moe and h == 6:
                        logits("LOG0", "wr", m)
                        gate_up(0, m)
                    if att and h >= 1:
                        values(h - 1, b)
                    if att and h in (6, 10, 14):
                        o_transposes((h - 6) // 4, b, b, has)

            pe.wait_ge(lo_split, CHUNKS)
            for b in (-1, 0, 1):
                turn(b, parts(b))
            with pe.Fori(2, B - 1) as b:
                turn(b, FULL)
            for b in (B - 1, B, B + 1):
                turn(b, parts(b))

        @block.scalar
        def _(act):
            def split_hi(c):
                act.wait_ge(ld_w[c], 16)
                nc.scalar.activation(w_hi[:, c * CHUNK:(c + 1) * CHUNK], stage[c % 2], ACT.Copy).then_inc(hi_split, 1)

            split_hi(0)
            split_hi(1)
            for layer in range(2):
                act.wait_ge(set_dve, 5 + 3 * layer)
                nc.scalar.activation(hs, hb, ACT.Tanh, scale=0.5).then_inc(set_act, 1)
            split_hi(2)
            split_hi(3)

            def copy_m(name, b, has, dst, scale=None):
                u = m_use(name, b, has)
                wait(act, m_full, u + 1)
                src = bank_m[:, 0:dst.free_size()]
                if scale is None:
                    i = nc.scalar.activation(dst, src, ACT.Copy)
                else:
                    i = nc.scalar.activation(dst, src, ACT.Copy, scale=scale)
                return i

            def copy_q(g, b, has):
                bq = b + 1 if g == 0 else b
                wait(act, s_full, bq * HEADS + 4 * g - 4)
                copy_m(f"QT{g}", b, has, qT[:, g % 2, :, :].rearrange("p j s -> p (j s)")).then_inc(m_free, 1)

            def copy_o(g, b, has):
                copy_m(f"OT{g}", b, has,
                       oT[:, 2 * g:2 * g + 2, :].rearrange("p j s -> p (j s)")).then_inc(m_free, 1)

            def exps(h, b):
                n = b * HEADS + h
                act.wait_ge(s_read, n + 1)
                p = prob[:, h % 4, :]
                for t, (at, w) in enumerate(((SB0, P + 1), (SB1, S + 1))):
                    i = nc.scalar.activation(p[:, at:at + w], p[:, at:at + w], ACT.Exp, scale=-1.0,
                                             bias=s_min[:, h % 4, t:t + 1], accum_out=s_sum[:, t, h:h + 1])
                i.then_inc(p_ready, 1)

            def copy_pt(h, b):
                n = b * HEADS + h
                act.wait_ge(pt_full, n + 1)
                wait(act, pv_done, n - 1)
                nc.scalar.activation(probT[:, h % 2, :], bank_pt[:, 0:3 * P], ACT.Copy).then_inc(pt_copied, 1)

            def gate_act(k, m):
                n = m * NGU + k
                act.wait_ge(g_full, n + 1)
                wait(act, g_read, n)
                w = S if k == X0 else 512
                if k < X0:
                    i = nc.scalar.activation(act_g[:, 0:w], bank_g[:, 0:w], ACT.Tanh, scale=0.5)
                else:
                    i = nc.scalar.activation(act_g[:, 0:w], bank_g[:, 0:w], ACT.Relu, scale=0.99)
                i.then_inc(act_ready, 1)

            def copy_hi(name, scale, m):
                act.wait_ge(d_full, d_use(name, m) + 1)
                nc.scalar.activation(yT_hi[:], bank_d[:, 0:S], ACT.Copy, scale=scale).then_inc(d_hi, 1)

            def route_tanh(i, m):
                act.wait_ge(diff_ready, 2 * m + i + 1)
                nc.scalar.activation(ldiff[:], ldiff[:], ACT.Tanh, scale=1.0 if i == 0 else 0.5).then_inc(tanh_ready, 1)

            def turn(b, has):
                att, pre, moe, tail = (has[n] for n in ("att", "pre", "moe", "tail"))
                m, m1 = b - 1, b - 2
                for h in range(HEADS):
                    if moe and h == 2:
                        copy_o(3, b, has)
                    if pre and h == 1:
                        copy_m("XT", b, has, xnT_hi[:], col("g_norm")).then_inc(m_hi, 1)
                    if pre and h == 12:
                        wait(act, s_full, (b + 1) * HEADS)
                        copy_m("KT", b, has, kT[:, SB1:SB1 + S], kscale[:, 0:1])
                        nc.scalar.activation(kT[:, SB0:SB0 + P], bank_m[:, 0:P], ACT.Copy,
                                             scale=kscale[:, 0:1]).then_inc(m_free, 1)
                    if moe and h == 6:
                        copy_hi("YT", col("g_out"), m)
                    if moe and h == 7:
                        route_tanh(0, m)
                    if tail:
                        if h == 0:
                            copy_hi("X1T", 1.0, m1)
                        if h == 2:
                            route_tanh(1, m1)
                        if h == 3:
                            act.wait_ge(d_full, d_use("WT", m1) + 1)
                            nc.scalar.activation(wT[:], bank_d[0:E, 0:S], ACT.Copy).then_inc(d_free, 1)
                        if h in (1, 2, 3):
                            gate_act(X0 + h - 1, m1)
                    if moe and 6 < h < 6 + X0:
                        gate_act(h - 6, m)
                    if att:
                        copy_pt(h, b)
                    if att and h in (0, 4, 8):
                        copy_q(h // 4 + 1, b, has)
                    if tail and h == 5:
                        act.wait_ge(d_full, d_use("DOWN", m1) + 1)
                        wait(act, out_ready, m1)
                        nc.scalar.activation(norm[:].rearrange("p t d -> p (t d)"), bank_d[:, 0:T * D],
                                             ACT.Copy).then_inc(d_free, 1)
                    if pre and h in Q_AT:
                        r = Q_AT[h]
                        if r == 0:
                            wait(act, qn_ready, (b + 1) * GROUPS)
                        copy_m(f"Q{r}", b, has, q_raw[:, r // 2, r % 2 * 512:(r % 2 + 1) * 512]).then_inc(m_free, 1)
                    if pre and h == 6:
                        wait(act, val_ready, b + 1)
                        copy_m("KV", b, has, kv_raw[:].rearrange("p t n -> p (t n)")).then_inc(m_free, 1)
                    if pre and h == 11:
                        copy_q(0, b, has)
                    if moe and h == 6:
                        gate_act(0, m)
                    if att and h in (6, 10, 14):
                        copy_o((h - 6) // 4, b, has)
                    ahead = h + LEAD
                    if att and ahead < HEADS:
                        exps(ahead, b)
                    if pre and ahead >= HEADS:
                        exps(ahead - HEADS, b + 1)

            act.wait_ge(set_dve, 11)
            for b in (-1, 0, 1):
                turn(b, parts(b))
            with act.Fori(2, B - 1) as b:
                turn(b, FULL)
            for b in (B - 1, B, B + 1):
                turn(b, parts(b))

        @block.gpsimd
        def _(pool):
            for c in range(CHUNKS):
                pool.wait_ge(hi_split, c + 1)
                cs = slice(c * CHUNK, (c + 1) * CHUNK)
                nc.gpsimd.tensor_tensor(w_lo[:, cs], stage[c % 2], w_hi[:, cs].bitcast(F32),
                                        ALU.subtract).then_inc(lo_split, 1)

            def batch_mask(h, b):
                wait(pool, s_read, b * HEADS + h + 1)
                if h == 0:
                    pool.wait_ge(mask_ready, b + 2)
                nc.gpsimd.tensor_tensor(bias_b[:, h, SB1:SB1 + S + 1], bias_all[:, h, :],
                                        mask_row[:, SB1:SB1 + S + 1], ALU.add)
                nc.gpsimd.tensor_tensor(bias_b[:, h, SB0:SB0 + P + 1], bias_all[:, h, P:S + 1],
                                        mask_row[:, SB0:SB0 + P + 1], ALU.add).then_inc(batch_bias, 1)

            def square(k, b, has):
                name = f"Q{k}" if k < 4 else "KV"
                pool.wait_ge(m_free, m_use(name, b, has) + 1)
                wait(pool, ss_ready, (b + 1) * QROUNDS + k - 1)
                if k < 4:
                    src = q_raw[:, k // 2, k % 2 * 512:(k % 2 + 1) * 512]
                    dst = sq[:, k % 2, :]
                else:
                    src = kv_raw[:, :, 0:DH]
                    dst = sq[:, k % 2, 0:T * DH].rearrange("p (t d) -> p t d", t=T)
                nc.gpsimd.tensor_tensor(dst, src, src, ALU.mult).then_inc(sq_ready, 1)

            def normalise_q(g, b, has):
                if g == 0:
                    pool.wait_ge(steps_pre, (b + 2) * PRE_STEPS)
                    if has["att"]:
                        pool.wait_ge(m_full, m_use("QT3", b, has) + 1)
                c = slice(4 * g * DH, 4 * (g + 1) * DH)
                inverse = rn[:, 0:T * HEADS].rearrange("p (t h) -> p t h", t=T)[:, :, 4 * g:4 * g + 4]
                nc.gpsimd.tensor_tensor(qn[:, :, c].rearrange("p t (h d) -> p t h d", d=DH),
                                        q_raw[:, :, c].rearrange("p t (h d) -> p t h d", d=DH),
                                        inverse[:, :, :, None].broadcast_to([P, T, 4, DH]), ALU.mult).then_inc(qn_ready, 1)

            def turn(b, has):
                for h in range(HEADS):
                    if has["pre"] and 10 <= h < 10 + GROUPS:
                        normalise_q(h - 10, b, has)
                    if has["pre"]:
                        batch_mask(h, b)
                        if h - 1 in Q_AT:
                            square(Q_AT[h - 1], b, has)
                        if h == 7:
                            square(4, b, has)
                    if has["tail"] and h == 1:
                        pool.wait_ge(d_free, d_use("X1T", b - 2))
                        wait(pool, out_ready, b - 2)
                        nc.gpsimd.tensor_tensor(resid[:], acc[:], krow("ln_b")[:, None, :].broadcast_to([P, T, D]),
                                                ALU.add).then_inc(resid_ready, 1)
                    if has["tail"] and h == 14:
                        pool.wait_ge(norm_ready, b - 1)
                        pool.wait_ge(resid_ready, b - 1)
                        wait(pool, out_stored, 16 * (b - 2))
                        nc.gpsimd.tensor_tensor(out_sb[:], norm[:], resid[:], ALU.add).then_inc(out_ready, 1)

            pool.wait_ge(bias_ready, 1)
            pool.wait_ge(set_dve, 11)
            for b in (-1, 0, 1):
                turn(b, parts(b))
            with pool.Fori(2, B - 1) as b:
                turn(b, FULL)
            for b in (B - 1, B, B + 1):
                turn(b, parts(b))

        @block.vector
        def _(dve):
            V = nc.vector
            chain = Steps(dve, sem("steps_set"), 0)
            chain.start(0)
            pre_steps = Steps(dve, steps_pre, PRE_STEPS)
            norm_steps = Steps(dve, steps_norm, NORM_STEPS)
            route_steps = Steps(dve, steps_route, ROUTE_STEPS)
            last_steps = Steps(dve, steps_last, NORM_STEPS + 1)

            def rsqrt(steps, y, x, tmp):
                rsqrt_begin(steps, y, x, tmp)
                rsqrt_end(steps, y, x, tmp)

            def rsqrt_begin(steps, y, x, tmp):
                steps.link(V.tensor_scalar(y.bitcast(I32), x.bitcast(I32), -0.5, RSQRT_MAGIC, ALU.mult, ALU.add))
                steps.link(V.tensor_tensor(tmp, y, y, ALU.mult))
                steps.link(V.scalar_tensor_tensor(out=tmp, in0=tmp, scalar=-0.5, in1=x, op0=ALU.mult, op1=ALU.mult))
                steps.link(V.scalar_tensor_tensor(out=y, in0=tmp, scalar=1.5, in1=y, op0=ALU.add, op1=ALU.mult))

            def rsqrt_end(steps, y, x, tmp):
                steps.link(V.tensor_tensor(tmp, y, y, ALU.mult))
                steps.link(V.scalar_tensor_tensor(out=tmp, in0=tmp, scalar=HALLEY_A, in1=x, op0=ALU.mult, op1=ALU.mult))
                steps.link(V.scalar_tensor_tensor(out=tmp, in0=tmp, scalar=HALLEY_B, in1=tmp, op0=ALU.add, op1=ALU.mult))
                steps.link(V.scalar_tensor_tensor(out=y, in0=tmp, scalar=1.875, in1=y, op0=ALU.add, op1=ALU.mult))

            dve.wait_ge(ld_small, 64)
            for half in range(2):
                dve.wait_ge(set_pe, COND_T0 + half)
                V.tensor_copy(cond_rep[:, 4 * half:4 * half + 4, :],
                              bank_u[0:DH, :].rearrange("p (b n) -> p b n", b=4)).then_inc(set_dve, 1)
            dve.wait_ge(set_pe, COND)
            V.tensor_copy(cond_logit[:], bank_g[:, 0:B * E])
            dve.wait_ge(set_pe, NV_T)
            V.tensor_copy(nv_rep, bank_d[:, 0:P]).then_inc(set_dve, 1)
            nk2, nk_ss, nk_r, nk_t = kn[:, 1, :], rn[:, 0:1], rn[:, 1:2], rn[:, 2:3]
            chain.link(V.tensor_tensor(nk2, row("nk"), row("nk"), ALU.mult))
            chain.link(V.tensor_reduce(nk_ss, nk2[:, 0:DH], AX, ALU.add))
            chain.link(V.tensor_scalar(nk_ss, nk_ss, 1e-24, None, ALU.max))
            rsqrt(chain, nk_r, nk_ss, nk_t)
            V.tensor_scalar(kn[:, 0, :], row("nk"), nk_r, None, ALU.mult).then_inc(set_dve, 1)
            chain.link(V.tensor_tensor(kscale[:], col("q_scale"), col("k_scale"), ALU.mult))
            chain.link(V.tensor_scalar(kscale[:], kscale[:], -SCALE_QK, None, ALU.mult))
            chain.link(V.memset(kT[:], 0.0))
            dve.wait_ge(set_pe, NK_T)
            chain.link(V.tensor_scalar(kT[:, S:S + 1], bank_pt[:, 0:1], kscale[:, 0:1], None, ALU.mult))
            chain.link(V.tensor_scalar(kT[:, SB0 + P:SB0 + P + 1], bank_pt[:, 0:1], kscale[:, 0:1], None, ALU.mult))

            def bias_layer(layer):
                gain = row(f"g{layer}")
                if layer == 0:
                    for t in range(2):
                        first = V.scalar_tensor_tensor(out=hb[:, t, :], in0=row("w0"), scalar=col(f"pos{t}"),
                                                       in1=row("b0"), op0=ALU.mult, op1=ALU.add)
                    chain.link(first)
                if layer == 1:
                    dve.wait_ge(set_pe, HW1)
                    chain.link(V.tensor_tensor(hb, bank_pv[:, 0:2 * D].rearrange("p (t d) -> p t d", t=2),
                                               row("b1")[:, None, :].broadcast_to([P, 2, D]), ALU.add))
                for t in range(2):
                    stat = V.bn_stats(y_stat[:, t, :], hb[:, t, :])
                chain.link(stat)
                for t in range(2):
                    stat = V.bn_aggr(y_mv[:, t, :], y_stat[:, t, :])
                chain.link(stat)
                chain.link(V.tensor_scalar(y_var[:], y_mv[:, :, 1], LN_EPS, None, ALU.add))
                rsqrt(chain, y_rstd[:], y_var[:], y_tmp[:])
                for t in range(2):
                    chain.link(V.tensor_scalar(hb[:, t, :], hb[:, t, :], y_mv[:, t, 0:1], y_rstd[:, t:t + 1],
                                               ALU.subtract, ALU.mult))
                V.tensor_tensor(hb, hb, gain[:, None, :].broadcast_to([P, 2, D]), ALU.mult).then_inc(set_dve, 1)
                dve.wait_ge(set_act, layer + 1)
                chain.link(V.scalar_tensor_tensor(out=hs, in0=hs, scalar=1.0, in1=hb, op0=ALU.add, op1=ALU.mult))
                V.tensor_scalar(hs, hs, 0.5, None, ALU.mult).then_inc(set_dve, 1)
                dve.wait_ge(set_pe, HT0 + 2 * layer)
                V.tensor_copy(hT, bank_m[:, 0:2 * P]).then_inc(set_dve, 1)

            bias_layer(0)
            bias_layer(1)
            dve.wait_ge(set_pe, HW2)
            V.tensor_scalar(rel[:, 0:S], bank_pv[0:HEADS, 0:S], col("b2", HEADS), -1.0, ALU.add, ALU.mult)
            V.memset(rel[:, S:REL], BIG).then_inc(rel_ready, 1)
            dve.wait_ge(ld_x, 16)
            for i in range(B * T):
                stat = V.bn_stats(x_stat[:, i, :], x_sb[:, i, :])
            chain.link(stat)
            for i in range(B * T):
                stat = V.bn_aggr(x_mv[:, i, :], x_stat[:, i, :])
            chain.link(stat)
            chain.link(V.tensor_scalar(x_var[:], x_mv[:, :, 1], LN_EPS, None, ALU.add))
            rsqrt(chain, x_rstd[:], x_var[:], x_tmp[:])
            chain.link(V.memset(cand[:, :, E:2 * E], -BIG))
            dve.wait_ge(ld_mask, 16)
            chain.link(V.memset(mask_add[:], 0.0))
            V.tensor_scalar(mask_add[:, :, SB1:SB1 + S], mask_u8[:], -BIG, BIG, ALU.mult, ALU.add)
            chain.link(V.tensor_scalar(mask_add[:, :, SB0:SB0 + P], mask_u8[:, :, 0:P], -BIG, BIG, ALU.mult, ALU.add))
            dve.wait_ge(set_pe, NULL_OUT)
            V.tensor_copy(null_out[:], bank_d[:, 0:D]).then_inc(set_dve, 1)
            dve.wait_ge(bias_loaded, 16)
            V.tensor_scalar(bias_all[:, :, S], krow("null_bias"), -1.0, None, ALU.mult).then_inc(bias_ready, 1)

            def carry_wait(at):
                V.memset(idle[:, at:at + 1], 0.0)

            def score_min(h, b):
                n = b * HEADS + h
                dve.wait_ge(s_full, n + 1)
                dve.wait_ge(batch_bias, n + 1)
                wait(dve, pt_full, n - 3)
                carry_wait(h)
                for t, (at, w) in enumerate(((SB0, P + 1), (SB1, S + 1))):
                    i = V.tensor_tensor_reduce(out=prob[:, h % 4, at:at + w], in0=bank_s[h % 2][:, at:at + w],
                                               in1=bias_b[:, h, at:at + w], scale=1.0, scalar=3e38, op0=ALU.add,
                                               op1=ALU.min, accum_out=s_min[:, h % 4, t:t + 1])
                i.then_inc(s_read, 1)

            def normalise_values(g, b):
                dve.wait_ge(pv_done, b * HEADS + 4 * g + 4)
                V.reciprocal(r_sum[:], s_sum[:, :, 4 * g:4 * g + 4]).then_inc(sum_ready, 1)
                dve.wait_ge(sum_ready, b * GROUPS + g + 1)
                V.tensor_tensor(on[:, g % 2].rearrange("p t (h d) -> p t h d", h=4),
                                bank_pv[:].rearrange("p (t h d) -> p t h d", t=T, h=4),
                                r_sum[:, :, :, None].broadcast_to([P, T, 4, DH]), ALU.mult).then_inc(on_ready, 1)

            def take_output(b, has):
                use = m_use("WO", b, has)
                dve.wait_ge(m_full, use + 1)
                V.tensor_tensor(y_raw[:], bank_m[:, 0:T * D].rearrange("p (t d) -> p t d", t=T),
                                null_out[:, None, :].broadcast_to([P, T, D]), ALU.add).then_inc(m_free, 1)

            def output_norm(b, has):
                norm_steps.start(b - 1)
                dve.wait_ge(m_free, m_use("WO", b, has) + 1)
                for t in range(T):
                    stat = V.bn_stats(y_stat[:, t, :], y_raw[:, t, :])
                norm_steps.link(stat)
                carry_wait(HEADS)
                for t in range(T):
                    stat = V.bn_aggr(y_mv[:, t, :], y_stat[:, t, :])
                norm_steps.link(stat)
                norm_steps.link(V.tensor_scalar(y_var[:], y_mv[:, :, 1], LN_EPS, None, ALU.add))
                rsqrt(norm_steps, y_rstd[:], y_var[:], y_tmp[:])
                for t in range(T):
                    i = V.tensor_scalar(yn[:, t, :], y_raw[:, t, :], y_mv[:, t, 0:1], y_rstd[:, t:t + 1],
                                        ALU.subtract, ALU.mult)
                i.then_inc(yn_ready, 1)
                norm_steps.end()

            def take_mask(b):
                wait(dve, batch_bias, (b + 1) * HEADS)
                V.tensor_scalar(mask_row[:], mask_add[:, b + 1, :], 1.0, None, ALU.mult).then_inc(mask_ready, 1)

            def normalise_x(b):
                for t in range(T):
                    n = (b + 1) * T + t
                    i = V.tensor_scalar(xn[:, t, :], x_sb[:, n, :], x_mv[:, n, 0:1], x_rstd[:, bass.ds(n, 1)],
                                        ALU.subtract, ALU.mult)
                i.then_inc(xn_ready, 1)

            def x_low(b):
                dve.wait_ge(m_hi, b + 2)
                V.scalar_tensor_tensor(out=xnT_lo[:], in0=bank_m[:, 0:S], scalar=col("g_norm"),
                                       in1=xnT_hi[:].bitcast(F32), op0=ALU.mult, op1=ALU.subtract).then_inc(m_free, 1)

            def sum_squares(k, b):
                dve.wait_ge(sq_ready, (b + 1) * QROUNDS + k + 1)
                if k < 4:
                    dst, n = ss[:, k * E:(k + 1) * E], 512
                else:
                    dst, n = ss[:, T * HEADS:T * HEADS + T], T * DH
                V.tensor_reduce(dst, sq[:, k % 2, 0:n].rearrange("p (h d) -> p h d", d=DH), AX,
                                ALU.add).then_inc(ss_ready, 1)

            def inverse_norms(b):
                dve.wait_ge(ss_ready, (b + 2) * QROUNDS)
                pre_steps.start(b + 1)
                pre_steps.link(V.tensor_scalar(ss[:], ss[:], 1e-24, None, ALU.max))
                rsqrt_begin(pre_steps, rn[:], ss[:], rn_tmp[:])

            def normalise_k(b):
                rsqrt_end(pre_steps, rn[:], ss[:], rn_tmp[:])
                pre_steps.end()
                for t in range(T):
                    i = V.tensor_scalar(kn[:, t, :].rearrange("p (c d) -> p c d", c=2),
                                        kv_raw[:, t, None, 0:DH].broadcast_to([P, 2, DH]),
                                        rn[:, T * HEADS + t:T * HEADS + t + 1], None, ALU.mult)
                i.then_inc(kn_ready, 1)

            def shift_values(b):
                wait(dve, pv_done, b * HEADS)
                V.tensor_tensor(val[:], kv_raw[:, :, DH:2 * DH], krow("nv_row")[:, None, :].broadcast_to([P, T, DH]),
                                ALU.subtract).then_inc(val_ready, 1)

            def token_low(name, i, scale, m):
                dve.wait_ge(d_hi, 2 * m + i + 1)
                V.scalar_tensor_tensor(out=yT_lo[:], in0=bank_d[:, 0:S], scalar=scale, in1=yT_hi[:].bitcast(F32),
                                       op0=ALU.mult, op1=ALU.subtract).then_inc(d_free, 1)

            def route(i, m):
                route_steps.start(2 * m + i)
                each = [P, T, E]
                use = d_use(f"LOG{i}", m)
                dve.wait_ge(d_full, use + 1)
                src = bank_d[:, 0:T * E].rearrange("p (t e) -> p t e", t=T)
                if i == 0:
                    V.tensor_scalar(lg[:], src, SCALE_R0, None, ALU.mult).then_inc(d_free, 1)
                    dve.wait_ge(d_free, use + 1)
                    route_steps.link(V.tensor_tensor(cand[:, :, 0:E], lg[:], krow("rb")[:, None, :].broadcast_to(each),
                                                     ALU.add))
                else:
                    V.tensor_tensor(lg[:], src, cond_logit[:, bass.ds(m * E, E)][:, None, :].broadcast_to(each),
                                    ALU.add).then_inc(d_free, 1)
                    dve.wait_ge(d_free, use + 1)
                    route_steps.link(V.tensor_scalar(cand[:, :, 0:E], lg[:], 1.0, None, ALU.mult))
                carry_wait(HEADS)
                for t in range(T):
                    first = V.max(out=top8[:, t, :], in_=cand[:, t, 0:E])
                route_steps.link(first)
                route_steps.link(V.memset(top8[:, :, 2:E], -BIG))
                carry_wait(HEADS + 1)
                for t in range(T):
                    out = V.match_replace(out=cand_left[:, t, :], in_to_replace=top8[:, t, :], in_values=cand[:, t, :],
                                          imm_value=-2 * BIG)
                route_steps.link(out)
                route_steps.link(V.tensor_tensor(chosen[:], cand_left[:, :, 0:E], cand[:, :, 0:E], ALU.not_equal))
                route_steps.link(V.tensor_tensor(ldiff[:], chosen[:], lg[:], ALU.mult))
                route_steps.link(V.tensor_reduce(lsum[:], ldiff[:], AX, ALU.add))
                V.scalar_tensor_tensor(out=ldiff[:], in0=lsum[:, :, None].broadcast_to(each), scalar=-0.5, in1=lg[:],
                                       op0=ALU.mult, op1=ALU.add).then_inc(diff_ready, 1)

            def route_weights(i, m):
                dve.wait_ge(tanh_ready, 2 * m + i + 1)
                w = V.scalar_tensor_tensor(out=w_tok[:], in0=ldiff[:], scalar=1.0, in1=chosen[:],
                                           op0=ALU.add, op1=ALU.mult)
                route_steps.link(w)
                V.tensor_scalar(w_tok[:], w_tok[:], 0.25 if i == 0 else 0.5, None, ALU.mult).then_inc(w_ready, 1)
                route_steps.end()

            def gate_up(k, m):
                n = m * NGU + k
                w = S if k == X0 else 512
                dve.wait_ge(act_ready, n + 1)
                wait(dve, u_read, n)
                if k < X0:
                    i = V.scalar_tensor_tensor(out=gated[:, 0:w], in0=act_g[:, 0:w], scalar=1.0, in1=bank_g[:, 0:w],
                                               op0=ALU.add, op1=ALU.mult)
                else:
                    i = V.scalar_tensor_tensor(out=gated[:, 0:w], in0=bank_g[:, 0:w], scalar=0.01, in1=act_g[:, 0:w],
                                               op0=ALU.mult, op1=ALU.add)
                i.then_inc(g_read, 1)
                dve.wait_ge(g_read, n + 1)
                dve.wait_ge(u_full, n + 1)
                if 2 <= k < X0:
                    dve.wait_ge(d_full, d_use(f"D{k - 2}", m) + 1)
                at = k % 2 * 512 if k < X0 else {X0: 4 * S, X0 + 1: 0, X0 + 2: 512}[k]
                V.tensor_tensor(hid[:, at:at + w], gated[:, 0:w], bank_u[:, 0:w], ALU.mult).then_inc(u_read, 1)

            def add_expert(e, m):
                use = d_use(f"D{e}", m)
                dve.wait_ge(d_full, use + 1)
                wait(dve, d_free, use)
                if e == 0:
                    dve.wait_ge(w_ready, 2 * m + 1)
                    wait(dve, resid_ready, m)
                for t in range(T):
                    before = x_sb[:, m * T + t, :] if e == 0 else acc[:, t, :]
                    scale = w_tok[:, t, e:e + 1] if e < E else 0.5
                    i = V.scalar_tensor_tensor(out=acc[:, t, :], in0=bank_d[:, t * D:(t + 1) * D], scalar=scale,
                                               in1=before, op0=ALU.mult, op1=ALU.add)
                i.then_inc(d_free, 1)

            def weight_hidden(r, m):
                dve.wait_ge(d_full, d_use(f"WB{r}", m) + 1)
                dve.wait_ge(u_read, m * NGU + X0 + 2 + r)
                h = hid[:, r * 512:(r + 1) * 512]
                V.tensor_tensor(h, h, bank_d[:], ALU.mult).then_inc(d_free, 1)

            def last_stats(m):
                last_steps.start(m)
                dve.wait_ge(d_free, d_use("DOWN", m) + 1)
                for t in range(T):
                    stat = V.bn_stats(o_stat[:, t, :], norm[:, t, :])
                last_steps.link(stat)
                carry_wait(HEADS + 1)
                for t in range(T):
                    stat = V.bn_aggr(o_mv[:, t, :], o_stat[:, t, :])
                last_steps.link(stat)
                last_steps.link(V.tensor_scalar(o_var[:], o_mv[:, :, 1], LN_EPS, None, ALU.add))

            def last_rsqrt(m):
                rsqrt(last_steps, o_rstd[:], o_var[:], o_tmp[:])

            def last_scale(m):
                for t in range(T):
                    i = V.tensor_scalar(norm[:, t, :], norm[:, t, :], o_mv[:, t, 0:1], o_rstd[:, t:t + 1],
                                        ALU.subtract, ALU.mult)
                last_steps.link(i)
                last_steps.end()
                V.tensor_tensor(norm[:], norm[:], krow("ln_g")[:, None, :].broadcast_to([P, T, D]),
                                ALU.mult).then_inc(norm_ready, 1)

            def turn(b, has):
                att, pre, moe, tail = (has[n] for n in ("att", "pre", "moe", "tail"))
                m, m1 = b - 1, b - 2
                for h in range(HEADS):
                    if pre and h == 0:
                        normalise_x(b)
                    if pre and h == 1:
                        x_low(b)
                    if att and h in (5, 9, 13):
                        normalise_values((h - 5) // 4, b)
                    if moe and h == 3:
                        take_output(b, has)
                    if moe and h == 6:
                        token_low("YT", 0, col("g_out"), m)
                    if tail:
                        if h == 0:
                            token_low("X1T", 1, 1.0, m1)
                        if h in (1, 2, 3):
                            gate_up(X0 + h - 1, m1)
                    if moe and 6 < h < 6 + X0:
                        gate_up(h - 6, m)
                    ahead = h + LEAD
                    if att and ahead < HEADS:
                        score_min(ahead, b)
                    if pre and ahead >= HEADS:
                        score_min(ahead - HEADS, b + 1)
                    if att and h == 0:
                        shift_values(b)
                    if moe and h == 0:
                        normalise_values(3, m)
                    if tail:
                        if h == 1:
                            route(1, m1)
                        if h == 2:
                            route_weights(1, m1)
                        if h in (3, 4):
                            weight_hidden(h - 3, m1)
                    if moe:
                        if h == 5:
                            output_norm(b, has)
                        if h == 7:
                            route_weights(0, m)
                        if 7 <= h < 7 + X0:
                            add_expert(h - 7, m)
                    if pre:
                        if h == 1:
                            take_mask(b)
                        if h - 2 in Q_AT:
                            sum_squares(Q_AT[h - 2], b)
                        if h == 8:
                            sum_squares(4, b)
                            inverse_norms(b)
                        if h == 9:
                            normalise_k(b)
                    if moe and h == 6:
                        route(0, m)
                        gate_up(0, m)
                    if tail:
                        if h == 10:
                            last_stats(m1)
                        if h == 11:
                            last_rsqrt(m1)
                        if h == 12:
                            last_scale(m1)

            for b in (-1, 0, 1):
                turn(b, parts(b))
            with dve.Fori(2, B - 1) as b:
                turn(b, FULL)
            for b in (B - 1, B, B + 1):
                turn(b, parts(b))


def kernel(**inputs):
    import numpy as np
    import concourse.bacc as bacc
    from concourse.bass_utils import run_bass_kernel_spmd

    i = {name: np.asarray(a) for name, a in inputs.items()}
    assert i["x"].shape == (B, S, D) and i["x"].shape[0] // i["L1_ffn_Wq"].shape[0] == 0

    def by_input(w):
        return w.transpose(1, 0, 2).reshape(w.shape[1], -1)

    def by_chunk(w):
        return w.reshape(-1, P, w.shape[-1]).transpose(1, 0, 2).reshape(P, -1)

    def padded(w):
        return np.concatenate([w, np.zeros((P - w.shape[0], w.shape[1]), w.dtype)]) if w.shape[0] < P else w

    c = np.concatenate
    split = c([i["L0_cond_Wq"], i["L0_cond_Wkv"], i["L0_ffn_Wr"], i["L1_cond_wt"].T,
               by_input(i["L0_ffn_W3"]), i["L0_ffn_Ws3"], by_input(i["L0_ffn_W1"]), i["L0_ffn_Ws1"],
               by_input(i["L1_cond_w_gate"]), i["L1_cond_sw_gate"], by_input(i["L1_cond_w_up"]),
               i["L1_cond_sw_up"]], axis=1)
    down = c([by_chunk(i["L0_ffn_W2"].reshape(-1, D)), by_chunk(i["L0_ffn_Ws2"]), by_chunk(i["L0_cond_Wout"]),
              by_chunk(i["L1_cond_w_down"].reshape(-1, D)), i["L1_cond_sw_down"]], axis=1)
    cond = i["cond_64"]
    rows = c([i["L0_cond_w0"][0], i["L0_cond_b0"], i["L0_cond_g0"], i["L0_cond_b1"], i["L0_cond_g1"],
              cond[0], cond[0], cond[1], cond[1], cond.reshape(-1)])
    krows = c([i["L0_cond_null_attn_bias"], i["L0_ffn_rb"], i["L1_ffn_ln_g"], i["L1_ffn_ln_b"], cond[1]])
    pos = np.arange(S - 1, -1, -1, dtype=np.float32).reshape(2, P)
    b2 = c([i["L0_cond_b2"], np.zeros(P - HEADS, np.float32)])
    cols = np.stack([i["L0_cond_g_norm"], c([i["L0_cond_q_scale"]] * 2), c([i["L0_cond_k_scale"]] * 2),
                     i["L0_cond_g_out"], b2, pos[0], pos[1]], axis=1)
    sel = np.repeat(np.eye(E, dtype=np.float32), M1, axis=1)
    mats = c([i["L0_cond_w1"], i["L0_cond_w2"], padded(i["L1_cond_wg"].T), np.eye(P, dtype=np.float32),
              padded(sel)], axis=1)
    arrays = {"x": i["x"], "mask": i["mask_BxS_bf1"].view(np.uint8), "split": split, "down": down, "rows": rows,
              "krows": krows, "cols": cols, "mats": mats}
    arrays = {name: np.ascontiguousarray(a) for name, a in arrays.items()}
    nc = bacc.Bacc("TRN2", target_bir_lowering=False, num_devices=1)
    args = [nc.dram_tensor(f"in_{name}", a.shape, mybir.dt.from_np(a.dtype), kind="ExternalInput").ap()
            for name, a in arrays.items()]
    rel = nc.dram_tensor("bias_by_distance", (HEADS, P, REL), F32, kind="Internal").ap()
    out = nc.dram_tensor("out", (B, S, D), F32, kind="ExternalOutput").ap()
    build(nc, *args, rel, out)
    r = run_bass_kernel_spmd(nc, [{f"in_{name}": a for name, a in arrays.items()}], core_ids=[0])
    return r.results[0]["out"]
```

```python
from contextlib import ExitStack

import concourse.bass as bass
from concourse import mybir

F32 = mybir.dt.float32
F32R = mybir.dt.float32r
I32 = mybir.dt.int32
U8 = mybir.dt.uint8
ALU = mybir.AluOpType
ACT = mybir.ActivationFunctionType
AX = mybir.AxisListType.X

P = 128
B, S, D = 8, 256, 128
T = S // P
HEADS, DH = 16, 64
PAIRS = HEADS // 2
GROUPS = HEADS // 4
E = 8
HID = 256
HC = HID // P
M1 = 64
X0 = E + 1
X1 = E // 2 + 1
BIG = 1e30
LN_EPS = 1e-5
SCALE_QK = 8.0
SCALE_R0 = 1.0 / float(D) ** 0.5
RSQRT_MAGIC = float(0x5F3759DF)
HALLEY_A = 0.375 ** 0.5
HALLEY_B = -1.25 / HALLEY_A

SPLIT = [("wq", HEADS * DH), ("wkv", 2 * DH), ("wr", E), ("wt", E), ("w3", X0 * HID), ("w1", X0 * HID),
         ("mg", X1 * P), ("mu", X1 * P)]
NSPLIT = sum(n for _, n in SPLIT)
HEAD = 2 * E + HEADS * DH + 2 * DH
PIECES = 10
PIECE_SLOTS = [(0, 5), (0, 6), (0, 7), (0, 8), (0, 9), (0, 10), (0, 14), (0, 15), (1, 0), (1, 1)]
PIECE = -(-(NSPLIT - HEAD) // (2 * PIECES)) * 2
DOWN = [("w2", X0 * HC * D), ("wout", PAIRS * D), ("wd", X1 * D)]
NDOWN = sum(n for _, n in DOWN)
ROWS = [("w0", D), ("b0", D), ("g0", D), ("b1", D), ("g1", D), ("nk", P), ("nv", P), ("cond", B * DH)]
NROWS = sum(n for _, n in ROWS)
KROWS = [("null_bias", HEADS), ("rb", E), ("ln_g", D), ("ln_b", D), ("nv_row", DH)]
NKROWS = sum(n for _, n in KROWS)
COLS = ["g_norm", "q_scale", "k_scale", "g_out", "b2", "pos0", "pos1"]
MATS = [("w1m", D), ("w2m", HEADS), ("wg", E), ("ident", P)]
NMATS = sum(n for _, n in MATS)

KT = S + 2
SB1, SB0 = 0, KT
SW = KT + P + 2
REL = S + P

M_ALL = [("QP2", "att"), ("QP3", "att"), ("XT", "pre"), ("Q0", "pre"), ("OT3", "moe"), ("Q1", "pre"), ("WO", "moe"),
         ("Q2", "pre"), ("QP4", "att"), ("QP5", "att"), ("Q3", "pre"), ("KV", "pre"), ("OT0", "att"), ("QP6", "att"),
         ("QP7", "att"), ("OT1", "att"), ("QP0", "pre"), ("KT", "pre"), ("QP1", "pre"), ("OT2", "att")]
Q_AT = {1: 0, 2: 1, 3: 2, 5: 3}
PAIRS_AT = {0: 3, 4: 4, 5: 5, 8: 6, 9: 7}
FIRST_PAIRS_AT = {11: 0, 13: 1}
LEAD = 3
D_ALL = ["YT", "LOG0"] + [f"D{e}" for e in range(X0)] + ["X1T", "LOG1", "WT", "WB0", "WB1", "DOWN"]
ND = len(D_ALL)
NGU = X0 + 3
NSUM = T * HEADS + T + 1
QROUNDS = 5

RSQRT_STEPS = 8
PRE_STEPS = 1 + RSQRT_STEPS
NORM_STEPS = 3 + RSQRT_STEPS
ROUTE_STEPS = 8


def offsets(parts):
    at, out = 0, {}
    for name, n in parts:
        out[name] = (at, n)
        at += n
    return out


def parts(b):
    return {"att": 0 <= b < B, "pre": b < B - 1, "moe": 1 <= b <= B, "tail": b >= 2}


FULL = {"att": True, "pre": True, "moe": True, "tail": True}


def piece_at(b, h):
    return PIECE_SLOTS.index((b, h)) if isinstance(b, int) and (b, h) in PIECE_SLOTS else None


def m_order(has):
    return [name for name, part in M_ALL if has[part]]


def m_first(b):
    if isinstance(b, int):
        return sum(len(m_order(parts(i))) for i in range(-1, b))
    return b * len(M_ALL) + sum(len(m_order(parts(i))) for i in (-1, 0)) - len(M_ALL)


def m_use(name, b, has):
    return m_first(b) + m_order(has).index(name)


def d_use(name, m):
    return m * ND + D_ALL.index(name)


def each_reversed(ap):
    return bass.AP(ap.tensor, ap.offset + P - 1, [list(ap.ap[0]), [P, 4], [-1, P]])


def wait(eng, sem, value):
    if isinstance(value, int) and value <= 0:
        return
    eng.wait_ge(sem, value)


class Steps:

    def __init__(self, eng, sem, per):
        self.eng, self.sem, self.per = eng, sem, per

    def start(self, b):
        self.b, self.k = b, 0

    def link(self, ins):
        self.k += 1
        ins.then_inc(self.sem, 1)
        self.eng.wait_ge(self.sem, self.b * self.per + self.k)

    def end(self):
        assert self.k == self.per, (self.k, self.per)


def build(nc, x_in, mask_in, split_in, down_in, rows_in, krows_in, cols_in, mats_in, sel_dram, rel_dram, out):
    with ExitStack() as ctx:
        def sb(name, shape, dt=F32):
            return ctx.enter_context(nc.sbuf_tensor(name, shape, dt))

        def sem(name):
            return ctx.enter_context(nc.semaphore(name))

        def bank(name):
            return ctx.enter_context(nc.psum_tensor(name, [P, 512], F32))
        bank_s = [bank("bank_s0"), bank("bank_s1")]
        bank_pt = bank("bank_pt")
        bank_pv = bank("bank_pv")
        bank_m = bank("bank_m")
        bank_g, bank_u, bank_d = bank("bank_g"), bank("bank_u"), bank("bank_d")

        w_hi, w_lo = sb("w_hi", [P, NSPLIT], F32R), sb("w_lo", [P, NSPLIT], F32R)
        down = sb("down", [P, NDOWN])
        krows, cols, mats = sb("krows", [P, NKROWS]), sb("cols", [P, len(COLS)]), sb("mats", [P, NMATS])
        x_sb = sb("x_sb", [P, B * T, D])
        bias_all = sb("bias_all", [P, HEADS, S + 1])
        bias_b = sb("bias_b", [P, HEADS, SW])
        mask_u8 = sb("mask_u8", [P, B, S], U8)
        mask_row, idle = sb("mask_row", [P, SW]), sb("idle", [P, HEADS + 2])
        x_stat, x_mv = sb("x_stat", [P, B * T, 6]), sb("x_mv", [P, B * T, 2])
        x_var, x_rstd, x_tmp = sb("x_var", [P, B * T]), sb("x_rstd", [P, B * T]), sb("x_tmp", [P, B * T])
        kscale = sb("kscale", [P, 1])
        cond_logit = sb("cond_logit", [P, B * E])
        null_out = sb("null_out", [P, D])
        xn = sb("xn", [P, T, D])
        xnT_hi, xnT_lo = sb("xnT_hi", [P, S], F32R), sb("xnT_lo", [P, S], F32R)
        q_raw = sb("q_raw", [P, T, HEADS * DH])
        kv_raw = sb("kv_raw", [P, T, 2 * DH])
        sq = sb("sq", [P, 2, 512])
        ss, rn, rn_tmp = sb("ss", [P, NSUM]), sb("rn", [P, NSUM]), sb("rn_tmp", [P, NSUM])
        qn = sb("qn", [P, T, HEADS, 2 * DH])
        kn = sb("kn", [P, T, P])
        val = sb("val", [P, T, DH])
        kT_hi, kT_lo = sb("kT_hi", [P, SW], F32R), sb("kT_lo", [P, SW], F32R)
        qT = sb("qT", [P, 2, 2, S], F32R)
        prob = sb("prob", [P, 4, SW])
        s_min, s_sum = sb("s_min", [P, 4, T]), sb("s_sum", [P, T, HEADS])
        probT = sb("probT", [P, 2, 3 * P])
        r_sum = sb("r_sum", [P, T, 4])
        on = sb("on", [P, 2, T, 4 * DH])
        oT = sb("oT", [P, PAIRS, S])
        yn = sb("yn", [P, T, D])
        y_stat, y_mv, y_var = sb("y_stat", [P, T, 6]), sb("y_mv", [P, T, 2]), sb("y_var", [P, T])
        y_rstd, y_tmp = sb("y_rstd", [P, T]), sb("y_tmp", [P, T])
        yT_hi, yT_lo = sb("yT_hi", [P, S], F32R), sb("yT_lo", [P, S], F32R)
        act_g = sb("act_g", [P, 512])
        hid = sb("hid", [P, X1 * S])
        acc = sb("acc", [P, T, D])
        lg, chosen, top8, ldiff, w_tok = (sb(n, [P, T, E]) for n in ("lg", "chosen", "top8", "ldiff", "w_tok"))
        cand, cand_left = sb("cand", [P, T, 2 * E]), sb("cand_left", [P, T, 2 * E])
        lsum = sb("lsum", [P, T])
        sel = sb("sel", [E, E // 2 * P], F32R)
        wT_hi = sb("wT_hi", [E, S], F32R)
        wT_lo = sb("wT_lo", [E, S], F32R)
        o_stat, o_mv, o_var = sb("o_stat", [P, T, 6]), sb("o_mv", [P, T, 2]), sb("o_var", [P, T])
        o_rstd, o_tmp = sb("o_rstd", [P, T]), sb("o_tmp", [P, T])
        norm, resid = sb("norm", [P, T, D]), sb("resid", [P, T, D])

        rows = oT[:].rearrange("p a s -> p (a s)")[:, 0:NROWS]
        stage_head = bias_b[:].rearrange("p h w -> p (h w)")[:, 0:HEAD]
        cond_rep = on[0:DH].rearrange("p a t d -> p (a t d)").rearrange("p (b n) -> p b n", b=B)
        stage = [hid[:, 0:PIECE], hid[:, PIECE:2 * PIECE]]
        hb, hs = (act_g[:, i * 2 * D:(i + 1) * 2 * D].rearrange("p (t d) -> p t d", t=2) for i in range(2))
        hT = acc[:].rearrange("p t d -> p (t d)")
        rel = prob[0:HEADS, 3, 0:REL]
        nv_rep, nk_sq, nk_scale = yn[:, 0, :], acc[:, 0, :], acc[:, 1, 0:1]

        so, do, ro, ko, mo = offsets(SPLIT), offsets(DOWN), offsets(ROWS), offsets(KROWS), offsets(MATS)

        def piece(c):
            return HEAD + c * PIECE, min(HEAD + (c + 1) * PIECE, NSPLIT)

        def hi(name, a=0, n=None):
            at, size = so[name]
            return w_hi[:, at + a:at + a + (size if n is None else n)]

        def lo(name, a=0, n=None):
            at, size = so[name]
            return w_lo[:, at + a:at + a + (size if n is None else n)]

        def dn(name, i):
            return down[:, do[name][0] + i * D:do[name][0] + (i + 1) * D]

        def row(name):
            return rows[:, ro[name][0]:ro[name][0] + ro[name][1]]

        def krow(name):
            return krows[:, ko[name][0]:ko[name][0] + ko[name][1]]

        def mat(name):
            return mats[:, mo[name][0]:mo[name][0] + mo[name][1]]

        def col(name, n=P):
            return cols[0:n, COLS.index(name):COLS.index(name) + 1]

        ident = mat("ident")
        sel_in = probT[0:E].rearrange("p a s -> p (a s)")[:, 0:E // 2 * P]

        def mask_bias(engine, h):
            engine.tensor_tensor(bias_b[:, h, SB1:SB1 + S + 1], bias_all[:, h, :], mask_row[:, SB1:SB1 + S + 1], ALU.add)
            return engine.tensor_tensor(bias_b[:, h, SB0:SB0 + P + 1], bias_all[:, h, P:S + 1],
                                        mask_row[:, SB0:SB0 + P + 1], ALU.add)

        ld_small, ld_mats, ld_krows, ld_x0, ld_x = (sem(n) for n in ("ld_small", "ld_mats", "ld_krows", "ld_x0", "ld_x"))
        ld_mask, ld_down, ld_head = sem("ld_mask"), sem("ld_down"), sem("ld_head")
        ld_sel, ld_null = sem("ld_sel"), sem("ld_null")
        ld_piece = [sem(f"ld_piece{c}") for c in range(PIECES)]
        rel_stored, out_stored = sem("rel_stored"), sem("out_stored")
        bias_loaded = [sem(f"bias_loaded{g}") for g in range(GROUPS)]
        hi_split, lo_split = sem("hi_split"), sem("lo_split")
        head_hi, head_lo, sel_ready = sem("head_hi"), sem("head_lo"), sem("sel_ready")
        net_pe, net_act, net_dve, rel_ready = sem("net_pe"), sem("net_act"), sem("net_dve"), sem("rel_ready")
        set_pe, set_dve = sem("set_pe"), sem("set_dve")
        steps_pre, steps_norm, steps_route, steps_last = (sem(n) for n in ("steps_pre", "steps_norm", "steps_route", "steps_last"))
        sum_ready = sem("sum_ready")
        m_full, m_free, m_hi = sem("m_full"), sem("m_free"), sem("m_hi")
        d_full, d_free, d_hi = sem("d_full"), sem("d_free"), sem("d_hi")
        xn_ready, sq_ready, ss_ready = sem("xn_ready"), sem("sq_ready"), sem("ss_ready")
        qm_ready, qh_ready, qn_ready = sem("qm_ready"), sem("qh_ready"), sem("qn_ready")
        kn_ready, val_ready, k_hi = sem("kn_ready"), sem("val_ready"), sem("k_hi")
        batch_bias, mask_ready, half_bias = sem("batch_bias"), sem("mask_ready"), sem("half_bias")
        s_full, s_read, p_ready = sem("s_full"), sem("s_read"), sem("p_ready")
        pt_full, pt_copied, pv_done, on_ready = sem("pt_full"), sem("pt_copied"), sem("pv_done"), sem("on_ready")
        yn_ready = sem("yn_ready")
        g_full, act_ready, g_read = sem("g_full"), sem("act_ready"), sem("g_read")
        u_full, u_read = sem("u_full"), sem("u_read")
        w_hi_ready = sem("w_hi_ready")
        diff_ready, tanh_ready, w_ready = sem("diff_ready"), sem("tanh_ready"), sem("w_ready")
        resid_ready, norm_ready = sem("resid_ready"), sem("norm_ready")
        gain_ready, out_ready = sem("gain_ready"), sem("out_ready")

        block = ctx.enter_context(nc.Block())

        HT0, HW1, HT1, HW2 = range(1, 5)
        TANH0_IN, HS0, HT0_COPIED, TANH1_IN, HS1, HT1_COPIED = range(1, 7)
        NK_T, NV_T, COND_T0, COND_T1, COND, NULL_OUT = range(1, 7)
        KT_ZEROED, NK_COLUMNS, NV_COPIED, COND_COPIED0, COND_COPIED1, LOGIT, SET = range(1, 8)

        @block.sync
        def _(sp):
            sp.dma_start(cols[:], cols_in).then_inc(ld_small, 16)
            net = ro["nk"][0]
            sp.dma_start(rows[:, 0:net], rows_in[0:net].partition_broadcast(P)).then_inc(ld_small, 16)
            x_v = x_in.rearrange("b (t p) d -> p (b t) d", p=P)
            sp.dma_start(x_sb[:, 0:T, :], x_v[:, 0:T, :]).then_inc(ld_x0, 16)
            sp.dma_start(mats[:], mats_in).then_inc(ld_mats, 16)
            sp.dma_start(stage_head, split_in[:, 0:HEAD]).then_inc(ld_head, 16)
            sp.dma_start(rows[:, net:NROWS], rows_in[net:NROWS].partition_broadcast(P)).then_inc(ld_null, 16)
            sp.dma_start(sel_in, sel_dram).then_inc(ld_sel, 16)
            sp.dma_start(mask_u8[:], mask_in.partition_broadcast(P)).then_inc(ld_mask, 16)
            sp.dma_start(krows[:], krows_in.partition_broadcast(P)).then_inc(ld_krows, 16)
            sp.dma_start(x_sb[:, T:B * T, :], x_v[:, T:B * T, :]).then_inc(ld_x, 16)
            sp.wait_ge(rel_ready, 1)
            sp.dma_start(rel_dram, rel).then_inc(rel_stored, 16)
            sp.wait_ge(rel_stored, 16)
            for g in range(GROUPS):
                band = bass.AP(rel_dram.tensor, 4 * g * REL, [[1, P], [REL, 4], [1, S]])
                sp.dma_start(bias_all[:, 4 * g:4 * g + 4, 0:S], band).then_inc(bias_loaded[g], 16)
            sp.dma_start(down[:], down_in).then_inc(ld_down, 16)
            for c in range(PIECES):
                if c >= 2:
                    sp.wait_ge(lo_split, c - 1)
                a, b = piece(c)
                sp.dma_start(stage[c % 2][:, 0:b - a], split_in[:, a:b]).then_inc(ld_piece[c], 16)
            out_v = out.rearrange("b (t p) d -> b p t d", p=P)

            def store(m):
                sp.wait_ge(out_ready, m + 1)
                sp.dma_start(out_v[m], norm[:]).then_inc(out_stored, 16)
            for m in range(B):
                store(m)
            sp.wait_ge(out_stored, 16 * B)

        @block.tensor
        def _(pe):
            def split3(dst, a_hi, a_lo, b_hi, b_lo):
                nc.tensor.matmul(dst, a_hi, b_hi, start=True, stop=False)
                nc.tensor.matmul(dst, a_lo, b_hi, start=False, stop=False)
                return nc.tensor.matmul(dst, a_hi, b_lo, start=False, stop=True)

            def take_m(name, b, has):
                wait(pe, m_free, m_use(name, b, has))

            def q_transposes(p, bq, b, has):
                take_m(f"QP{p}", b, has)
                pe.wait_ge(qn_ready, bq * GROUPS + p // 2 + 1)
                for j in range(2):
                    for t in range(T):
                        mm = nc.tensor.transpose(bank_m[:, (j * T + t) * P:(j * T + t + 1) * P], qn[:, t, 2 * p + j, :],
                                                 ident)
                mm.then_inc(m_full, 1)

            def scores(h, bq, use=None):
                if use is not None:
                    pe.wait_ge(m_free, use + 1)
                wait(pe, s_read, bq * HEADS + h - 1)
                q = qT[:, h // 2 % 2, h % 2, :]
                for t, (at, w) in enumerate(((SB0, P + 2), (SB1, S + 2))):
                    dst = bank_s[h % 2][:, at:at + w]
                    nc.tensor.matmul(dst, q[:, t * P:(t + 1) * P], kT_hi[:, at:at + w], start=True, stop=False)
                    mm = nc.tensor.matmul(dst, q[:, t * P:(t + 1) * P], kT_lo[:, at:at + w], start=False, stop=True)
                mm.then_inc(s_full, 1)

            def p_transposes(h, b):
                n = b * HEADS + h
                pe.wait_ge(p_ready, n + 1)
                wait(pe, pt_copied, n)
                p = prob[:, h % 4, :]
                nc.tensor.transpose(bank_pt[:, 0:P], p[:, SB0:SB0 + P], ident)
                nc.tensor.transpose(bank_pt[:, P:2 * P], p[:, SB1:SB1 + P], ident)
                nc.tensor.transpose(bank_pt[:, 2 * P:3 * P], p[:, SB1 + P:SB1 + 2 * P], ident).then_inc(pt_full, 1)

            def values(h, b):
                n = b * HEADS + h
                pe.wait_ge(pt_copied, n + 1)
                if h == 0:
                    pe.wait_ge(val_ready, b + 1)
                if h % 4 == 0:
                    wait(pe, on_ready, b * GROUPS + h // 4)
                pt, o = probT[:, h % 2, :], (h % 4) * DH
                out0 = bank_pv[:, o:o + DH]
                out1 = bank_pv[:, 4 * DH + o:4 * DH + o + DH]
                nc.tensor.matmul(out0, pt[:, 0:P], val[:, 0, :], start=True, stop=True)
                nc.tensor.matmul(out1, pt[:, P:2 * P], val[:, 0, :], start=True, stop=False)
                nc.tensor.matmul(out1, pt[:, 2 * P:3 * P], val[:, 1, :], start=False, stop=True).then_inc(pv_done, 1)

            def o_transposes(g, bo, b, has):
                take_m(f"OT{g}", b, has)
                pe.wait_ge(on_ready, bo * GROUPS + g + 1)
                for j in range(2):
                    for t in range(T):
                        mm = nc.tensor.transpose(bank_m[:, (j * T + t) * P:(j * T + t + 1) * P],
                                                 on[:, g % 2, t, j * P:(j + 1) * P], ident)
                mm.then_inc(m_full, 1)

            def out_projection(b, has):
                take_m("WO", b, has)
                for t in range(T):
                    for j in range(PAIRS):
                        mm = nc.tensor.matmul(bank_m[:, t * D:(t + 1) * D], oT[:, j, t * P:(t + 1) * P], dn("wout", j),
                                              start=(j == 0), stop=(j == PAIRS - 1))
                mm.then_inc(m_full, 1)

            def x_transposes(b, has):
                take_m("XT", b, has)
                pe.wait_ge(xn_ready, b + 2)
                for t in range(T):
                    mm = nc.tensor.transpose(bank_m[:, t * P:(t + 1) * P], xn[:, t, :], ident)
                mm.then_inc(m_full, 1)

            def q_round(r, b, has):
                take_m(f"Q{r}", b, has)
                t, c = r // 2, r % 2 * 512
                split3(bank_m[:], xnT_hi[:, t * P:(t + 1) * P], xnT_lo[:, t * P:(t + 1) * P],
                       hi("wq", c, 512), lo("wq", c, 512)).then_inc(m_full, 1)

            def kv_round(b, has):
                take_m("KV", b, has)
                for t in range(T):
                    mm = split3(bank_m[:, t * P:(t + 1) * P], xnT_hi[:, t * P:(t + 1) * P],
                                xnT_lo[:, t * P:(t + 1) * P], hi("wkv"), lo("wkv"))
                mm.then_inc(m_full, 1)

            def k_transposes(b, has):
                take_m("KT", b, has)
                pe.wait_ge(kn_ready, b + 2)
                for t in range(T):
                    mm = nc.tensor.transpose(bank_m[:, t * P:(t + 1) * P], kn[:, t, :], ident)
                mm.then_inc(m_full, 1)

            def take_d(name, m):
                wait(pe, d_free, d_use(name, m))

            def tok_transposes(name, src, ready, m):
                take_d(name, m)
                if ready is not None:
                    pe.wait_ge(ready, m + 1)
                for t in range(T):
                    mm = nc.tensor.transpose(bank_d[:, t * P:(t + 1) * P], src[:, t, :], ident)
                mm.then_inc(d_full, 1)

            def logits(name, weight, m):
                take_d(name, m)
                for t in range(T):
                    mm = split3(bank_d[:, t * E:(t + 1) * E], yT_hi[:, t * P:(t + 1) * P],
                                yT_lo[:, t * P:(t + 1) * P], hi(weight), lo(weight))
                mm.then_inc(d_full, 1)

            def gate_up(k, m):
                if k < X0:
                    parts = [(("w3", "w1"), (k * HC + c) * P) for c in range(HC)]
                else:
                    pairs = {X0: [X1 - 1], X0 + 1: [0, 1], X0 + 2: [2, 3]}[k]
                    parts = [(("mg", "mu"), j * P) for j in pairs]
                for side, (dst, read, full) in enumerate(((bank_g, g_read, g_full), (bank_u, u_read, u_full))):
                    wait(pe, read, m * NGU + k)
                    for c, (names, at) in enumerate(parts):
                        mm = split3(dst[:, c * S:(c + 1) * S], hi(names[side], at, P), lo(names[side], at, P),
                                    yT_hi[:], yT_lo[:])
                    mm.then_inc(full, 1)

            def expert_down(e, m):
                take_d(f"D{e}", m)
                pe.wait_ge(u_read, m * NGU + e + 1)
                for t in range(T):
                    for c in range(HC):
                        h0 = (e % 2) * 512 + c * S + t * P
                        mm = nc.tensor.matmul(bank_d[:, t * D:(t + 1) * D], hid[:, h0:h0 + P], dn("w2", e * HC + c),
                                              start=(c == 0), stop=(c == HC - 1))
                mm.then_inc(d_full, 1)

            def weight_transposes(m):
                take_d("WT", m)
                pe.wait_ge(w_ready, 2 * m + 2)
                for t in range(T):
                    mm = nc.tensor.transpose(bank_d[0:E, t * P:(t + 1) * P], w_tok[:, t, :], ident)
                mm.then_inc(d_full, 1)

            def weight_rows(r, m):
                take_d(f"WB{r}", m)
                for j in range(2):
                    dst, pair = bank_d[:, j * S:(j + 1) * S], sel[:, (2 * r + j) * P:(2 * r + j + 1) * P]
                    nc.tensor.matmul(dst, pair, wT_hi[:], start=True, stop=False)
                    mm = nc.tensor.matmul(dst, pair, wT_lo[:], start=False, stop=True)
                mm.then_inc(d_full, 1)

            def layer1_down(m):
                take_d("DOWN", m)
                for t in range(T):
                    for j in range(X1):
                        mm = nc.tensor.matmul(bank_d[:, t * D:(t + 1) * D], hid[:, j * S + t * P:j * S + (t + 1) * P],
                                              dn("wd", j), start=(j == 0), stop=(j == X1 - 1))
                mm.then_inc(d_full, 1)

            def turn(b, has):
                att, pre, moe, tail = (has[n] for n in ("att", "pre", "moe", "tail"))
                m, m1 = b - 1, b - 2
                for h in range(HEADS):
                    if att and h == 0:
                        q_transposes(2, b, b, has)
                    ahead = h + LEAD
                    if att and ahead < HEADS:
                        scores(ahead, b, m_use(f"QP{ahead // 2}", b, has) if ahead % 2 == 0 else None)
                    if pre and ahead >= HEADS:
                        n = ahead - HEADS
                        scores(n, b + 1, m_use(("KT", "QP1")[n // 2], b, has) if n % 2 == 0 else None)
                    if moe and h == 2:
                        o_transposes(3, m, b, has)
                    if moe and h == 3:
                        out_projection(b, has)
                    if pre and h == 12:
                        k_transposes(b, has)
                    if isinstance(b, int) and b == 1 and h == 6:
                        pe.wait_ge(lo_split, PIECES)
                    if tail:
                        if h == 0:
                            tok_transposes("X1T", acc, None, m1)
                        if h == 1:
                            logits("LOG1", "wt", m1)
                        if h == 3:
                            weight_transposes(m1)
                    if pre and h == 1:
                        x_transposes(b, has)
                    if tail:
                        if h in (1, 2, 3):
                            gate_up(X0 + h - 1, m1)
                    if moe and h == 0:
                        values(HEADS - 1, m)
                    if moe and 6 < h < 6 + X0:
                        gate_up(h - 6, m)
                    if att:
                        p_transposes(h, b)
                    if moe and h == 6:
                        tok_transposes("YT", yn, yn_ready, m)
                    if att and h in PAIRS_AT:
                        q_transposes(PAIRS_AT[h], b, b, has)
                    if pre and h in FIRST_PAIRS_AT:
                        q_transposes(FIRST_PAIRS_AT[h], b + 1, b, has)
                    if tail:
                        if h in (3, 4):
                            weight_rows(h - 3, m1)
                        if h == 5:
                            layer1_down(m1)
                    if moe and 7 <= h < 7 + X0:
                        expert_down(h - 7, m)
                    if att and h == 1:
                        values(h - 1, b)
                    if pre and h in Q_AT:
                        q_round(Q_AT[h], b, has)
                    if pre and h == 6:
                        kv_round(b, has)
                    if att and h == 6:
                        values(h - 1, b)
                    if moe and h == 6:
                        logits("LOG0", "wr", m)
                        gate_up(0, m)
                    if att and h >= 1 and h not in (1, 6):
                        values(h - 1, b)
                    if att and h in (6, 10, 14):
                        o_transposes((h - 6) // 4, b, b, has)

            def hidden_transposes(layer):
                pe.wait_ge(net_dve, (HS0, HS1)[layer])
                for t in range(2):
                    mm = nc.tensor.transpose(bank_pt[:, t * P:(t + 1) * P], hs[:, t, :], ident)
                mm.then_inc(net_pe, 1)

            first = parts(-1)
            pe.wait_ge(ld_mats, 16)
            hidden_transposes(0)
            x_transposes(-1, first)
            pe.wait_ge(net_dve, HT0_COPIED)
            for t in range(2):
                mm = nc.tensor.matmul(bank_pv[:, t * D:(t + 1) * D], hT[:, t * P:(t + 1) * P], mat("w1m"),
                                      start=True, stop=True)
            mm.then_inc(net_pe, 1)
            pe.wait_ge(head_lo, 1)
            for r in range(4):
                q_round(r, -1, first)
            hidden_transposes(1)
            kv_round(-1, first)
            pe.wait_ge(net_dve, HT1_COPIED)
            nc.tensor.matmul(bank_pv[0:HEADS, 0:S], mat("w2m"), hT, start=True, stop=True).then_inc(net_pe, 1)
            pe.wait_ge(ld_null, 16)
            nc.tensor.transpose(bank_s[1][:, 0:P], row("nk"), ident).then_inc(set_pe, 1)
            nc.tensor.transpose(bank_d[:, 0:P], row("nv"), ident).then_inc(set_pe, 1)
            for half, dst in enumerate((bank_u, bank_g)):
                for i in range(4):
                    b0 = (4 * half + i) * DH
                    mm = nc.tensor.transpose(dst[0:DH, i * P:(i + 1) * P], row("cond")[:, b0:b0 + DH], ident)
                mm.then_inc(set_pe, 1)
            q_transposes(0, 0, -1, first)
            k_transposes(-1, first)
            scores(0, 0, m_use("KT", -1, first))
            scores(1, 0)
            q_transposes(1, 0, -1, first)
            scores(2, 0, m_use("QP1", -1, first))
            pe.wait_ge(set_dve, COND_COPIED1)
            for b in range(B):
                mm = nc.tensor.matmul(bank_d[:, b * E:(b + 1) * E], cond_rep[:, b, :], mat("wg")[0:DH, :],
                                      start=True, stop=True)
            mm.then_inc(set_pe, 1)
            pe.wait_ge(ld_down, 16)
            for j in range(PAIRS):
                mm = nc.tensor.matmul(bank_u[:, 0:D], nv_rep, dn("wout", j), start=(j == 0), stop=(j == PAIRS - 1))
            mm.then_inc(set_pe, 1)

            for b in (0, 1):
                if b == 1:
                    pe.wait_ge(set_dve, SET)
                    pe.wait_ge(sel_ready, 1)
                turn(b, parts(b))
            with pe.Fori(2, B - 1) as b:
                turn(b, FULL)
            for b in (B - 1, B, B + 1):
                turn(b, parts(b))

        @block.scalar
        def _(act):
            def split_hi(c):
                act.wait_ge(ld_piece[c], 16)
                a, b = piece(c)
                nc.scalar.activation(w_hi[:, a:b], stage[c % 2][:, 0:b - a], ACT.Copy).then_inc(hi_split, 1)

            def net_tanh(layer):
                act.wait_ge(net_dve, (TANH0_IN, TANH1_IN)[layer])
                nc.scalar.activation(hs, hb, ACT.Tanh, scale=0.5).then_inc(net_act, 1)

            def copy_m(name, b, has, dst, scale=None):
                u = m_use(name, b, has)
                wait(act, m_full, u + 1)
                src = each_reversed(bank_m[:]) if name[0:2] in ("QP", "OT") else bank_m[:, 0:dst.free_size()]
                if scale is None:
                    i = nc.scalar.activation(dst, src, ACT.Copy)
                else:
                    i = nc.scalar.activation(dst, src, ACT.Copy, scale=scale)
                return i

            def copy_q(p, bq, b, has):
                wait(act, s_full, bq * HEADS + 2 * p - 2)
                copy_m(f"QP{p}", b, has, qT[:, p % 2, :, :].rearrange("p j (t s) -> p (j t) s", t=T)).then_inc(m_free, 1)

            def q_high(g, b):
                act.wait_ge(qm_ready, (b + 1) * GROUPS + g + 1)
                nc.scalar.activation(qn[:, :, 4 * g:4 * g + 4, 0:DH].bitcast(F32R),
                                     q_raw[:, :, 4 * g * DH:4 * (g + 1) * DH].rearrange("p t (h d) -> p t h d", d=DH),
                                     ACT.Copy).then_inc(qh_ready, 1)

            def copy_o(g, b, has):
                copy_m(f"OT{g}", b, has,
                       oT[:, 2 * g:2 * g + 2, :].rearrange("p j (t s) -> p (j t) s", t=T)).then_inc(m_free, 1)

            def copy_x(b, has):
                copy_m("XT", b, has, xnT_hi[:], col("g_norm")).then_inc(m_hi, 1)

            def copy_q_round(r, b, has):
                if r == 0:
                    wait(act, qn_ready, (b + 1) * GROUPS)
                copy_m(f"Q{r}", b, has, q_raw[:, r // 2, r % 2 * 512:(r % 2 + 1) * 512]).then_inc(m_free, 1)

            def copy_kv(b, has):
                wait(act, val_ready, b + 1)
                copy_m("KV", b, has, kv_raw[:].rearrange("p t n -> p (t n)")).then_inc(m_free, 1)

            def copy_k(b, has):
                wait(act, s_full, (b + 1) * HEADS)
                copy_m("KT", b, has, kT_hi[:, SB1:SB1 + S], kscale[:, 0:1])
                nc.scalar.activation(kT_hi[:, SB0:SB0 + P], bank_m[:, 0:P], ACT.Copy,
                                     scale=kscale[:, 0:1]).then_inc(k_hi, 1)

            def exps(h, b):
                n = b * HEADS + h
                act.wait_ge(s_read, n + 1)
                p = prob[:, h % 4, :]
                for t, (at, w) in enumerate(((SB0, P + 1), (SB1, S + 1))):
                    i = nc.scalar.activation(p[:, at:at + w], p[:, at:at + w], ACT.Exp, scale=-1.0,
                                             bias=s_min[:, h % 4, t:t + 1], accum_out=s_sum[:, t, h:h + 1])
                i.then_inc(p_ready, 1)

            def copy_pt(h, b):
                n = b * HEADS + h
                act.wait_ge(pt_full, n + 1)
                wait(act, pv_done, n - 1)
                nc.scalar.activation(probT[:, h % 2, :], bank_pt[:, 0:3 * P], ACT.Copy).then_inc(pt_copied, 1)

            def gate_act(k, m):
                n = m * NGU + k
                act.wait_ge(g_full, n + 1)
                wait(act, g_read, n)
                w = S if k == X0 else 512
                if k < X0:
                    i = nc.scalar.activation(act_g[:, 0:w], bank_g[:, 0:w], ACT.Tanh, scale=0.5)
                else:
                    i = nc.scalar.activation(act_g[:, 0:w], bank_g[:, 0:w], ACT.Relu, scale=0.99)
                i.then_inc(act_ready, 1)

            def copy_hi(name, scale, m):
                act.wait_ge(d_full, d_use(name, m) + 1)
                nc.scalar.activation(yT_hi[:], bank_d[:, 0:S], ACT.Copy, scale=scale).then_inc(d_hi, 1)

            def route_tanh(i, m):
                act.wait_ge(diff_ready, 2 * m + i + 1)
                nc.scalar.activation(ldiff[:], ldiff[:], ACT.Tanh, scale=1.0 if i == 0 else 0.5).then_inc(tanh_ready, 1)

            def turn(b, has):
                att, pre, moe, tail = (has[n] for n in ("att", "pre", "moe", "tail"))
                m, m1 = b - 1, b - 2
                for h in range(HEADS):
                    if att and h == 0:
                        copy_q(2, b, b, has)
                    if moe and h == 2:
                        copy_o(3, b, has)
                    if pre and h == 1:
                        copy_x(b, has)
                    if pre and h == 12:
                        copy_k(b, has)
                    if moe and h == 6:
                        copy_hi("YT", col("g_out"), m)
                    if moe and h == 7:
                        route_tanh(0, m)
                    if tail:
                        if h == 0:
                            copy_hi("X1T", 1.0, m1)
                        if h == 2:
                            route_tanh(1, m1)
                        if h == 3:
                            act.wait_ge(d_full, d_use("WT", m1) + 1)
                            nc.scalar.activation(wT_hi[:], bank_d[0:E, 0:S], ACT.Copy).then_inc(w_hi_ready, 1)
                        if h in (1, 2, 3):
                            gate_act(X0 + h - 1, m1)
                    if moe and 6 < h < 6 + X0:
                        gate_act(h - 6, m)
                    if att:
                        copy_pt(h, b)
                    if pre and 10 <= h < 10 + GROUPS:
                        q_high(h - 10, b)
                    if att and h in PAIRS_AT:
                        copy_q(PAIRS_AT[h], b, b, has)
                    if pre and h in FIRST_PAIRS_AT:
                        copy_q(FIRST_PAIRS_AT[h], b + 1, b, has)
                    if tail and h == 5:
                        act.wait_ge(d_full, d_use("DOWN", m1) + 1)
                        wait(act, out_stored, 16 * m1)
                        nc.scalar.activation(norm[:].rearrange("p t d -> p (t d)"), bank_d[:, 0:T * D],
                                             ACT.Copy).then_inc(d_free, 1)
                    if pre and h in Q_AT:
                        copy_q_round(Q_AT[h], b, has)
                    if pre and h == 6:
                        copy_kv(b, has)
                    if moe and h == 6:
                        gate_act(0, m)
                    if att and h in (6, 10, 14):
                        copy_o((h - 6) // 4, b, has)
                    ahead = h + LEAD
                    if att and ahead < HEADS:
                        exps(ahead, b)
                    if pre and ahead >= HEADS:
                        exps(ahead - HEADS, b + 1)
                    if piece_at(b, h) is not None:
                        split_hi(piece_at(b, h))

            first = parts(-1)
            net_tanh(0)
            act.wait_ge(ld_sel, 16)
            act.wait_ge(ld_head, 16)
            nc.scalar.activation(w_hi[:, 0:HEAD], stage_head, ACT.Copy).then_inc(head_hi, 1)
            nc.scalar.activation(sel[:], sel_in, ACT.Copy).then_inc(sel_ready, 1)
            copy_x(-1, first)
            copy_q_round(0, -1, first)
            net_tanh(1)
            for r in range(1, 4):
                copy_q_round(r, -1, first)
            copy_kv(-1, first)
            act.wait_ge(set_dve, KT_ZEROED)
            q_high(0, -1)
            copy_q(0, 0, -1, first)
            copy_k(-1, first)
            copy_q(1, 0, -1, first)
            q_high(1, -1)
            exps(0, 0)
            exps(1, 0)
            q_high(2, -1)
            exps(2, 0)
            q_high(3, -1)

            for b in (0, 1):
                turn(b, parts(b))
            with act.Fori(2, B - 1) as b:
                turn(b, FULL)
            for b in (B - 1, B, B + 1):
                turn(b, parts(b))

        @block.gpsimd
        def _(pool):
            def split_lo(c):
                pool.wait_ge(hi_split, c + 1)
                a, b = piece(c)
                nc.gpsimd.tensor_tensor(w_lo[:, a:b], stage[c % 2][:, 0:b - a], w_hi[:, a:b].bitcast(F32),
                                        ALU.subtract).then_inc(lo_split, 1)

            def batch_mask(h, b, done=1):
                wait(pool, s_read, b * HEADS + h + 1)
                if h == 0:
                    pool.wait_ge(mask_ready, b + 2)
                mask_bias(nc.gpsimd, h).then_inc(batch_bias, done)

            def square(k, b, has):
                name = f"Q{k}" if k < 4 else "KV"
                pool.wait_ge(m_free, m_use(name, b, has) + 1)
                wait(pool, ss_ready, (b + 1) * QROUNDS + k - 1)
                if k < 4:
                    src = q_raw[:, k // 2, k % 2 * 512:(k % 2 + 1) * 512]
                    dst = sq[:, k % 2, :]
                else:
                    src = kv_raw[:, :, 0:DH]
                    dst = sq[:, k % 2, 0:T * DH].rearrange("p (t d) -> p t d", t=T)
                nc.gpsimd.tensor_tensor(dst, src, src, ALU.mult).then_inc(sq_ready, 1)

            def normalise_q(g, b, has):
                if g == 0:
                    pool.wait_ge(steps_pre, (b + 2) * PRE_STEPS)
                q = q_raw[:, :, 4 * g * DH:4 * (g + 1) * DH].rearrange("p t (h d) -> p t h d", d=DH)
                inverse = rn[:, 0:T * HEADS].rearrange("p (t h) -> p t h", t=T)[:, :, 4 * g:4 * g + 4]
                nc.gpsimd.tensor_tensor(q, q, inverse[:, :, :, None].broadcast_to([P, T, 4, DH]),
                                        ALU.mult).then_inc(qm_ready, 1)

            def q_low(g, b):
                pool.wait_ge(qh_ready, (b + 1) * GROUPS + g + 1)
                heads = qn[:, :, 4 * g:4 * g + 4, :]
                nc.gpsimd.tensor_tensor(heads[:, :, :, DH:2 * DH],
                                        q_raw[:, :, 4 * g * DH:4 * (g + 1) * DH].rearrange("p t (h d) -> p t h d", d=DH),
                                        heads[:, :, :, 0:DH], ALU.subtract).then_inc(qn_ready, 1)

            def turn(b, has):
                for h in range(HEADS):
                    if has["pre"]:
                        batch_mask(h, b)
                        if 10 <= h < 10 + GROUPS:
                            q_low(h - 10, b)
                        if 9 <= h < 9 + GROUPS:
                            normalise_q(h - 9, b, has)
                        if h - 1 in Q_AT:
                            square(Q_AT[h - 1], b, has)
                        if h == 7:
                            square(4, b, has)
                    if has["tail"] and h == 1:
                        pool.wait_ge(d_free, d_use("X1T", b - 2))
                        wait(pool, out_ready, b - 2)
                        nc.gpsimd.tensor_tensor(resid[:], acc[:], krow("ln_b")[:, None, :].broadcast_to([P, T, D]),
                                                ALU.add).then_inc(resid_ready, 1)
                    if has["tail"] and h == 15:
                        pool.wait_ge(norm_ready, b - 1)
                        nc.gpsimd.tensor_tensor(norm[:], norm[:], krow("ln_g")[:, None, :].broadcast_to([P, T, D]),
                                                ALU.mult).then_inc(gain_ready, 1)
                        pool.wait_ge(gain_ready, b - 1)
                        pool.wait_ge(resid_ready, b - 1)
                        nc.gpsimd.tensor_tensor(norm[:], norm[:], resid[:], ALU.add).then_inc(out_ready, 1)
                    if piece_at(b, h) is not None:
                        split_lo(piece_at(b, h))

            first = parts(-1)
            pool.wait_ge(head_hi, 1)
            nc.gpsimd.tensor_tensor(w_lo[:, 0:HEAD], stage_head, w_hi[:, 0:HEAD].bitcast(F32),
                                    ALU.subtract).then_inc(head_lo, 1)
            for k in range(QROUNDS):
                square(k, -1, first)
            normalise_q(0, -1, first)
            q_low(0, -1)
            pool.wait_ge(head_lo, 1)
            for h in range(HEADS // 2):
                if h % 4 == 0:
                    pool.wait_ge(bias_loaded[h // 4], 16)
                if h == HEADS // 2 - 1:
                    pool.wait_ge(half_bias, 2)
                batch_mask(h, -1, 1 if h < HEADS // 2 - 1 else 1 + HEADS // 2)
                if h in (0, 2, 4):
                    normalise_q(h // 2 + 1, -1, first)
                if h in (1, 3, 5):
                    q_low(h // 2 + 1, -1)

            for b in (0, 1):
                turn(b, parts(b))
            with pool.Fori(2, B - 1) as b:
                turn(b, FULL)
            for b in (B - 1, B, B + 1):
                turn(b, parts(b))

        @block.vector
        def _(dve):
            V = nc.vector
            chain = Steps(dve, sem("steps_set"), 0)
            chain.start(0)
            pre_steps = Steps(dve, steps_pre, PRE_STEPS)
            norm_steps = Steps(dve, steps_norm, NORM_STEPS)
            route_steps = Steps(dve, steps_route, ROUTE_STEPS)
            last_steps = Steps(dve, steps_last, NORM_STEPS)

            def rsqrt(steps, y, x, tmp):
                rsqrt_begin(steps, y, x, tmp)
                rsqrt_end(steps, y, x, tmp)

            def rsqrt_begin(steps, y, x, tmp):
                steps.link(V.tensor_scalar(y.bitcast(I32), x.bitcast(I32), -0.5, RSQRT_MAGIC, ALU.mult, ALU.add))
                steps.link(V.tensor_tensor(tmp, y, y, ALU.mult))
                steps.link(V.scalar_tensor_tensor(out=tmp, in0=tmp, scalar=-0.5, in1=x, op0=ALU.mult, op1=ALU.mult))
                steps.link(V.scalar_tensor_tensor(out=y, in0=tmp, scalar=1.5, in1=y, op0=ALU.add, op1=ALU.mult))

            def rsqrt_end(steps, y, x, tmp):
                steps.link(V.tensor_tensor(tmp, y, y, ALU.mult))
                steps.link(V.scalar_tensor_tensor(out=tmp, in0=tmp, scalar=HALLEY_A, in1=x, op0=ALU.mult, op1=ALU.mult))
                steps.link(V.scalar_tensor_tensor(out=tmp, in0=tmp, scalar=HALLEY_B, in1=tmp, op0=ALU.add, op1=ALU.mult))
                steps.link(V.scalar_tensor_tensor(out=y, in0=tmp, scalar=1.875, in1=y, op0=ALU.add, op1=ALU.mult))

            def carry_wait(at):
                V.memset(idle[:, at:at + 1], 0.0)

            def score_min(h, b):
                n = b * HEADS + h
                dve.wait_ge(s_full, n + 1)
                dve.wait_ge(batch_bias, n + 1)
                wait(dve, pt_full, n - 3)
                carry_wait(h)
                for t, (at, w) in enumerate(((SB0, P + 1), (SB1, S + 1))):
                    i = V.tensor_tensor_reduce(out=prob[:, h % 4, at:at + w], in0=bank_s[h % 2][:, at:at + w],
                                               in1=bias_b[:, h, at:at + w], scale=1.0, scalar=3e38, op0=ALU.add,
                                               op1=ALU.min, accum_out=s_min[:, h % 4, t:t + 1])
                i.then_inc(s_read, 1)

            def normalise_values(g, b):
                dve.wait_ge(pv_done, b * HEADS + 4 * g + 4)
                V.reciprocal(r_sum[:], s_sum[:, :, 4 * g:4 * g + 4]).then_inc(sum_ready, 1)
                dve.wait_ge(sum_ready, b * GROUPS + g + 1)
                V.tensor_tensor(on[:, g % 2].rearrange("p t (h d) -> p t h d", h=4),
                                bank_pv[:].rearrange("p (t h d) -> p t h d", t=T, h=4),
                                r_sum[:, :, :, None].broadcast_to([P, T, 4, DH]), ALU.mult).then_inc(on_ready, 1)

            def take_output(b, has):
                use = m_use("WO", b, has)
                dve.wait_ge(m_full, use + 1)
                V.tensor_tensor(yn[:], bank_m[:, 0:T * D].rearrange("p (t d) -> p t d", t=T),
                                null_out[:, None, :].broadcast_to([P, T, D]), ALU.add).then_inc(m_free, 1)

            def output_stats(b, has):
                norm_steps.start(b - 1)
                dve.wait_ge(m_free, m_use("WO", b, has) + 1)
                for t in range(T):
                    stat = V.bn_stats(y_stat[:, t, :], yn[:, t, :])
                norm_steps.link(stat)
                carry_wait(HEADS)
                for t in range(T):
                    stat = V.bn_aggr(y_mv[:, t, :], y_stat[:, t, :])
                norm_steps.link(stat)
                norm_steps.link(V.tensor_scalar(y_var[:], y_mv[:, :, 1], LN_EPS, None, ALU.add))
                rsqrt_begin(norm_steps, y_rstd[:], y_var[:], y_tmp[:])

            def output_scale():
                rsqrt_end(norm_steps, y_rstd[:], y_var[:], y_tmp[:])
                for t in range(T):
                    i = V.tensor_scalar(yn[:, t, :], yn[:, t, :], y_mv[:, t, 0:1], y_rstd[:, t:t + 1],
                                        ALU.subtract, ALU.mult)
                i.then_inc(yn_ready, 1)
                norm_steps.end()

            def take_mask(b):
                wait(dve, batch_bias, (b + 1) * HEADS)
                V.tensor_scalar(mask_row[:, SB1:SB1 + S], mask_u8[:, b + 1, :], -BIG, BIG, ALU.mult, ALU.add)
                V.tensor_scalar(mask_row[:, SB0:SB0 + P], mask_u8[:, b + 1, 0:P], -BIG, BIG, ALU.mult,
                                ALU.add).then_inc(mask_ready, 1)

            def normalise_x(b):
                for t in range(T):
                    n = (b + 1) * T + t
                    i = V.tensor_scalar(xn[:, t, :], x_sb[:, n, :], x_mv[:, n, 0:1], x_rstd[:, bass.ds(n, 1)],
                                        ALU.subtract, ALU.mult)
                i.then_inc(xn_ready, 1)

            def x_low(b):
                dve.wait_ge(m_hi, b + 2)
                V.scalar_tensor_tensor(out=xnT_lo[:], in0=bank_m[:, 0:S], scalar=col("g_norm"),
                                       in1=xnT_hi[:].bitcast(F32), op0=ALU.mult, op1=ALU.subtract).then_inc(m_free, 1)

            def sum_squares(k, b):
                dve.wait_ge(sq_ready, (b + 1) * QROUNDS + k + 1)
                if k < 4:
                    dst, n = ss[:, k * E:(k + 1) * E], 512
                else:
                    dst, n = ss[:, T * HEADS:T * HEADS + T], T * DH
                V.tensor_reduce(dst, sq[:, k % 2, 0:n].rearrange("p (h d) -> p h d", d=DH), AX,
                                ALU.add).then_inc(ss_ready, 1)

            def inverse_norms(b):
                dve.wait_ge(ss_ready, (b + 2) * QROUNDS)
                pre_steps.start(b + 1)
                pre_steps.link(V.tensor_scalar(ss[:], ss[:], 1e-24, None, ALU.max))
                rsqrt_begin(pre_steps, rn[:], ss[:], rn_tmp[:])

            def normalise_k(b):
                rsqrt_end(pre_steps, rn[:], ss[:], rn_tmp[:])
                pre_steps.end()
                for t in range(T):
                    i = V.tensor_scalar(kn[:, t, :].rearrange("p (c d) -> p c d", c=2),
                                        kv_raw[:, t, None, 0:DH].broadcast_to([P, 2, DH]),
                                        rn[:, T * HEADS + t:T * HEADS + t + 1], None, ALU.mult)
                i.then_inc(kn_ready, 1)

            def key_low(at, keys, scale=kscale):
                cs = slice(at, at + keys.free_size())
                return V.scalar_tensor_tensor(out=kT_lo[0:DH, cs], in0=keys, scalar=scale[0:DH, 0:1],
                                              in1=kT_hi[0:DH, cs].bitcast(F32), op0=ALU.mult, op1=ALU.subtract)

            def k_low(b):
                dve.wait_ge(k_hi, b + 2)
                key_low(SB1, bank_m[0:DH, 0:S])
                key_low(SB0, bank_m[0:DH, 0:P]).then_inc(m_free, 1)

            def shift_values(b):
                wait(dve, pv_done, b * HEADS)
                V.tensor_tensor(val[:], kv_raw[:, :, DH:2 * DH], krow("nv_row")[:, None, :].broadcast_to([P, T, DH]),
                                ALU.subtract).then_inc(val_ready, 1)

            def token_low(name, i, scale, m):
                dve.wait_ge(d_hi, 2 * m + i + 1)
                V.scalar_tensor_tensor(out=yT_lo[:], in0=bank_d[:, 0:S], scalar=scale, in1=yT_hi[:].bitcast(F32),
                                       op0=ALU.mult, op1=ALU.subtract).then_inc(d_free, 1)

            def route_begin(i, m):
                route_steps.start(2 * m + i)
                each = [P, T, E]
                use = d_use(f"LOG{i}", m)
                dve.wait_ge(d_full, use + 1)
                src = bank_d[:, 0:T * E].rearrange("p (t e) -> p t e", t=T)
                if i == 0:
                    V.tensor_scalar(lg[:], src, SCALE_R0, None, ALU.mult).then_inc(d_free, 1)
                    dve.wait_ge(d_free, use + 1)
                    route_steps.link(V.tensor_tensor(cand[:, :, 0:E], lg[:], krow("rb")[:, None, :].broadcast_to(each),
                                                     ALU.add))
                else:
                    V.tensor_tensor(lg[:], src, cond_logit[:, bass.ds(m * E, E)][:, None, :].broadcast_to(each),
                                    ALU.add).then_inc(d_free, 1)
                    dve.wait_ge(d_free, use + 1)
                    route_steps.link(V.tensor_scalar(cand[:, :, 0:E], lg[:], 1.0, None, ALU.mult))
                carry_wait(HEADS)
                for t in range(T):
                    first = V.max(out=top8[:, t, :], in_=cand[:, t, 0:E])
                route_steps.link(first)
                route_steps.link(V.memset(top8[:, :, 2:E], -BIG))

            def route_end(i):
                each = [P, T, E]
                carry_wait(HEADS + 1)
                for t in range(T):
                    out = V.match_replace(out=cand_left[:, t, :], in_to_replace=top8[:, t, :], in_values=cand[:, t, :],
                                          imm_value=-2 * BIG)
                route_steps.link(out)
                route_steps.link(V.tensor_tensor(chosen[:], cand_left[:, :, 0:E], cand[:, :, 0:E], ALU.not_equal))
                route_steps.link(V.tensor_tensor(ldiff[:], chosen[:], lg[:], ALU.mult))
                route_steps.link(V.tensor_reduce(lsum[:], ldiff[:], AX, ALU.add))
                V.scalar_tensor_tensor(out=ldiff[:], in0=lsum[:, :, None].broadcast_to(each), scalar=-0.5, in1=lg[:],
                                       op0=ALU.mult, op1=ALU.add).then_inc(diff_ready, 1)

            def route_weights(i, m):
                dve.wait_ge(tanh_ready, 2 * m + i + 1)
                w = V.scalar_tensor_tensor(out=w_tok[:], in0=ldiff[:], scalar=1.0, in1=chosen[:],
                                           op0=ALU.add, op1=ALU.mult)
                route_steps.link(w)
                V.tensor_scalar(w_tok[:], w_tok[:], 0.25 if i == 0 else 0.5, None, ALU.mult).then_inc(w_ready, 1)
                route_steps.end()

            def gate_up(k, m):
                n = m * NGU + k
                w = S if k == X0 else 512
                dve.wait_ge(act_ready, n + 1)
                if 2 <= k < X0:
                    dve.wait_ge(d_full, d_use(f"D{k - 2}", m) + 1)
                at = k % 2 * 512 if k < X0 else {X0: 4 * S, X0 + 1: 0, X0 + 2: 512}[k]
                h = hid[:, at:at + w]
                if k < X0:
                    i = V.scalar_tensor_tensor(out=h, in0=act_g[:, 0:w], scalar=1.0, in1=bank_g[:, 0:w],
                                               op0=ALU.add, op1=ALU.mult)
                else:
                    i = V.scalar_tensor_tensor(out=h, in0=bank_g[:, 0:w], scalar=0.01, in1=act_g[:, 0:w],
                                               op0=ALU.mult, op1=ALU.add)
                i.then_inc(g_read, 1)
                dve.wait_ge(g_read, n + 1)
                dve.wait_ge(u_full, n + 1)
                V.tensor_tensor(h, h, bank_u[:, 0:w], ALU.mult).then_inc(u_read, 1)

            def add_expert(e, m):
                use = d_use(f"D{e}", m)
                dve.wait_ge(d_full, use + 1)
                wait(dve, d_free, use)
                if e == 0:
                    dve.wait_ge(w_ready, 2 * m + 1)
                    wait(dve, resid_ready, m)
                for t in range(T):
                    before = x_sb[:, m * T + t, :] if e == 0 else acc[:, t, :]
                    scale = w_tok[:, t, e:e + 1] if e < E else 0.5
                    i = V.scalar_tensor_tensor(out=acc[:, t, :], in0=bank_d[:, t * D:(t + 1) * D], scalar=scale,
                                               in1=before, op0=ALU.mult, op1=ALU.add)
                i.then_inc(d_free, 1)

            def weights_low(m):
                dve.wait_ge(w_hi_ready, m + 1)
                V.tensor_tensor(wT_lo[:], bank_d[0:E, 0:S], wT_hi[:].bitcast(F32), ALU.subtract).then_inc(d_free, 1)

            def weight_hidden(r, m):
                dve.wait_ge(d_full, d_use(f"WB{r}", m) + 1)
                dve.wait_ge(u_read, m * NGU + X0 + 2 + r)
                h = hid[:, r * 512:(r + 1) * 512]
                V.tensor_tensor(h, h, bank_d[:], ALU.mult).then_inc(d_free, 1)

            def last_stats(m):
                last_steps.start(m)
                dve.wait_ge(d_free, d_use("DOWN", m) + 1)
                for t in range(T):
                    stat = V.bn_stats(o_stat[:, t, :], norm[:, t, :])
                last_steps.link(stat)
                carry_wait(HEADS + 1)
                for t in range(T):
                    stat = V.bn_aggr(o_mv[:, t, :], o_stat[:, t, :])
                last_steps.link(stat)
                last_steps.link(V.tensor_scalar(o_var[:], o_mv[:, :, 1], LN_EPS, None, ALU.add))

            def last_scale(m):
                for t in range(T):
                    i = V.tensor_scalar(norm[:, t, :], norm[:, t, :], o_mv[:, t, 0:1], o_rstd[:, t:t + 1],
                                        ALU.subtract, ALU.mult)
                i.then_inc(norm_ready, 1)
                last_steps.end()

            def turn(b, has):
                att, pre, moe, tail = (has[n] for n in ("att", "pre", "moe", "tail"))
                m, m1 = b - 1, b - 2
                for h in range(HEADS):
                    if pre and h == 0:
                        normalise_x(b)
                    if pre and h == 1:
                        x_low(b)
                    if att and h in (5, 9, 13):
                        normalise_values((h - 5) // 4, b)
                    if moe and h == 3:
                        take_output(b, has)
                    if moe and h == 6:
                        token_low("YT", 0, col("g_out"), m)
                    if pre and h == 12:
                        k_low(b)
                    if tail:
                        if h == 0:
                            token_low("X1T", 1, 1.0, m1)
                        if h == 3:
                            weights_low(m1)
                        if h in (1, 2, 3):
                            gate_up(X0 + h - 1, m1)
                    if moe and 6 < h < 6 + X0:
                        gate_up(h - 6, m)
                    ahead = h + LEAD
                    if att and ahead < HEADS:
                        score_min(ahead, b)
                    if pre and ahead >= HEADS:
                        score_min(ahead - HEADS, b + 1)
                    if att and h == 0:
                        shift_values(b)
                    if moe and h == 0:
                        normalise_values(3, m)
                    if tail:
                        if h == 1:
                            route_begin(1, m1)
                            route_end(1)
                        if h == 2:
                            route_weights(1, m1)
                        if h in (3, 4):
                            weight_hidden(h - 3, m1)
                    if moe:
                        if h == 4:
                            output_stats(b, has)
                        if h == 5:
                            output_scale()
                        if h == 7:
                            route_weights(0, m)
                        if 7 <= h < 7 + X0:
                            add_expert(h - 7, m)
                    if pre:
                        if h == 1:
                            take_mask(b)
                        if h - 2 in Q_AT:
                            sum_squares(Q_AT[h - 2], b)
                        if h == 8:
                            sum_squares(4, b)
                            inverse_norms(b)
                        if h == 9:
                            normalise_k(b)
                    if moe and h == 6:
                        route_begin(0, m)
                        gate_up(0, m)
                        route_end(0)
                    if tail:
                        if h == 10:
                            last_stats(m1)
                        if h == 11:
                            rsqrt_begin(last_steps, o_rstd[:], o_var[:], o_tmp[:])
                        if h == 12:
                            rsqrt_end(last_steps, o_rstd[:], o_var[:], o_tmp[:])
                        if h == 14:
                            last_scale(m1)

            def bias_layer(layer, early, *meanwhile):
                both = [P, 2, D]
                if layer == 0:
                    for t in range(2):
                        z = V.scalar_tensor_tensor(out=hb[:, t, :], in0=row("w0"), scalar=col(f"pos{t}"),
                                                   in1=row("b0"), op0=ALU.mult, op1=ALU.add)
                    chain.link(z)
                else:
                    dve.wait_ge(net_pe, HW1)
                    chain.link(V.tensor_tensor(hb, bank_pv[:, 0:2 * D].rearrange("p (t d) -> p t d", t=2),
                                               row("b1")[:, None, :].broadcast_to(both), ALU.add))
                for t in range(2):
                    stat = V.bn_stats(y_stat[:, t, :], hb[:, t, :])
                chain.link(stat)
                for t in range(2):
                    stat = V.bn_aggr(y_mv[:, t, :], y_stat[:, t, :])
                chain.link(stat)
                early()
                chain.link(V.tensor_scalar(y_var[:], y_mv[:, :, 1], LN_EPS, None, ALU.add))
                rsqrt(chain, y_rstd[:], y_var[:], y_tmp[:])
                for t in range(2):
                    z = V.tensor_scalar(hb[:, t, :], hb[:, t, :], y_mv[:, t, 0:1], y_rstd[:, t:t + 1],
                                        ALU.subtract, ALU.mult)
                chain.link(z)
                V.tensor_tensor(hb, hb, row(f"g{layer}")[:, None, :].broadcast_to(both), ALU.mult).then_inc(net_dve, 1)
                meanwhile[0]()
                dve.wait_ge(net_act, layer + 1)
                chain.link(V.scalar_tensor_tensor(out=hs, in0=hs, scalar=1.0, in1=hb, op0=ALU.add, op1=ALU.mult))
                V.tensor_scalar(hs, hs, 0.5, None, ALU.mult).then_inc(net_dve, 1)
                meanwhile[1]()
                dve.wait_ge(net_pe, (HT0, HT1)[layer])
                V.tensor_copy(hT, bank_pt[:, 0:2 * P]).then_inc(net_dve, 1)
                meanwhile[2]()

            def x_stats(a, b, begin=True, end=True):
                if begin:
                    for i in range(a, b):
                        stat = V.bn_stats(x_stat[:, i, :], x_sb[:, i, :])
                    chain.link(stat)
                    for i in range(a, b):
                        stat = V.bn_aggr(x_mv[:, i, :], x_stat[:, i, :])
                    chain.link(stat)
                    chain.link(V.tensor_scalar(x_var[:, a:b], x_mv[:, a:b, 1], LN_EPS, None, ALU.add))
                if end:
                    rsqrt(chain, x_rstd[:, a:b], x_var[:, a:b], x_tmp[:, a:b])

            def first_stats():
                dve.wait_ge(ld_x0, 16)
                x_stats(0, T, end=False)

            def first_tokens():
                x_stats(0, T, begin=False)
                normalise_x(-1)

            def null_key():
                V.tensor_tensor(kscale[:], col("q_scale"), col("k_scale"), ALU.mult)
                dve.wait_ge(ld_null, 16)
                chain.link(V.tensor_tensor(nk_sq, row("nk"), row("nk"), ALU.mult))
                V.tensor_scalar(kscale[:], kscale[:], -SCALE_QK, None, ALU.mult)
                chain.link(V.tensor_reduce(ss[:, NSUM - 1:NSUM], nk_sq[:, 0:DH], AX, ALU.add))

            V.memset(kT_hi[:].bitcast(F32), 0.0)
            V.memset(kT_lo[:].bitcast(F32), 0.0).then_inc(set_dve, 1)
            dve.wait_ge(ld_small, 32)
            bias_layer(0, lambda: None, first_stats, first_tokens, lambda: x_low(-1))
            bias_layer(1, null_key, lambda: sum_squares(0, -1), lambda: sum_squares(1, -1),
                       lambda: sum_squares(2, -1))
            dve.wait_ge(net_pe, HW2)
            V.memset(rel[:, S:REL], BIG)
            V.tensor_scalar(rel[:, 0:S], bank_pv[0:HEADS, 0:S], col("b2", HEADS), -1.0, ALU.add,
                            ALU.mult).then_inc(rel_ready, 1)
            V.memset(mask_row[:, S:S + 2], 0.0)
            V.memset(mask_row[:, SB0 + P:SW], 0.0)
            dve.wait_ge(ld_mask, 16)
            take_mask(-1)
            dve.wait_ge(ld_krows, 16)
            V.memset(cand[:, :, E:2 * E], -BIG)
            V.tensor_scalar(bias_all[:, :, S], krow("null_bias"), -1.0, None, ALU.mult)
            for k in range(3, QROUNDS):
                sum_squares(k, -1)
            inverse_norms(-1)
            normalise_k(-1)
            chain.link(V.tensor_tensor(nk_scale, kscale[:], rn[:, NSUM - 1:NSUM], ALU.mult))
            dve.wait_ge(set_pe, NK_T)
            for at in (S, SB0 + P):
                chain.link(V.tensor_scalar(kT_hi[:, at:at + 1], bank_s[1][:, 0:1], nk_scale, None, ALU.mult))
                low = key_low(at, bank_s[1][0:DH, 0:1], nk_scale)
            low.then_inc(set_dve, 1)
            dve.wait_ge(ld_x, 16)
            x_stats(T, B * T, end=False)
            k_low(-1)
            dve.wait_ge(set_pe, NV_T)
            V.tensor_copy(nv_rep, bank_d[:, 0:P]).then_inc(set_dve, 1)
            for half, src in enumerate((bank_u, bank_g)):
                dve.wait_ge(set_pe, COND_T0 + half)
                V.tensor_copy(cond_rep[:, 4 * half:4 * half + 4, :],
                              src[0:DH, :].rearrange("p (b n) -> p b n", b=4)).then_inc(set_dve, 1)
            dve.wait_ge(mask_ready, 1)
            dve.wait_ge(head_lo, 1)
            for g, then in ((2, (0, 1)), (3, (2,))):
                dve.wait_ge(bias_loaded[g], 16)
                for h in range(4 * g, 4 * g + 4):
                    i = mask_bias(V, h)
                i.then_inc(half_bias, 1)
                for h in then:
                    score_min(h, 0)
            dve.wait_ge(set_pe, COND)
            V.tensor_copy(cond_logit[:], bank_d[:, 0:B * E]).then_inc(set_dve, 1)
            x_stats(T, B * T, begin=False)
            dve.wait_ge(set_pe, NULL_OUT)
            V.tensor_copy(null_out[:], bank_u[:, 0:D]).then_inc(set_dve, 1)

            for b in (0, 1):
                turn(b, parts(b))
            with dve.Fori(2, B - 1) as b:
                turn(b, FULL)
            for b in (B - 1, B, B + 1):
                turn(b, parts(b))


def kernel(**inputs):
    import numpy as np
    import concourse.bacc as bacc
    from concourse.bass_utils import run_bass_kernel_spmd

    i = {name: np.asarray(a) for name, a in inputs.items()}
    assert i["x"].shape == (B, S, D) and i["x"].shape[0] // i["L1_ffn_Wq"].shape[0] == 0

    def by_input(w):
        return w.transpose(1, 0, 2).reshape(w.shape[1], -1)

    def by_chunk(w):
        return w.reshape(-1, P, w.shape[-1]).transpose(1, 0, 2).reshape(P, -1)

    def padded(w):
        return np.concatenate([w, np.zeros((P - w.shape[0], w.shape[1]), w.dtype)]) if w.shape[0] < P else w

    c = np.concatenate
    split = c([i["L0_cond_Wq"], i["L0_cond_Wkv"], i["L0_ffn_Wr"], i["L1_cond_wt"].T,
               by_input(i["L0_ffn_W3"]), i["L0_ffn_Ws3"], by_input(i["L0_ffn_W1"]), i["L0_ffn_Ws1"],
               by_input(i["L1_cond_w_gate"]), i["L1_cond_sw_gate"], by_input(i["L1_cond_w_up"]),
               i["L1_cond_sw_up"]], axis=1)
    down = c([by_chunk(i["L0_ffn_W2"].reshape(-1, D)), by_chunk(i["L0_ffn_Ws2"]), by_chunk(i["L0_cond_Wout"]),
              by_chunk(i["L1_cond_w_down"].reshape(-1, D)), i["L1_cond_sw_down"]], axis=1)
    cond = i["cond_64"]
    rows = c([i["L0_cond_w0"][0], i["L0_cond_b0"], i["L0_cond_g0"], i["L0_cond_b1"], i["L0_cond_g1"],
              cond[0], cond[0], cond[1], cond[1], cond.reshape(-1)])
    krows = c([i["L0_cond_null_attn_bias"], i["L0_ffn_rb"], i["L1_ffn_ln_g"], i["L1_ffn_ln_b"], cond[1]])
    pos = np.arange(S - 1, -1, -1, dtype=np.float32).reshape(2, P)
    b2 = c([i["L0_cond_b2"], np.zeros(P - HEADS, np.float32)])
    cols = np.stack([i["L0_cond_g_norm"], c([i["L0_cond_q_scale"]] * 2), c([i["L0_cond_k_scale"]] * 2),
                     i["L0_cond_g_out"], b2, pos[0], pos[1]], axis=1)
    sel = np.repeat(np.eye(E, dtype=np.float32), M1, axis=1)
    mats = c([i["L0_cond_w1"], i["L0_cond_w2"], padded(i["L1_cond_wg"].T), np.eye(P, dtype=np.float32)], axis=1)
    arrays = {"x": i["x"], "mask": i["mask_BxS_bf1"].view(np.uint8), "split": split, "down": down, "rows": rows,
              "krows": krows, "cols": cols, "mats": mats, "sel": sel}
    arrays = {name: np.ascontiguousarray(a) for name, a in arrays.items()}
    nc = bacc.Bacc("TRN2", target_bir_lowering=False, num_devices=1)
    args = [nc.dram_tensor(f"in_{name}", a.shape, mybir.dt.from_np(a.dtype), kind="ExternalInput").ap()
            for name, a in arrays.items()]
    rel = nc.dram_tensor("bias_by_distance", (HEADS, REL), F32, kind="Internal").ap()
    out = nc.dram_tensor("out", (B, S, D), F32, kind="ExternalOutput").ap()
    build(nc, *args, rel, out)
    r = run_bass_kernel_spmd(nc, [{f"in_{name}": a for name, a in arrays.items()}], core_ids=[0])
    return r.results[0]["out"]
```
